# Optimizing a Trainium2 kernel written in Bass

```python
import numpy as np
import jax
import jax.numpy as jnp

def _softmax(x, axis=-1):
    return jax.nn.softmax(x, axis=axis)

def _gelu(x):
    return jax.nn.gelu(x, approximate=True)

def _silu(x):
    return jax.nn.silu(x)

def _sigmoid(x):
    return jax.nn.sigmoid(x)

def _layernorm(x, axis=-1, eps=1e-05):
    m = jnp.mean(x, axis=axis, keepdims=True)
    v = jnp.var(x, axis=axis, keepdims=True)
    return (x - m) / jnp.sqrt(v + eps)

def _scatter_add(tgt, idx, src, axis=0):
    return tgt.at[idx].add(src)

def _segment_sum(src, seg, n):
    return jax.ops.segment_sum(src, seg, n)
kernel_name = 'mk_seq_postln_d2_jaxref_r4_42e2cf'

def setup_inputs(seed: int=0):
    np.random.seed(seed)
    _w = jnp.asarray

    def _L0_attn_setup():
        import jax, jax.numpy as jnp
        import numpy as np
        DIM = 512
        N_HEADS = 32
        N_KV_HEADS = 8
        ROPE_THETA = 10000.0

        def _rope(x, theta):
            B, N, H, D = x.shape
            freq = theta ** (-(jnp.arange(D // 2, dtype=jnp.float32) * (2.0 / D)))
            phase = jnp.arange(N, dtype=jnp.float32)[:, None] * freq[None, :]
            c = jnp.cos(phase)[None, :, None, :]
            s = jnp.sin(phase)[None, :, None, :]
            x0, x1 = (x[..., 0::2], x[..., 1::2])
            return jnp.stack([x0 * c - x1 * s, x0 * s + x1 * c], axis=-1).reshape(B, N, H, D)
        key = jax.random.key(seed)
        k0, k1, k2, k3, k4 = jax.random.split(key, 5)
        B, N = (2, 256)
        kv_dim = DIM // (N_HEADS // N_KV_HEADS)
        return {'x': jax.random.normal(k0, (B, N, DIM), jnp.float32), 'wq': jax.random.normal(k1, (DIM, DIM), jnp.float32) * 0.02, 'wk': jax.random.normal(k2, (DIM, kv_dim), jnp.float32) * 0.02, 'wv': jax.random.normal(k3, (DIM, kv_dim), jnp.float32) * 0.02, 'wo': jax.random.normal(k4, (DIM, DIM), jnp.float32) * 0.02}
    _L0_attn_in = _L0_attn_setup()

    def _L0_ffn_setup():
        import jax, jax.numpy as jnp
        import numpy as np
        EPS = 1e-06
        Q_B = 128.0

        def layer_norm(x):
            mean = jnp.mean(x, axis=-1, keepdims=True)
            var = jnp.var(x, axis=-1, keepdims=True)
            return (x - mean) / jnp.sqrt(var + EPS)

        def absmax_quant(x):
            gamma = jnp.max(jnp.abs(x), axis=-1, keepdims=True)
            x_hat = jnp.clip(x * Q_B / gamma, -Q_B + EPS, Q_B - EPS)
            return x_hat * gamma / Q_B

        def ternarize_weights(w):
            gamma = jnp.mean(jnp.abs(w))
            return jnp.sign(jnp.round(w / (gamma + EPS))) * gamma

        def bitlinear(x, w):
            xn = layer_norm(x)
            x_hat = xn + jax.lax.stop_gradient(absmax_quant(xn) - xn)
            w_hat = w + jax.lax.stop_gradient(ternarize_weights(w) - w)
            return jnp.einsum('bsd,od->bso', x_hat, w_hat)
        key = jax.random.key(seed)
        k1, k2, k3 = jax.random.split(key, 3)
        B, S, D = (4, 512, 512)
        x = jax.random.normal(k1, (B, S, D), dtype=jnp.float32)
        w_fc = jax.random.normal(k2, (4 * D, D), dtype=jnp.float32) / np.sqrt(D)
        w_proj = jax.random.normal(k3, (D, 4 * D), dtype=jnp.float32) / np.sqrt(4 * D)
        return {'x': x, 'w_fc': w_fc, 'w_proj': w_proj}
    _L0_ffn_in = _L0_ffn_setup()

    def _L1_attn_setup():
        import jax, jax.numpy as jnp
        import numpy as np
        B, N, E = (4, 1024, 512)
        H_DIM = 512
        HEADS = 16
        DH = H_DIM // HEADS
        LN_EPS = 1e-05

        def _heads(t):
            b, n, _ = t.shape
            return t.reshape(b, n, HEADS, DH).transpose(0, 2, 1, 3)

        def _layernorm(x, g, b):
            mu = jnp.mean(x, axis=-1, keepdims=True)
            var = jnp.mean(jnp.square(x - mu), axis=-1, keepdims=True)
            return (x - mu) * jax.lax.rsqrt(var + LN_EPS) * g + b
        key = jax.random.key(seed)
        ks = jax.random.split(key, 10)
        s = 1.0 / np.sqrt(E)
        so = 1.0 / np.sqrt(H_DIM)
        return {'x': jax.random.normal(ks[0], (B, N, E), jnp.float32), 'Wqk': jax.random.normal(ks[1], (E, H_DIM), jnp.float32) * s, 'bqk': jnp.zeros((H_DIM,), jnp.float32), 'Wv': jax.random.normal(ks[2], (E, H_DIM), jnp.float32) * s, 'bv': jnp.zeros((H_DIM,), jnp.float32), 'Wu': jax.random.normal(ks[3], (E, H_DIM), jnp.float32) * s, 'bu': jnp.zeros((H_DIM,), jnp.float32), 'Wo': jax.random.normal(ks[4], (H_DIM, E), jnp.float32) * so, 'bo': jnp.zeros((E,), jnp.float32), 'ln_g': jnp.ones((H_DIM,), jnp.float32), 'ln_b': jnp.zeros((H_DIM,), jnp.float32)}
    _L1_attn_in = _L1_attn_setup()

    def _L1_ffn_setup():
        import jax, jax.numpy as jnp
        import numpy as np
        H = 512
        I = 352
        E = 16
        K = 2
        SI = I * 2

        def _swiglu(gu, inter):
            g, u = (gu[..., :inter], gu[..., inter:])
            return jax.nn.silu(g) * u
        key = jax.random.key(seed)
        ks = jax.random.split(key, 6)
        s = 0.02
        hidden_states = jax.random.normal(ks[0], (1, 256, H), dtype=jnp.float32)
        gate_w = jax.random.normal(ks[1], (E, H), dtype=jnp.float32) * s
        w_gate_up = jax.random.normal(ks[2], (E, H, 2 * I), dtype=jnp.float32) * s
        w_down = jax.random.normal(ks[3], (E, I, H), dtype=jnp.float32) * s
        shared_gate_up = jax.random.normal(ks[4], (H, 2 * SI), dtype=jnp.float32) * s
        shared_down = jax.random.normal(ks[5], (SI, H), dtype=jnp.float32) * s
        return {'hidden_states': hidden_states, 'gate_w': gate_w, 'w_gate_up': w_gate_up, 'w_down': w_down, 'shared_gate_up': shared_gate_up, 'shared_down': shared_down}
    _L1_ffn_in = _L1_ffn_setup()
    _d = {'L0_attn_x': _L0_attn_in['x'], 'L0_attn_wq': _L0_attn_in['wq'], 'L0_attn_wk': _L0_attn_in['wk'], 'L0_attn_wv': _L0_attn_in['wv'], 'L0_attn_wo': _L0_attn_in['wo'], 'L0_ffn_w_fc': _L0_ffn_in['w_fc'], 'L0_ffn_w_proj': _L0_ffn_in['w_proj'], 'L1_attn_Wqk': _L1_attn_in['Wqk'], 'L1_attn_bqk': _L1_attn_in['bqk'], 'L1_attn_Wv': _L1_attn_in['Wv'], 'L1_attn_bv': _L1_attn_in['bv'], 'L1_attn_Wu': _L1_attn_in['Wu'], 'L1_attn_bu': _L1_attn_in['bu'], 'L1_attn_Wo': _L1_attn_in['Wo'], 'L1_attn_bo': _L1_attn_in['bo'], 'L1_attn_ln_g': _L1_attn_in['ln_g'], 'L1_attn_ln_b': _L1_attn_in['ln_b'], 'L1_ffn_gate_w': _L1_ffn_in['gate_w'], 'L1_ffn_w_gate_up': _L1_ffn_in['w_gate_up'], 'L1_ffn_w_down': _L1_ffn_in['w_down'], 'L1_ffn_shared_gate_up': _L1_ffn_in['shared_gate_up'], 'L1_ffn_shared_down': _L1_ffn_in['shared_down']}
    _x0 = _d['L0_attn_x']
    _d['L0_attn_x'] = jax.random.normal(jax.random.fold_in(jax.random.key(seed), 1), (2, 1024, 512), dtype=_x0.dtype)
    del _x0
    return _d

def reference(L0_attn_x, L0_attn_wq, L0_attn_wk, L0_attn_wv, L0_attn_wo, L0_ffn_w_fc, L0_ffn_w_proj, L1_attn_Wqk, L1_attn_bqk, L1_attn_Wv, L1_attn_bv, L1_attn_Wu, L1_attn_bu, L1_attn_Wo, L1_attn_bo, L1_attn_ln_g, L1_attn_ln_b, L1_ffn_gate_w, L1_ffn_w_gate_up, L1_ffn_w_down, L1_ffn_shared_gate_up, L1_ffn_shared_down):

    def _L0_attn_ref(x, wq, wk, wv, wo):
        import jax, jax.numpy as jnp
        import numpy as np
        DIM = 512
        N_HEADS = 32
        N_KV_HEADS = 8
        ROPE_THETA = 10000.0

        def _rope(x, theta):
            B, N, H, D = x.shape
            freq = theta ** (-(jnp.arange(D // 2, dtype=jnp.float32) * (2.0 / D)))
            phase = jnp.arange(N, dtype=jnp.float32)[:, None] * freq[None, :]
            c = jnp.cos(phase)[None, :, None, :]
            s = jnp.sin(phase)[None, :, None, :]
            x0, x1 = (x[..., 0::2], x[..., 1::2])
            return jnp.stack([x0 * c - x1 * s, x0 * s + x1 * c], axis=-1).reshape(B, N, H, D)
        B, N, D = x.shape
        H, J = (N_HEADS, N_KV_HEADS)
        hd = D // H
        q = (x @ wq).reshape(B, N, H, hd)
        k = (x @ wk).reshape(B, N, J, hd)
        v = (x @ wv).reshape(B, N, J, hd)
        q = _rope(q, ROPE_THETA)
        k = _rope(k, ROPE_THETA)
        rep = H // J
        k = jnp.repeat(k, rep, axis=2)
        v = jnp.repeat(v, rep, axis=2)
        q = q.transpose(0, 2, 1, 3)
        k = k.transpose(0, 2, 1, 3)
        v = v.transpose(0, 2, 1, 3)
        scores = jnp.einsum('bhqd,bhkd->bhqk', q, k) / jnp.sqrt(jnp.float32(hd))
        causal = jnp.tril(jnp.ones((N, N), dtype=bool))
        scores = jnp.where(causal[None, None], scores, -jnp.inf)
        weight = jax.nn.softmax(scores, axis=-1)
        out = jnp.einsum('bhqk,bhkd->bhqd', weight, v)
        out = out.transpose(0, 2, 1, 3).reshape(B, N, D)
        return out @ wo

    def _L0_ffn_ref(x, w_fc, w_proj):
        import jax, jax.numpy as jnp
        import numpy as np
        EPS = 1e-06
        Q_B = 128.0

        def layer_norm(x):
            mean = jnp.mean(x, axis=-1, keepdims=True)
            var = jnp.var(x, axis=-1, keepdims=True)
            return (x - mean) / jnp.sqrt(var + EPS)

        def absmax_quant(x):
            gamma = jnp.max(jnp.abs(x), axis=-1, keepdims=True)
            x_hat = jnp.clip(x * Q_B / gamma, -Q_B + EPS, Q_B - EPS)
            return x_hat * gamma / Q_B

        def ternarize_weights(w):
            gamma = jnp.mean(jnp.abs(w))
            return jnp.sign(jnp.round(w / (gamma + EPS))) * gamma

        def bitlinear(x, w):
            xn = layer_norm(x)
            x_hat = xn + jax.lax.stop_gradient(absmax_quant(xn) - xn)
            w_hat = w + jax.lax.stop_gradient(ternarize_weights(w) - w)
            return jnp.einsum('bsd,od->bso', x_hat, w_hat)
        h = bitlinear(x, w_fc)
        h = jax.nn.gelu(h, approximate=False)
        return bitlinear(h, w_proj)

    def _L1_attn_ref(x, Wqk, bqk, Wv, bv, Wu, bu, Wo, bo, ln_g, ln_b):
        import jax, jax.numpy as jnp
        import numpy as np
        B, N, E = (4, 1024, 512)
        H_DIM = 512
        HEADS = 16
        DH = H_DIM // HEADS
        LN_EPS = 1e-05

        def _heads(t):
            b, n, _ = t.shape
            return t.reshape(b, n, HEADS, DH).transpose(0, 2, 1, 3)

        def _layernorm(x, g, b):
            mu = jnp.mean(x, axis=-1, keepdims=True)
            var = jnp.mean(jnp.square(x - mu), axis=-1, keepdims=True)
            return (x - mu) * jax.lax.rsqrt(var + LN_EPS) * g + b
        q = x @ Wqk + bqk
        k = x @ Wqk + bqk
        v = jax.nn.silu(x @ Wv + bv)
        u = jax.nn.silu(x @ Wu + bu)
        q = jax.nn.elu(_heads(q))
        kh = jax.nn.elu(_heads(k))
        vh = _heads(v)
        kv = jnp.einsum('bhnd,bhne->bhde', kh, vh)
        out = jnp.einsum('bhnd,bhde->bhne', q, kv)
        out = out.transpose(0, 2, 1, 3).reshape(x.shape[0], x.shape[1], H_DIM)
        out = _layernorm(out, ln_g, ln_b)
        out = u * out
        return out @ Wo + bo

    def _L1_ffn_ref(hidden_states, gate_w, w_gate_up, w_down, shared_gate_up, shared_down):
        import jax, jax.numpy as jnp
        import numpy as np
        H = 512
        I = 352
        E = 16
        K = 2
        SI = I * 2

        def _swiglu(gu, inter):
            g, u = (gu[..., :inter], gu[..., inter:])
            return jax.nn.silu(g) * u
        orig_shape = hidden_states.shape
        x = hidden_states.reshape(-1, H)
        logits = jnp.einsum('th,eh->te', x, gate_w)
        scores = jax.nn.softmax(logits, axis=-1)
        topk_w, topk_idx = jax.lax.top_k(scores, K)
        combine = jnp.sum(jax.nn.one_hot(topk_idx, E, dtype=x.dtype) * topk_w[..., None], axis=1)
        gu = jnp.einsum('th,ehj->etj', x, w_gate_up)
        h = _swiglu(gu, I)
        y = jnp.einsum('eti,eih,te->th', h, w_down, combine)
        gu_s = x @ shared_gate_up
        y = y + _swiglu(gu_s, SI) @ shared_down
        return y.reshape(orig_shape)
    x = L0_attn_x
    x = _layernorm(x + _L0_attn_ref(x, L0_attn_wq, L0_attn_wk, L0_attn_wv, L0_attn_wo), axis=-1)
    x = _layernorm(x + _L0_ffn_ref(x, L0_ffn_w_fc, L0_ffn_w_proj), axis=-1)
    x = _layernorm(x + _L1_attn_ref(x, L1_attn_Wqk, L1_attn_bqk, L1_attn_Wv, L1_attn_bv, L1_attn_Wu, L1_attn_bu, L1_attn_Wo, L1_attn_bo, L1_attn_ln_g, L1_attn_ln_b), axis=-1)
    x = _layernorm(x + _L1_ffn_ref(x, L1_ffn_gate_w, L1_ffn_w_gate_up, L1_ffn_w_down, L1_ffn_shared_gate_up, L1_ffn_shared_down), axis=-1)
    return x

_drawn_inputs = setup_inputs


def setup_inputs(seed=0):
    import zlib

    import numpy as np

    out = dict(_drawn_inputs(seed))
    spreads = {'L1_attn_bqk': (0.0, 0.1),
     'L1_attn_bv': (0.0, 0.1),
     'L1_attn_bu': (0.0, 0.1),
     'L1_attn_bo': (0.0, 0.1),
     'L1_attn_ln_g': (1.0, 0.2),
     'L1_attn_ln_b': (0.0, 0.1)}
    factors = {'L0_attn_wq': 8.0,
     'L0_attn_wk': 8.0,
     'L1_ffn_gate_w': 8.0,
     'L1_ffn_w_gate_up': 7.374,
     'L1_ffn_w_down': 7.325,
     'L1_ffn_shared_gate_up': 8.0,
     'L1_ffn_shared_down': 8.0}
    for name, (base, spread) in spreads.items():
        noise = np.random.default_rng([zlib.crc32(name.encode()), seed]).standard_normal(out[name].shape)
        drawn = base * np.exp(spread * noise) if base else spread * noise
        out[name] = jnp.asarray(drawn.astype(out[name].dtype))
    for name, factor in factors.items():
        out[name] = (out[name] * factor).astype(out[name].dtype)
    return out
```

```python
from contextlib import ExitStack

import numpy as np

import concourse.bass as bass
from concourse import mybir

P = 128
D = 512
KC = D // P
B, N = 2, 1024
NT = B * N // P
TB = N // P
HQ, HKV, HD = 32, 8, 16
GQ = HQ // HKV
KV = HKV * HD
FF = 4 * D
HL = 16
DL = D // HL
NE, TOPK, FE = 16, 2, 352
SI = 2 * FE
WS = 64.0

LO_ROW = 32
KV_SCALE = 1.0 / 16

F32, F16, BF16 = mybir.dt.float32, mybir.dt.float16, mybir.dt.bfloat16
I32, U32 = mybir.dt.int32, mybir.dt.uint32
ALU = mybir.AluOpType
ACT = mybir.ActivationFunctionType
AX = mybir.AxisListType


def run_tiles(eng, n, stages):
    lag = max(l for l, _ in stages)

    def step(s, par):
        for l, fn in stages:
            if not isinstance(s, int) or 0 <= s - l < n:
                fn(s - l, (par - l) % 2)

    first = (lag + 3) // 2 * 2
    pairs = (n - first) // 2
    if pairs < 2:
        first, pairs = n + lag, 0
    for s in range(first):
        step(s, s % 2)
    if pairs:
        with eng.Fori(0, pairs) as i:
            for par in range(2):
                step(i * 2 + (first + par), par)
        for s in range(first + 2 * pairs, n + lag):
            step(s, s % 2)


def after(eng, sem, count):
    if not isinstance(count, int) or count > 0:
        eng.wait_ge(sem, count)


class Phase:

    def __init__(self, nc, name):
        self.nc, self.name = nc, name
        self.ctx, self.sem_ctx, self.held = ExitStack(), ExitStack(), []

    def __enter__(self):
        self.ctx.__enter__()
        self.sem_ctx.__enter__()
        return self

    def __exit__(self, *e):
        with self.nc.Block() as block:
            @block.gpsimd
            def _(pool):
                for s in self.held:
                    pool.sem_clear(s)
        self.sem_ctx.__exit__(*e)
        return self.ctx.__exit__(*e)

    def sb(self, name, shape, dt):
        return self.ctx.enter_context(self.nc.sbuf_tensor(f"{self.name}_{name}", shape, dt))

    def ps(self, name, shape, dt):
        return self.ctx.enter_context(self.nc.psum_tensor(f"{self.name}_{name}", shape, dt))

    def sem(self, name):
        self.held.append(self.sem_ctx.enter_context(self.nc.semaphore(f"{self.name}_{name}")))
        return self.held[-1]

    def sems(self, names):
        return [self.sem(n) for n in names.split()]

    def block(self):
        return self.nc.Block()


def products(pe, out, lhs_hi, lhs_lo, rhs_hi, rhs_lo, chunks):
    last = None
    for k in range(chunks):
        for n, (a, b) in enumerate(((lhs_hi, rhs_hi), (lhs_hi, rhs_lo), (lhs_lo, rhs_hi))):
            last = pe.matmul(out, a(k), b(k), start=(k == 0 and n == 0), stop=(k == chunks - 1 and n == 2))
    return last


def transpose_parts(pe, out, parts, m):
    for part in range(2):
        for k in range(out.shape[2]):
            last = pe.transpose(out[:, part, k, :], parts[:, part, k * P:(k + 1) * P], m.ident16[:, :])
    return last


def load_and_prepare(nc, m, d):
    NO = FF // P
    NP_ = D // P
    with Phase(nc, "prep") as f:
        w_fc = f.sb("w_fc", [P, NO, D], F32)
        w_proj = f.sb("w_proj", [P, NP_, FF], F32)
        t_fc = f.sb("t_fc", [P, NO, D], F16)
        t_proj = f.sb("t_proj", [P, NP_, FF], F16)
        w_qkv = f.sb("w_qkv", [P, KC, D + 2 * KV], F32)
        w_o = f.sb("w_o", [P, KC, D], F32)
        part = f.sb("part", [P, 8], F32)
        total = f.sb("total", [P, 2], F32)
        thr = f.sb("thr", [P, 2, 2], F32)
        ps_sum = f.ps("ps_sum", [P, 8], F32)
        ps_t = [f.ps(f"ps_t{i}", [P, 1024], F16) for i in range(4)]
        consts_in, x_in, wa_in = f.sems("consts_in x_in wa_in")
        fc_in = [f.sem(f"fc_in{c}") for c in range(4)]
        proj_in = [f.sem(f"proj_in{c}") for c in range(4)]
        ident_done, hi_done, lo_done, abs_done, sum_done, tot_done, thr_done = f.sems(
            "ident_done hi_done lo_done abs_done sum_done tot_done thr_done")
        neg_done, tern_done, tr_done, evac_done = f.sems("neg_done tern_done tr_done evac_done")
        fc_rows = d["L0_ffn_w_fc"].rearrange("(n p) k -> p n k", p=P)
        proj_rows = d["L0_ffn_w_proj"].rearrange("(n p) k -> p n k", p=P)
        C4 = NO // 4

        def chunk(c):
            if c < 4:
                s = slice(c * C4, (c + 1) * C4)
                return w_fc[:, s, :], t_fc[:, s, :], fc_in[c]
            return w_proj[:, c - 4, :], t_proj[:, c - 4, :], proj_in[c - 4]

        with f.block() as block:
            @block.sync
            def _(sp):
                sp.dma_start(m.consts[:, :], d["consts"]).then_inc(consts_in, 16)
                for c in range(4):
                    sp.dma_start(w_fc[:, c * C4:(c + 1) * C4, :], fc_rows[:, c * C4:(c + 1) * C4, :]).then_inc(fc_in[c], 16)
                for c in range(4):
                    sp.dma_start(w_proj[:, c, :], proj_rows[:, c, :]).then_inc(proj_in[c], 16)

            @block.gpsimd
            def _(pool):
                pool.memset(m.ones[:, :], 1.0).then_inc(ident_done, 1)
                pool.memset(m.minus_half[:, :], -0.5)

            @block.scalar
            def _(act):
                for n, (w, at, size) in enumerate((("wq", 0, D), ("wk", D, KV), ("wv", D + KV, KV))):
                    act.dma_start(w_qkv[:, :, at:at + size],
                                  d[f"L0_attn_{w}"].rearrange("(k p) n -> p k n", p=P)).then_inc(wa_in, 16)
                act.dma_start(w_o[:, :, :], d["L0_attn_wo"].rearrange("(k p) n -> p k n", p=P)).then_inc(wa_in, 16)
                act.dma_start(m.X[:, :, :], d["L0_attn_x"].rearrange("b (t p) n -> p (b t) n", p=P)).then_inc(x_in, 16)
                act.wait_ge(consts_in, 16)
                act.activation(m.ident16[:, :], m.ident, ACT.Copy).then_inc(ident_done, 1)
                act.activation(m.masks16[:, :, :], m.masks, ACT.Copy).then_inc(ident_done, 1)
                act.activation(m.identb[:, :], m.ident, ACT.Copy).then_inc(ident_done, 1)
                act.wait_ge(wa_in, 64)
                act.activation(m.wqkv_h[:, :, :], w_qkv[:, :, :], ACT.Copy, scale=WS).then_inc(hi_done, 1)
                act.activation(m.wo_h[:, :, :], w_o[:, :, :], ACT.Copy, scale=WS).then_inc(hi_done, 1)
                for c in range(8):
                    src, junk, arrived = chunk(c)
                    act.wait_ge(arrived, 16)
                    act.activation(junk, src, ACT.Abs, accum_out=part[:, c:c + 1]).then_inc(abs_done, 1)
                for g in range(16):
                    act.wait_ge(tr_done, g + 1)
                    dst = m.wfcT[:, g // 2, (g % 2) * 1024:(g % 2 + 1) * 1024] if g < 8 else \
                        m.wprojT[:, 2 * (g - 8):2 * (g - 8) + 2, :].rearrange("p a n -> p (a n)")
                    act.activation(dst, ps_t[g % 4][:, :], ACT.Copy).then_inc(evac_done, 1)
                act.wait_ge(x_in, 16)

            @block.tensor
            def _(pe):
                pe.wait_ge(ident_done, 4)
                pe.wait_ge(abs_done, 8)
                pe.matmul(ps_sum[:, :], m.ones[:, :], part[:, :], start=True, stop=True).then_inc(sum_done, 1)
                for g in range(16):
                    after(pe, evac_done, g - 3)
                    if g < 8:
                        pe.wait_ge(tern_done, 4 if g % 2 else 2)
                    else:
                        pe.wait_ge(tern_done, 8)
                    for r in range(8):
                        if g < 8:
                            src = t_fc[:, (g % 2) * 8 + r, (g // 2) * P:(g // 2 + 1) * P]
                        else:
                            ic = 2 * (g - 8) + r // 4
                            src = t_proj[:, r % 4, ic * P:(ic + 1) * P]
                        last = pe.transpose(ps_t[g % 4][:, r * P:(r + 1) * P], src, m.ident16[:, :])
                    last.then_inc(tr_done, 1)

            @block.vector
            def _(dve):
                dve.wait_ge(hi_done, 1)
                dve.scalar_tensor_tensor(m.wqkv_l[:, :, :], w_qkv[:, :, :], WS, m.wqkv_h[:, :, :],
                                         ALU.mult, ALU.subtract).then_inc(lo_done, 1)
                dve.wait_ge(hi_done, 2)
                dve.scalar_tensor_tensor(m.wo_l[:, :, :], w_o[:, :, :], WS, m.wo_h[:, :, :],
                                         ALU.mult, ALU.subtract).then_inc(lo_done, 1)
                dve.wait_ge(sum_done, 1)
                dve.tensor_reduce(total[:, :], ps_sum[:, :].rearrange("p (w c) -> p w c", w=2), AX.X,
                                  ALU.add).then_inc(tot_done, 1)
                dve.wait_ge(tot_done, 1)
                dve.tensor_scalar(m.gamma[:, :], total[:, :], 1.0 / (D * FF), None, ALU.mult).then_inc(thr_done, 1)
                dve.tensor_scalar(thr[:, 0, :], total[:, :], 0.5 / (D * FF), 0.5e-6, ALU.mult,
                                  ALU.add).then_inc(thr_done, 1)
                dve.tensor_scalar(thr[:, 1, :], total[:, :], -0.5 / (D * FF), -0.5e-6, ALU.mult,
                                  ALU.add).then_inc(thr_done, 1)
                dve.wait_ge(thr_done, 3)
                for c in range(8):
                    src, dst, _ = chunk(c)
                    w = c // 4
                    dve.tensor_scalar(dst, src, thr[:, 1, w:w + 1], None, ALU.is_lt).then_inc(neg_done, 1)
                    dve.wait_ge(neg_done, c + 1)
                    dve.scalar_tensor_tensor(dst, src, thr[:, 0, w:w + 1], dst, ALU.is_gt,
                                             ALU.subtract).then_inc(tern_done, 1)


def project_qkv(nc, m, b, QT, KT, V):
    HB = HQ + 2 * HKV
    with Phase(nc, f"qkv{b}") as f:
        x2 = [f.sb(f"x2{u}", [P, 2, D], F16) for u in range(2)]
        xT = [f.sb(f"xT{u}", [P, 2, KC, P], F16) for u in range(2)]
        t1 = [f.sb(f"t1{u}", [P, HQ + HKV, HD], F32) for u in range(2)]
        t2 = [f.sb(f"t2{u}", [P, HQ + HKV, HD], F32) for u in range(2)]
        rot = t1
        stack = [f.sb(f"stack{u}", [P, HB, 64], F16) for u in range(2)]
        pad = f.sb("pad", [P, 1], F32)
        ps_xt = [f.ps(f"ps_xt{u}", [P, 2, KC, P], F16) for u in range(2)]
        ps_qkv = f.ps("ps_qkv", [P, 1024], F32)
        ps_v = f.ps("ps_v", [P, 512], F32)
        ps_q = [f.ps(f"ps_q{u}", [P, 8, P], F16) for u in range(2)]
        ps_k = f.ps("ps_k", [P, 8, P], F16)
        xh_done, xl_done, xt_done, xt_evac, proj_done, v_done = f.sems(
            "xh_done xl_done xt_done xt_evac proj_done v_done")
        rope_done, rot_done, qhi_done, qlo_done, khi_done, kst_done = f.sems(
            "rope_done rot_done qhi_done qlo_done khi_done kst_done")
        tr_done, qevac, kevac, init_done, halves, kt_zero = f.sems("tr_done qevac kevac init_done halves kt_zero")

        with f.block() as block:
            @block.tensor
            def _(pe):
                def xt(t, u):
                    pe.wait_ge(xl_done, t + 1)
                    after(pe, xt_evac, t - 1)
                    transpose_parts(pe, ps_xt[u], x2[u], m).then_inc(xt_done, 1)

                def proj(t, u):
                    pe.wait_ge(xt_evac, t + 1)
                    after(pe, rope_done, t)
                    after(pe, v_done, t)
                    for at, size, out in ((0, D, ps_qkv[:, 0:D]), (D, KV, ps_qkv[:, D:D + KV]), (D + KV, KV, ps_v[:, 0:KV])):
                        last = products(pe, out, lambda k: xT[u][:, 0, k, :],
                                        lambda k: xT[u][:, 1, k, :], lambda k: m.wqkv_h[:, k, at:at + size],
                                        lambda k: m.wqkv_l[:, k, at:at + size], KC)
                    last.then_inc(proj_done, 1)

                def tr(t, u):
                    pe.wait_ge(qhi_done, t + 1)
                    pe.wait_ge(qlo_done, t + 1)
                    pe.wait_ge(kst_done, t + 1)
                    after(pe, qevac, t)
                    after(pe, kevac, t)
                    for g, out in enumerate((ps_q[0], ps_q[1], ps_k)):
                        for r in range(8):
                            at = 2 * (8 * g + r)
                            last = pe.transpose(out[:, r, :], stack[u][:, at:at + 2, :], m.ident16[:, :])
                    last.then_inc(tr_done, 1)

                run_tiles(pe, TB, [(0, xt), (2, tr), (1, proj)])

            @block.scalar
            def _(act):
                def xhi(t, u):
                    after(act, xt_done, t - 1)
                    act.activation(x2[u][:, 0, :], m.X[:, t + b * TB, :], ACT.Copy).then_inc(xh_done, 1)

                def vals(t, u):
                    act.wait_ge(proj_done, t + 1)
                    act.activation(V[:, t, :, 0:HD], ps_v[:, 0:KV].rearrange(
                        "p (h d) -> p h d", d=HD), ACT.Copy, scale=1.0 / WS).then_inc(v_done, 1)

                def qhi(t, u):
                    act.wait_ge(rot_done, t + 1)
                    after(act, tr_done, t - 1)
                    for at in (0, 2 * HD):
                        last = act.activation(stack[u][:, 0:HQ, at:at + HD], rot[u][:, 0:HQ, :], ACT.Copy)
                    last.then_inc(qhi_done, 1)

                def evac(t, u):
                    act.wait_ge(tr_done, t + 1)
                    for g in range(2):
                        last = act.activation(QT[:, 8 * g:8 * g + 8, bass.ds(t * P, P)], ps_q[g][:, :, :], ACT.Copy)
                    last.then_inc(qevac, 1)

                act.wait_ge(init_done, 3)
                run_tiles(act, TB, [(0, xhi), (1, vals), (1, qhi), (2, evac)])

            @block.vector
            def _(dve):
                for u in range(2):
                    dve.memset(stack[u][:, :, 3 * HD:64], 0.0).then_inc(halves, 1)
                dve.wait_ge(halves, 2)
                for u in range(2):
                    dve.memset(stack[u][:, HQ:HB, 3 * HD:3 * HD + 1], 1.0).then_inc(init_done, 1)
                dve.memset(V[:, :, :, HD + 1:32], 0.0)
                dve.memset(V[:, :, :, HD:HD + 1], 1.0).then_inc(init_done, 1)

                def xevac(t, u):
                    dve.wait_ge(xt_done, t + 1)
                    after(dve, proj_done, t - 1)
                    dve.tensor_copy(xT[u][:, :, :, :], ps_xt[u][:, :, :, :]).then_inc(xt_evac, 1)

                def rope(t, u):
                    dve.wait_ge(proj_done, t + 1)
                    after(dve, qhi_done, t - 1)
                    after(dve, kst_done, t - 1)
                    H = HQ + HKV
                    qk = ps_qkv[:, 0:D + KV].rearrange("p (h d) -> p h d", d=HD)
                    cos = m.rope[:, 0, t, :][:, None, :].to_broadcast([P, H, HD])
                    dve.tensor_tensor(t1[u][:, :, :], qk, cos, ALU.mult)
                    pairs = qk.rearrange("p h (i e) -> p h i e", e=2)
                    outs = t2[u][:, :, :].rearrange("p h (i e) -> p h i e", e=2)
                    sins = m.rope[:, 1, t, :].rearrange("p (i e) -> p i e", e=2)
                    for e in range(2):
                        last = dve.tensor_tensor(outs[:, :, :, e], pairs[:, :, :, 1 - e],
                                                 sins[:, :, e][:, None, :].to_broadcast([P, H, HD // 2]), ALU.mult)
                    last.then_inc(rope_done, 1)

                def qlo(t, u):
                    dve.wait_ge(qhi_done, t + 1)
                    dve.tensor_tensor(stack[u][:, 0:HQ, HD:2 * HD], rot[u][:, 0:HQ, :], stack[u][:, 0:HQ, 0:HD],
                                      ALU.subtract).then_inc(qlo_done, 1)

                def evac(t, u):
                    dve.wait_ge(tr_done, t + 1)
                    for half in range(2):
                        r = slice(64 * half, 64 * half + 64)
                        last = dve.tensor_copy(KT[half][r, :, bass.ds(t * P, P)], ps_k[r, :, :])
                    last.then_inc(kevac, 1)

                if b == 0:
                    dve.wait_ge(kt_zero, 2)
                run_tiles(dve, TB, [(0, xevac), (1, rope), (1, qlo), (2, evac)])

            @block.gpsimd
            def _(pool):
                if b == 0:
                    for half in range(2):
                        pool.memset(KT[half][:, :, :], 0.0).then_inc(kt_zero, 1)
                pool.wait_ge(init_done, 3)

                def xlo(t, u):
                    pool.wait_ge(xh_done, t + 1)
                    after(pool, xt_done, t - 1)
                    pool.tensor_tensor(x2[u][:, 1, :], m.X[:, t + b * TB, :], x2[u][:, 0, :],
                                       ALU.subtract).then_inc(xl_done, 1)

                def rotate(t, u):
                    after(pool, tr_done, t - 1)
                    pool.wait_ge(rope_done, t + 1)
                    pool.tensor_tensor(rot[u][:, :, :], t1[u][:, :, :], t2[u][:, :, :], ALU.add).then_inc(rot_done, 1)

                def keys(t, u):
                    pool.wait_ge(rot_done, t + 1)
                    pool.tensor_tensor(pad[:, :], m.minus_half[:, :], m.minus_half[:, :], ALU.add)
                    k = rot[u][:, HQ:HQ + HKV, :]
                    blocks = stack[u][:, HQ:HB, :].rearrange("p (j c) d -> p j c d", c=2)
                    for c in range(2):
                        for at in (0, HD):
                            last = pool.tensor_copy(blocks[:, :, c, at:at + HD], k)
                    last.then_inc(khi_done, 1)
                    pool.wait_ge(khi_done, t + 1)
                    for c in range(2):
                        last = pool.tensor_tensor(blocks[:, :, c, 2 * HD:3 * HD], k, blocks[:, :, c, 0:HD], ALU.subtract)
                    last.then_inc(kst_done, 1)

                run_tiles(pool, TB, [(0, xlo), (1, rotate), (1, keys)])


def score_items():
    items = []
    for qt in range(TB):
        for c in range(1 + qt // 4):
            n = min(4, qt + 1 - 4 * c) * P
            per = 512 // n if n <= 256 else 1
            for h in range(0, GQ, per):
                items.append((qt, c, list(range(h, h + per)), n))
    return items


def attend(nc, m, b, QT, KT, V):
    S = score_items()
    T = [(qt, kt) for qt in range(TB) for kt in range(qt + 1)]
    PAIRS = len(T) // 2
    QUADS = PAIRS // 2
    assert len(T) % 4 == 0
    SPREAD = PAIRS - 4
    VC = HD + 1

    def events():
        out, ring = [], 0
        sums, later = [], []
        for j in range(-1, HKV):
            n = 0
            for p in range(PAIRS):
                g = j * PAIRS + p
                if j >= 0:
                    out.append(("t", g, j, p))
                upto = len(S) * (p + 1) // SPREAD if p < SPREAD else len(S)
                while j + 1 < HKV and n < upto:
                    out.append(("s", ring, j + 1, n))
                    ring, n = ring + 1, n + 1
                if j + 1 < HKV and p == SPREAD:
                    out.append(("m", ring, j + 1))
                    ring += 1
                for jj, qt in sums:
                    out.append(("c", ring, jj, qt))
                    ring += 1
                sums, later = later, []
                if j >= 0 and g % 2 and g >= 3:
                    out.append(("v", (g - 3) // 2))
                    later = ended((g - 3) // 2)
        for q in (HKV * QUADS - 1,):
            out.append(("v", q))
            later += ended(q)
        for jj, qt in sums + later:
            out.append(("c", ring, jj, qt))
            ring += 1
        return out

    def banks(q):
        j, at = q // QUADS, 4 * (q % QUADS)
        return [(2 * q + i // 2, i % 2, j, *T[at + i]) for i in range(4)]

    def ended(q):
        return [(j, qt) for _, _, j, qt, kt in banks(q) if kt == qt]

    EVENTS = events()
    summed = {e[2] * TB + e[3]: e[1] + 1 for e in EVENTS if e[0] == "c"}
    maxima = {e[2]: e[1] + 1 for e in EVENTS if e[0] == "m"}
    with Phase(nc, f"attn{b}") as f:
        prob = [f.sb(f"prob{u}", [P, 1024], F32) for u in range(4)]
        oT = [f.sb(f"oT{u}", [P, GQ, P], F32) for u in range(2)]
        mx = f.sb("mx", [P, 2, GQ, TB], F32)
        mm = f.sb("mm", [P, GQ, TB], F32)
        negm = f.sb("negm", [P, GQ, TB], F16)
        mT = f.sb("mT", [GQ * TB, P], F16)
        rec = [f.sb(f"rec{u}", [P, GQ], F32) for u in range(2)]
        ps_s = [f.ps(f"ps_s{u}", [P, 512], F32) for u in range(2)]
        ps_t = [f.ps(f"ps_t{u}", [P, 1024], F32) for u in range(2)]
        ps_o = [f.ps(f"ps_o{u}", [P, GQ, P], F32) for u in range(2)]
        ring_done, ring_free, mx_init, mm_done, negm_done, mt_in = f.sems(
            "ring_done ring_free mx_init mm_done negm_done mt_in")
        t_done, exp_done, v_done, o_evac, rec_done = f.sems("t_done exp_done v_done o_evac rec_done")

        with f.block() as block:
            @block.tensor
            def _(pe):
                for kind, *a in EVENTS:
                    if kind in "smc":
                        after(pe, ring_free, a[0] - 1)
                        bank = ps_s[a[0] % 2]
                    if kind == "s":
                        _, j, n = a
                        qt, c, heads, cols = S[n]
                        diagonal = c == qt // 4
                        for at, h in enumerate(heads):
                            out = bank[:, at * cols:(at + 1) * cols]
                            last = pe.matmul(out, QT[:, j * 2 + h // 2, qt * P:(qt + 1) * P],
                                             KT[h % 2][:, j, c * 512:c * 512 + cols], start=True, stop=not diagonal)
                            if diagonal:
                                last = pe.matmul(out[:, cols - P:cols], m.identb[:, :], m.masks16[:, 0, :],
                                                 start=False, stop=True)
                        last.then_inc(ring_done, 1)
                    if kind == "m":
                        pe.wait_ge(negm_done, a[1] + 1)
                        pe.transpose(bank[0:GQ * TB, 0:P // 2].bitcast(F16), negm[:, :, :],
                                     m.ident16[:, :]).then_inc(ring_done, 1)
                    if kind == "t":
                        g, j, p = a
                        if p == 0:
                            pe.wait_ge(mt_in, j * 32 + 32)
                        after(pe, exp_done, g - 1)
                        for i, (qt, kt) in enumerate(T[2 * p:2 * p + 2]):
                            for par in range(2):
                                out = ps_t[g % 2][:, i * 512 + par * 256:i * 512 + par * 256 + 256]
                                last = pe.matmul(out, KT[par][:, j, kt * P:(kt + 1) * P],
                                                 QT[:, 2 * j:2 * j + 2, qt * P:(qt + 1) * P],
                                                 start=True, stop=kt != qt)
                                if kt == qt:
                                    last = pe.matmul(out, m.identb[:, :], m.masks16[:, 1:3, :], start=False, stop=True)
                        last.then_inc(t_done, 1)
                    if kind == "v":
                        q, = a
                        pe.wait_ge(exp_done, 2 * q + 2)
                        for pair, half, j, qt, kt in banks(q):
                            if kt == 0:
                                after(pe, o_evac, j * TB + qt - 1)
                            c = kt % 4
                            pe.matmul(ps_o[(j * TB + qt) % 2][32 * c:32 * c + 32, :, :], V[:, kt, j, :],
                                      prob[pair % 4][:, half * 512:half * 512 + 512],
                                      start=kt < 4, stop=kt + 4 > qt, skip_group_check=True).then_inc(v_done, 1)
                    if kind == "c":
                        _, j, qt = a
                        o = j * TB + qt
                        rows = 32 * min(qt + 1, 4)
                        pe.wait_ge(o_evac, o + 1)
                        for slot in range(GQ):
                            last = pe.matmul(bank[:, slot * VC:(slot + 1) * VC], oT[o % 2][0:rows, slot, :],
                                             m.select[0:rows, 0:VC], start=True, stop=True)
                        last.then_inc(ring_done, 1)

            @block.scalar
            def _(act):
                for kind, *a in EVENTS:
                    if kind == "t":
                        g = a[0]
                        act.wait_ge(t_done, g + 1)
                        after(act, v_done, 2 * (g - 4) + 2)
                        act.activation(prob[g % 4][:, :], ps_t[g % 2][:, :], ACT.Exp,
                                       scale=HD ** -0.5).then_inc(exp_done, 1)
                    if kind == "v":
                        for i, (_, _, j, qt, kt) in enumerate(banks(a[0])):
                            if kt < qt:
                                continue
                            o = j * TB + qt
                            rows = 32 * min(qt + 1, 4)
                            act.wait_ge(v_done, 4 * a[0] + i + 1)
                            after(act, ring_done, summed.get(o - 2, 0))
                            act.activation(oT[o % 2][0:rows, :, :], ps_o[o % 2][0:rows, :, :],
                                           ACT.Copy).then_inc(o_evac, 1)

            @block.vector
            def _(dve):
                dve.memset(mx[:, 1, :, :], -3.0e38).then_inc(mx_init, 1)
                dve.wait_ge(mx_init, 1)
                for kind, *a in EVENTS:
                    if kind in "smc":
                        dve.wait_ge(ring_done, a[0] + 1)
                        bank = ps_s[a[0] % 2]
                    if kind == "s":
                        _, j, n = a
                        qt, c, heads, cols = S[n]
                        h = heads[0]
                        dve.tensor_reduce(mx[:, c, h:h + len(heads), qt],
                                          bank[:, 0:len(heads) * cols].rearrange("p (h k) -> p h k", k=cols),
                                          AX.X, ALU.max).then_inc(ring_free, 1)
                        if n == len(S) - 1:
                            dve.wait_ge(ring_free, a[0] + 1)
                            dve.tensor_tensor(mm[:, :, :], mx[:, 0, :, :], mx[:, 1, :, :], ALU.max).then_inc(mm_done, 1)
                            dve.wait_ge(mm_done, j + 1)
                            dve.tensor_scalar(negm[:, :, :].rearrange("p (e a) q -> p a e q", e=2),
                                              mm[:, :, :].rearrange("p (a e) q -> p a e q", e=2), -1.0, None,
                                              ALU.mult).then_inc(negm_done, 1)
                    if kind == "m":
                        after(dve, mt_in, a[1] * 32)
                        dve.tensor_copy(mT[:, :], bank[0:GQ * TB, 0:P // 2].bitcast(F16)).then_inc(ring_free, 1)
                    if kind == "c":
                        _, j, qt = a
                        u = qt % 2
                        o = bank[:, 0:GQ * VC].rearrange("p (s v) -> p s v", v=VC)
                        dve.reciprocal(rec[u][:, :], o[:, :, HD]).then_inc(rec_done, 1)
                        dve.wait_ge(rec_done, j * TB + qt + 1)
                        out = m.O[:, qt, j * GQ * HD:(j + 1) * GQ * HD]
                        dve.tensor_tensor(out.rearrange("p (a e v) -> p e a v", a=2, e=2),
                                          o[:, :, 0:HD].rearrange("p (e a) v -> p e a v", e=2),
                                          rec[u][:, :].rearrange("p (e a) -> p e a", e=2)[:, :, :, None]
                                          .to_broadcast([P, 2, 2, HD]), ALU.mult).then_inc(ring_free, 1)

            @block.sync
            def _(sp):
                R = 2 * TB
                for j in range(HKV):
                    sp.wait_ge(ring_free, maxima[j])
                    for par in range(2):
                        row = 64 * par + 3 * HD
                        sp.dma_start(QT[row:row + 1, 2 * j:2 * j + 2, :], mT[par * R:(par + 1) * R, :]).then_inc(mt_in, 16)


class LayerNorm:

    def __init__(self, f, m, name, eps, n=1):
        self.n, self.m, self.eps = n, m, eps
        self.stats = [f.sb(f"{name}_stats{u}", [P, n, 6], F32) for u in range(2)]
        self.pad = f.sb(f"{name}_pad", [P, 1], F32)
        self.mv = [f.sb(f"{name}_mv{u}", [P, 2], F32) for u in range(2)]
        self.var = [f.sb(f"{name}_var{u}", [P, 1], F32) for u in range(2)]
        self.rstd = [f.sb(f"{name}_rstd{u}", [P, 1], F32) for u in range(2)]
        self.s_stats, self.s_mv, self.s_var, self.s_rstd, self.s_used = f.sems(
            f"{name}_stats {name}_mv {name}_var {name}_rstd {name}_used")

    def statistics(self, dve, x, t, u):
        for c in range(self.n):
            last = dve.bn_stats(self.stats[u][:, c, :], x[:, c, :])
        last.then_inc(self.s_stats, 1)
        dve.wait_ge(self.s_stats, t + 1)
        dve.memset(self.pad[:, :], 0.0)
        dve.bn_aggr(self.mv[u][:, :], self.stats[u][:, :, :]).then_inc(self.s_mv, 1)
        dve.wait_ge(self.s_mv, t + 1)
        dve.tensor_scalar(self.var[u][:, :], self.mv[u][:, 1:2], self.eps, None, ALU.add).then_inc(self.s_var, 1)

    def root(self, pool, t, u):
        pool.wait_ge(self.s_var, t + 1)
        after(pool, self.s_used, t - 1)
        pool.tensor_tensor(self.rstd[u][:, :], self.var[u][:, :], self.m.minus_half[:, :],
                           ALU.pow).then_inc(self.s_rstd, 1)

    def normalize(self, dve, out, x, t, u):
        dve.wait_ge(self.s_rstd, t + 1)
        dve.tensor_scalar(out, x, self.mv[u][:, 0:1], self.rstd[u][:, :], ALU.subtract, ALU.mult).then_inc(self.s_used, 1)


def attention_output(nc, m, b):
    with Phase(nc, f"wo{b}") as f:
        o2 = [f.sb(f"o2{u}", [P, 2, D], F16) for u in range(2)]
        oT = [f.sb(f"oT{u}", [P, 2, KC, P], F16) for u in range(2)]
        r = [f.sb(f"r{u}", [P, D], F32) for u in range(2)]
        ps_ot = [f.ps(f"ps_ot{u}", [P, 2, KC, P], F16) for u in range(2)]
        ps_y = [f.ps(f"ps_y{u}", [P, D], F32) for u in range(2)]
        oh_done, ol_done, ot_done, ot_evac, y_done, r_done = f.sems("oh_done ol_done ot_done ot_evac y_done r_done")
        ln = LayerNorm(f, m, "ln", 1e-5)
        with f.block() as block:
            @block.tensor
            def _(pe):
                def ot(t, u):
                    pe.wait_ge(ol_done, t + 1)
                    after(pe, ot_evac, t - 1)
                    transpose_parts(pe, ps_ot[u], o2[u], m).then_inc(ot_done, 1)

                def wo(t, u):
                    pe.wait_ge(ot_evac, t + 1)
                    after(pe, r_done, t - 1)
                    products(pe, ps_y[u][:, :], lambda k: oT[u][:, 0, k, :], lambda k: oT[u][:, 1, k, :],
                             lambda k: m.wo_h[:, k, :], lambda k: m.wo_l[:, k, :], KC).then_inc(y_done, 1)

                run_tiles(pe, TB, [(0, ot), (1, wo)])

            @block.scalar
            def _(act):
                def hi(t, u):
                    after(act, ot_done, t - 1)
                    act.activation(o2[u][:, 0, :], m.O[:, t, :], ACT.Copy).then_inc(oh_done, 1)

                run_tiles(act, TB, [(0, hi)])

            @block.vector
            def _(dve):
                def oevac(t, u):
                    dve.wait_ge(ot_done, t + 1)
                    after(dve, y_done, t - 1)
                    dve.tensor_copy(oT[u][:, :, :, :], ps_ot[u][:, :, :, :]).then_inc(ot_evac, 1)

                def residual(t, u):
                    dve.wait_ge(y_done, t + 1)
                    dve.scalar_tensor_tensor(r[u][:, :], ps_y[u][:, :], 1.0 / WS, m.X[:, t + b * TB, :],
                                             ALU.mult, ALU.add).then_inc(r_done, 1)
                    dve.wait_ge(r_done, t + 1)
                    ln.statistics(dve, r[u][:, None, :], t, u)

                def norm(t, u):
                    ln.normalize(dve, m.X[:, t + b * TB, :], r[u][:, :], t, u)

                run_tiles(dve, TB, [(0, oevac), (2, norm), (1, residual)])

            @block.gpsimd
            def _(pool):
                def lo(t, u):
                    pool.wait_ge(oh_done, t + 1)
                    after(pool, ot_done, t - 1)
                    pool.tensor_tensor(o2[u][:, 1, :], m.O[:, t, :], o2[u][:, 0, :], ALU.subtract).then_inc(ol_done, 1)

                run_tiles(pool, TB, [(0, lo), (1, lambda t, u: ln.root(pool, t, u))])


class AbsmaxQuantizer:
    LIMIT = (128.0 - 1e-6) / 128.0

    def __init__(self, f, name):
        self.g = [f.sb(f"{name}_g{u}", [P, 1], F32) for u in range(2)]
        self.limit = [f.sb(f"{name}_limit{u}", [P, 2], F32) for u in range(2)]
        self.s_max, self.s_limit, self.s_clipped = f.sems(f"{name}_max {name}_limit {name}_clipped")

    def apply(self, dve, x, t, u):
        dve.tensor_reduce(self.g[u][:, :], x, AX.X, ALU.max, apply_absolute_value=True).then_inc(self.s_max, 1)
        dve.wait_ge(self.s_max, t + 1)
        for n, sign in enumerate((1.0, -1.0)):
            dve.tensor_scalar(self.limit[u][:, n:n + 1], self.g[u][:, :], sign * self.LIMIT, None,
                              ALU.mult).then_inc(self.s_limit, 1)
        dve.wait_ge(self.s_limit, t * 2 + 2)
        dve.tensor_scalar(x, x, self.limit[u][:, 0:1], self.limit[u][:, 1:2], ALU.min,
                          ALU.max).then_inc(self.s_clipped, 1)


def ternary_ffn(nc, m):
    NB = FF // D
    NK = FF // P
    with Phase(nc, "ffn") as f:
        xn = [f.sb(f"xn{u}", [P, D], F32) for u in range(2)]
        x2 = [f.sb(f"x2{u}", [P, 2, D], F16) for u in range(2)]
        xT = [f.sb(f"xT{u}", [P, 2, KC, P], F16) for u in range(2)]
        h = [f.sb(f"h{u}", [P, NB, D], F32) for u in range(2)]
        h2 = [f.sb(f"h2{u}", [P, 2, FF], F16) for u in range(2)]
        hT = [f.sb(f"hT{u}", [P, 2, NK, P], F16) for u in range(2)]
        r = [f.sb(f"r{u}", [P, D], F32) for u in range(2)]
        ps_x = f.ps("ps_x", [P, 2, KC, P], F16)
        ps_fc = [f.ps(f"ps_fc{n}", [P, D], F32) for n in range(NB)]
        ps_h = [f.ps(f"ps_h{n}", [P, 8, P], F16) for n in range(2)]
        ps_y = f.ps("ps_y", [P, D], F32)
        ln_x = LayerNorm(f, m, "lnx", 1e-6)
        ln_h = LayerNorm(f, m, "lnh", 1e-6, NB)
        ln_r = LayerNorm(f, m, "lnr", 1e-5)
        q_x, q_h = AbsmaxQuantizer(f, "qx"), AbsmaxQuantizer(f, "qh")
        xh_done, xl_done, xt_done, xt_evac, fc_done, gelu_done = f.sems("xh_done xl_done xt_done xt_evac fc_done gelu_done")
        hh_done, hl_done, ht_done, ht_evac_a, ht_evac_d, y_done, r_done = f.sems(
            "hh_done hl_done ht_done ht_evac_a ht_evac_d y_done r_done")

        def part_of(g):
            return g // 2, (g % 2) * 8

        with f.block() as block:
            @block.tensor
            def _(pe):
                def xt(t, u):
                    pe.wait_ge(xh_done, t + 1)
                    pe.wait_ge(xl_done, t + 1)
                    after(pe, xt_evac, t)
                    transpose_parts(pe, ps_x, x2[u], m).then_inc(xt_done, 1)

                def fc(t, u):
                    pe.wait_ge(xt_evac, t + 1)
                    for n in range(NB):
                        after(pe, gelu_done, t * NB - (NB - n - 1))
                        for k in range(KC):
                            for part in range(2):
                                last = pe.matmul(ps_fc[n][:, :], xT[u][:, part, k, :],
                                                 m.wfcT[:, k, n * D:(n + 1) * D],
                                                 start=(k == 0 and part == 0), stop=(k == KC - 1 and part == 1))
                        last.then_inc(fc_done, 1)

                def ht(t, u):
                    pe.wait_ge(hh_done, t + 1)
                    pe.wait_ge(hl_done, t + 1)
                    for g in range(4):
                        part, k0 = part_of(g)
                        after(pe, (ht_evac_a, ht_evac_d)[g % 2], t * 2 + g // 2)
                        for k in range(8):
                            last = pe.transpose(ps_h[g % 2][:, k, :],
                                                h2[u][:, part, (k0 + k) * P:(k0 + k + 1) * P], m.ident16[:, :])
                        last.then_inc(ht_done, 1)

                def proj(t, u):
                    pe.wait_ge(ht_evac_a, t * 2 + 2)
                    pe.wait_ge(ht_evac_d, t * 2 + 2)
                    after(pe, r_done, t)
                    for part in range(2):
                        for k in range(NK):
                            last = pe.matmul(ps_y[:, :], hT[u][:, part, k, :], m.wprojT[:, k, :],
                                             start=(k == 0 and part == 0), stop=(k == NK - 1 and part == 1))
                    last.then_inc(y_done, 1)

                run_tiles(pe, NT, [(5, ht), (2, fc), (5, proj), (1, xt)])

            def evacuate(eng, copy, sem, odd):
                def evac(t, u):
                    after(eng, y_done, t - 1)
                    for g in (odd, 2 + odd):
                        part, k0 = part_of(g)
                        eng.wait_ge(ht_done, t * 4 + g + 1)
                        copy(hT[u][:, part, k0:k0 + 8, :], ps_h[odd][:, :, :]).then_inc(sem, 1)
                return evac

            @block.scalar
            def _(act):
                def xhi(t, u):
                    act.wait_ge(q_x.s_clipped, t + 1)
                    after(act, xt_done, t - 1)
                    act.activation(x2[u][:, 0, :], xn[u][:, :], ACT.Copy).then_inc(xh_done, 1)

                def gelu(t, u):
                    after(act, hl_done, t - 1)
                    for n in range(NB):
                        act.wait_ge(fc_done, t * NB + n + 1)
                        act.activation(h[u][:, n, :], ps_fc[n][:, :], ACT.Gelu, scale=m.gamma[:, 0:1]).then_inc(gelu_done, 1)

                def hhi(t, u):
                    act.wait_ge(q_h.s_clipped, t + 1)
                    after(act, ht_done, t * 4 - 4)
                    act.activation(h2[u][:, 0, :], h[u][:, :, :], ACT.Copy).then_inc(hh_done, 1)

                copy = lambda out, in_: act.activation(out, in_, ACT.Copy)
                run_tiles(act, NT, [(5, evacuate(act, copy, ht_evac_a, 0)), (4, hhi), (2, gelu), (1, xhi)])

            @block.vector
            def _(dve):
                def x_stats(t, u):
                    ln_x.statistics(dve, m.X[:, t, :][:, None, :], t, u)

                def x_norm(t, u):
                    after(dve, xl_done, t - 1)
                    ln_x.normalize(dve, xn[u][:, :], m.X[:, t, :], t, u)
                    dve.wait_ge(ln_x.s_used, t + 1)
                    q_x.apply(dve, xn[u][:, :], t, u)

                def x_evac(t, u):
                    dve.wait_ge(xt_done, t + 1)
                    after(dve, fc_done, t * NB - NB)
                    dve.tensor_copy(xT[u][:, :, :, :], ps_x[:, :, :, :]).then_inc(xt_evac, 1)

                def h_stats(t, u):
                    dve.wait_ge(gelu_done, t * NB + NB)
                    ln_h.statistics(dve, h[u], t, u)

                def h_norm(t, u):
                    ln_h.normalize(dve, h[u][:, :, :], h[u][:, :, :], t, u)
                    dve.wait_ge(ln_h.s_used, t + 1)
                    q_h.apply(dve, h[u][:, :, :].rearrange("p n k -> p (n k)"), t, u)

                def residual(t, u):
                    dve.wait_ge(y_done, t + 1)
                    dve.scalar_tensor_tensor(r[u][:, :], ps_y[:, :], m.gamma[:, 1:2], m.X[:, t, :],
                                             ALU.mult, ALU.add).then_inc(r_done, 1)
                    dve.wait_ge(r_done, t + 1)
                    ln_r.statistics(dve, r[u][:, None, :], t, u)

                def norm(t, u):
                    ln_r.normalize(dve, m.X[:, t, :], r[u][:, :], t, u)

                run_tiles(dve, NT, [(7, norm), (6, residual), (5, evacuate(dve, dve.tensor_copy, ht_evac_d, 1)),
                                    (4, h_norm), (3, h_stats), (1, x_norm), (1, x_evac), (0, x_stats)])

            @block.gpsimd
            def _(pool):
                def xlo(t, u):
                    pool.wait_ge(xh_done, t + 1)
                    after(pool, xt_done, t - 1)
                    pool.tensor_tensor(x2[u][:, 1, :], xn[u][:, :], x2[u][:, 0, :], ALU.subtract).then_inc(xl_done, 1)

                def hlo(t, u):
                    pool.wait_ge(hh_done, t + 1)
                    after(pool, ht_done, t * 4 - 4)
                    pool.tensor_tensor(h2[u][:, 1, :], h[u][:, :, :].rearrange("p n k -> p (n k)"), h2[u][:, 0, :],
                                       ALU.subtract).then_inc(hl_done, 1)

                run_tiles(pool, NT, [(6, lambda t, u: ln_r.root(pool, t, u)), (3, lambda t, u: ln_h.root(pool, t, u)),
                                     (4, hlo), (1, xlo), (0, lambda t, u: ln_x.root(pool, t, u))])


def linear_weights(nc, m, d):
    names = ("Wqk", "Wv", "Wu", "Wo")
    with Phase(nc, "linw") as f:
        raw = [f.sb(f"raw{n}", [P, KC, D], F32) for n in names]
        brow = f.sb("brow", [LO_ROW + 1, 4, D], F32)
        w_in = [f.sem(f"in_{n}") for n in names]
        b_in, b_zero, bh_done, ones_done, hi_done, lo_done, bl_done = f.sems(
            "b_in b_zero bh_done ones_done hi_done lo_done bl_done")
        with f.block() as block:
            @block.sync
            def _(sp):
                for i, n in enumerate(names):
                    sp.dma_start(raw[i][:, :, :], d[f"L1_attn_{n}"].rearrange("(k p) n -> p k n", p=P)).then_inc(w_in[i], 16)
                for i, n in enumerate(("ln_g", "ln_b")):
                    sp.dma_start(m.ln_gb[:, i, :], d[f"L1_attn_{n}"][None, :].to_broadcast([P, D])).then_inc(m.gb_in, 16)

            @block.gpsimd
            def _(pool):
                pool.memset(brow[:, :, :], 0.0).then_inc(b_zero, 1)
                pool.memset(m.ones_row[:, :], 1.0).then_inc(ones_done, 1)
                pool.wait_ge(b_zero, 1)
                for i, n in enumerate(("bqk", "bv", "bu", "bo")):
                    for row in (0, LO_ROW):
                        pool.dma_start(brow[row:row + 1, i, :], d[f"L1_attn_{n}"][None, :]).then_inc(b_in, 16)

            @block.scalar
            def _(act):
                for i in range(4):
                    act.wait_ge(w_in[i], 16)
                    act.activation(m.w1[:, 0, i, :, :], raw[i][:, :, :], ACT.Copy, scale=WS).then_inc(hi_done, 1)
                act.wait_ge(b_in, 16 * 8)
                act.activation(m.bias[:, :, :], brow[:, :, :], ACT.Copy, scale=WS).then_inc(bh_done, 1)

            @block.vector
            def _(dve):
                for i in range(4):
                    dve.wait_ge(hi_done, i + 1)
                    dve.scalar_tensor_tensor(m.w1[:, 1, i, :, :], raw[i][:, :, :], WS, m.w1[:, 0, i, :, :],
                                             ALU.mult, ALU.subtract).then_inc(lo_done, 1)
                dve.wait_ge(bh_done, 1)
                low = slice(LO_ROW, LO_ROW + 1)
                dve.scalar_tensor_tensor(m.bias[low, :, :], brow[low, :, :], WS, m.bias[low, :, :],
                                         ALU.mult, ALU.subtract).then_inc(bl_done, 1)


def biased(pe, m, out, i, xT):
    pe.matmul(out, m.ones_row[:, :], m.bias[:, i, :], start=True, stop=False)
    for k in range(KC):
        for n, (a, b) in enumerate(((0, 0), (0, 1), (1, 0))):
            last = pe.matmul(out, xT[:, a, k, :], m.w1[:, b, i, k, :], start=False, stop=(k == KC - 1 and n == 2))
    return last


def linear_features(nc, m, b):
    with Phase(nc, f"lin{b}") as f:
        x2 = [f.sb(f"x2{u}", [P, 2, D], F16) for u in range(2)]
        xT = [f.sb(f"xT{u}", [P, 2, KC, P], F16) for u in range(2)]
        e = [f.sb(f"e{u}", [P, D], F32) for u in range(2)]
        relu = [f.sb(f"relu{u}", [P, D], F32) for u in range(2)]
        k1 = [f.sb(f"k1{u}", [P, D], F32) for u in range(2)]
        tanh = [f.sb(f"tanh{u}", [P, 2, D], F32) for u in range(2)]
        k_ = [f.sb(f"k{u}", [P, D], F32) for u in range(2)]
        v_ = [f.sb(f"v{u}", [P, D], F32) for u in range(2)]
        ps_x = f.ps("ps_x", [P, 2, KC, P], F16)
        ps_z = [f.ps(f"ps_z{n}", [P, D], F32) for n in range(3)]
        ps_kv = f.ps("ps_kv", [P, KC, P], F32)
        ps_k = f.ps("ps_k", [P, KC, P], F32)
        xh_done, xl_done, xt_done, xt_evac, z_done, e_done, tanh_done, relu_done, k1_done = f.sems(
            "xh_done xl_done xt_done xt_evac z_done e_done tanh_done relu_done k1_done")
        k_done, v_done, u_done, kv_done, kt_done, kth_done, ktl_done, kvh_done, kvl_done, zero_done = f.sems(
            "k_done v_done u_done kv_done kt_done kth_done ktl_done kvh_done kvl_done zero_done")
        with f.block() as block:
            @block.tensor
            def _(pe):
                def xt(t, u):
                    pe.wait_ge(xl_done, t + 1)
                    after(pe, xt_evac, t)
                    transpose_parts(pe, ps_x, x2[u], m).then_inc(xt_done, 1)

                def z(t, u):
                    pe.wait_ge(xt_evac, t + 1)
                    for n, sem in enumerate((relu_done, v_done, u_done)):
                        after(pe, sem, t)
                        biased(pe, m, ps_z[n][:, :], n, xT[u]).then_inc(z_done, 1)

                def kv(t, u):
                    pe.wait_ge(k_done, t + 1)
                    pe.wait_ge(v_done, t + 1)
                    for g in range(KC):
                        s = slice(g * P, (g + 1) * P)
                        last = pe.matmul(ps_kv[:, g, :], k_[u][:, s], v_[u][:, s],
                                         start=isinstance(t, int) and t == 0 and g == 0,
                                         stop=isinstance(t, int) and t == TB - 1 and g == KC - 1)
                    last.then_inc(kv_done, 1)
                    after(pe, kth_done, t)
                    after(pe, ktl_done, t)
                    for g in range(KC):
                        last = pe.transpose(ps_k[:, g, :], k_[u][:, g * P:(g + 1) * P], m.ident)
                    last.then_inc(kt_done, 1)

                run_tiles(pe, TB, [(1, xt), (2, z), (3, kv)])

            @block.scalar
            def _(act):
                def xhi(t, u):
                    after(act, xt_done, t - 1)
                    act.activation(x2[u][:, 0, :], m.X[:, t + b * TB, :], ACT.Copy).then_inc(xh_done, 1)

                def nonlinear(t, u):
                    after(act, k1_done, t - 1)
                    act.wait_ge(z_done, t * 3 + 1)
                    act.activation(e[u][:, :], ps_z[0][:, :], ACT.Exp, scale=1.0 / WS).then_inc(e_done, 1)
                    after(act, u_done, t - 1)
                    for n in range(2):
                        act.wait_ge(z_done, t * 3 + 2 + n)
                        act.activation(tanh[u][:, n, :], ps_z[1 + n][:, :], ACT.Tanh, scale=0.5 / WS).then_inc(tanh_done, 1)

                def kt_hi(t, u):
                    act.wait_ge(kt_done, t + 1)
                    act.activation(m.kT[:, 0, :, bass.ds(t * P, P)], ps_k[:, :, :], ACT.Copy).then_inc(kth_done, 1)

                run_tiles(act, TB, [(0, xhi), (2, nonlinear), (3, kt_hi)])
                act.wait_ge(zero_done, 2)
                act.wait_ge(kv_done, TB)
                for a in range(4):
                    s = slice(a * DL, (a + 1) * DL)
                    act.activation(m.kv[s, 0, :, s], ps_kv[s, :, s], ACT.Copy, scale=KV_SCALE / (2 * WS)).then_inc(kvh_done, 1)

            @block.vector
            def _(dve):
                for part in range(2):
                    dve.memset(m.kv[:, part, :, :], 0.0).then_inc(zero_done, 1)

                def xevac(t, u):
                    dve.wait_ge(xt_done, t + 1)
                    after(dve, z_done, t * 3 - 3)
                    dve.tensor_copy(xT[u][:, :, :, :], ps_x[:, :, :, :]).then_inc(xt_evac, 1)

                def features(t, u):
                    dve.wait_ge(e_done, t + 1)
                    after(dve, k_done, t - 1)
                    dve.tensor_scalar(relu[u][:, :], ps_z[0][:, :], 0.0, 1.0 / WS, ALU.max, ALU.mult).then_inc(relu_done, 1)
                    dve.wait_ge(relu_done, t + 1)
                    dve.scalar_tensor_tensor(k1[u][:, :], e[u][:, :], 1.0, relu[u][:, :], ALU.min, ALU.add).then_inc(k1_done, 1)
                    dve.wait_ge(tanh_done, t * 2 + 1)
                    after(dve, kv_done, t - 1)
                    dve.scalar_tensor_tensor(v_[u][:, :], tanh[u][:, 0, :], 1.0, ps_z[1][:, :], ALU.add, ALU.mult).then_inc(v_done, 1)
                    dve.wait_ge(tanh_done, t * 2 + 2)
                    dve.scalar_tensor_tensor(m.U[:, t, :], tanh[u][:, 1, :], 1.0, ps_z[2][:, :], ALU.add, ALU.mult).then_inc(u_done, 1)

                def kt_lo(t, u):
                    dve.wait_ge(kth_done, t + 1)
                    s = bass.ds(t * P, P)
                    dve.tensor_tensor(m.kT[:, 1, :, s], ps_k[:, :, :], m.kT[:, 0, :, s], ALU.subtract).then_inc(ktl_done, 1)

                run_tiles(dve, TB, [(1, xevac), (2, features), (3, kt_lo)])
                dve.wait_ge(zero_done, 2)
                for a in range(4):
                    s = slice(a * DL, (a + 1) * DL)
                    dve.wait_ge(kvh_done, a + 1)
                    dve.scalar_tensor_tensor(m.kv[s, 1, :, s], ps_kv[s, :, s], KV_SCALE / (2 * WS), m.kv[s, 0, :, s],
                                             ALU.mult, ALU.subtract).then_inc(kvl_done, 1)

            @block.gpsimd
            def _(pool):
                def xlo(t, u):
                    pool.wait_ge(xh_done, t + 1)
                    after(pool, xt_done, t - 1)
                    pool.tensor_tensor(x2[u][:, 1, :], m.X[:, t + b * TB, :], x2[u][:, 0, :], ALU.subtract).then_inc(xl_done, 1)

                def minus_one(t, u):
                    pool.wait_ge(k1_done, t + 1)
                    after(pool, kt_done, t - 1)
                    pool.tensor_tensor(k_[u][:, :], k1[u][:, :], m.ones[:, 0:1].to_broadcast([P, D]), ALU.subtract).then_inc(k_done, 1)

                run_tiles(pool, TB, [(0, xlo), (2, minus_one)])


def linear_output(nc, m, b):
    with Phase(nc, f"lino{b}") as f:
        w = [f.sb(f"w{u}", [P, D], F32) for u in range(2)]
        n1 = [f.sb(f"n1{u}", [P, D], F32) for u in range(2)]
        n2 = [f.sb(f"n2{u}", [P, D], F32) for u in range(2)]
        w2 = [f.sb(f"w2{u}", [P, 2, D], F16) for u in range(2)]
        wT = [f.sb(f"wT{u}", [P, 2, KC, P], F16) for u in range(2)]
        r = [f.sb(f"r{u}", [P, D], F32) for u in range(2)]
        ps_q = [f.ps(f"ps_q{u}", [P, KC, P], F32) for u in range(2)]
        ps_w = [f.ps(f"ps_w{u}", [P, 2, KC, P], F16) for u in range(2)]
        ps_y = [f.ps(f"ps_y{u}", [P, D], F32) for u in range(2)]
        ln_q = LayerNorm(f, m, "lnq", 1e-5 * KV_SCALE ** 2)
        ln_r = LayerNorm(f, m, "lnr", 1e-5)
        q_done, n1_done, n2_done, w_done, wh_done, wl_done, wt_done, wt_evac, y_done, r_done = f.sems(
            "q_done n1_done n2_done w_done wh_done wl_done wt_done wt_evac y_done r_done")
        with f.block() as block:
            @block.tensor
            def _(pe):
                def q(t, u):
                    after(pe, n1_done, t - 1)
                    s = bass.ds(t * P, P)
                    for g in range(KC):
                        for n, (a, c) in enumerate(((0, 0), (0, 1), (1, 0))):
                            last = pe.matmul(ps_q[u][:, g, :], m.kT[:, a, g, s], m.kv[:, c, g, :], start=(n == 0), stop=(n == 2))
                    last.then_inc(q_done, 1)

                def wt(t, u):
                    pe.wait_ge(wl_done, t + 1)
                    after(pe, wt_evac, t - 1)
                    transpose_parts(pe, ps_w[u], w2[u], m).then_inc(wt_done, 1)

                def wo(t, u):
                    pe.wait_ge(wt_evac, t + 1)
                    after(pe, r_done, t - 1)
                    biased(pe, m, ps_y[u][:, :], 3, wT[u]).then_inc(y_done, 1)

                run_tiles(pe, TB, [(3, wo), (2, wt), (0, q)])

            @block.scalar
            def _(act):
                def whi(t, u):
                    act.wait_ge(w_done, t + 1)
                    after(act, wt_done, t - 1)
                    act.activation(w2[u][:, 0, :], w[u][:, :], ACT.Copy).then_inc(wh_done, 1)

                def wevac(t, u):
                    act.wait_ge(wt_done, t + 1)
                    after(act, y_done, t - 1)
                    act.activation(wT[u][:, :, :, :], ps_w[u][:, :, :, :], ACT.Copy).then_inc(wt_evac, 1)

                run_tiles(act, TB, [(1, whi), (2, wevac)])

            @block.vector
            def _(dve):
                def stats(t, u):
                    dve.wait_ge(q_done, t + 1)
                    ln_q.statistics(dve, ps_q[u][:, :, :].rearrange("p g n -> p (g n)")[:, None, :], t, u)

                def gate(t, u):
                    dve.scalar_tensor_tensor(n1[u][:, :], ps_q[u][:, :, :].rearrange("p g n -> p (g n)"),
                                             ln_q.mv[u][:, 0:1], m.ln_gb[:, 0, :], ALU.subtract, ALU.mult).then_inc(n1_done, 1)
                    dve.wait_ge(n1_done, t + 1)
                    dve.wait_ge(ln_q.s_rstd, t + 1)
                    dve.scalar_tensor_tensor(n2[u][:, :], n1[u][:, :], ln_q.rstd[u][:, :], m.ln_gb[:, 1, :],
                                             ALU.mult, ALU.add).then_inc(ln_q.s_used, 1)
                    dve.wait_ge(ln_q.s_used, t + 1)
                    after(dve, wl_done, t - 1)
                    dve.scalar_tensor_tensor(w[u][:, :], m.U[:, t, :], 0.5 / WS, n2[u][:, :], ALU.mult, ALU.mult).then_inc(w_done, 1)

                def residual(t, u):
                    dve.wait_ge(y_done, t + 1)
                    dve.scalar_tensor_tensor(r[u][:, :], ps_y[u][:, :], 1.0 / WS, m.X[:, t + b * TB, :],
                                             ALU.mult, ALU.add).then_inc(r_done, 1)
                    dve.wait_ge(r_done, t + 1)
                    ln_r.statistics(dve, r[u][:, None, :], t, u)

                def norm(t, u):
                    ln_r.normalize(dve, m.X[:, t + b * TB, :], r[u][:, :], t, u)

                if b == 0:
                    dve.wait_ge(m.gb_in, 32)
                run_tiles(dve, TB, [(4, norm), (1, gate), (0, stats), (3, residual)])

            @block.gpsimd
            def _(pool):
                def wlo(t, u):
                    pool.wait_ge(wh_done, t + 1)
                    after(pool, wt_done, t - 1)
                    pool.tensor_tensor(w2[u][:, 1, :], w[u][:, :], w2[u][:, 0, :], ALU.subtract).then_inc(wl_done, 1)

                run_tiles(pool, TB, [(1, wlo), (0, lambda t, u: ln_q.root(pool, t, u)),
                                     (3, lambda t, u: ln_r.root(pool, t, u))])


def linear_attention(nc, m, d):
    with ExitStack() as ctx:
        def sb(name, shape, dt):
            return ctx.enter_context(nc.sbuf_tensor(name, shape, dt))

        m.w1 = sb("w1", [P, 2, 4, KC, D], F16)
        m.bias = sb("bias", [LO_ROW + 1, 4, D], F16)
        m.ones_row = sb("ones_row", [LO_ROW + 1, P], F16)
        m.ln_gb = sb("ln_gb", [P, 2, D], F32)
        m.gb_in = ctx.enter_context(nc.semaphore("gb_in"))
        linear_weights(nc, m, d)
        m.kT = sb("kT", [P, 2, KC, N], F16)
        m.kv = sb("kv", [P, 2, KC, P], F16)
        m.U = sb("U", [P, TB, D], F32)
        for b in range(B):
            linear_features(nc, m, b)
            linear_output(nc, m, b)


def route(nc, m, d):
    with Phase(nc, "route") as f:
        gate = f.sb("gate", [NE, D], F32)
        gT = f.sb("gT", [P, 2, KC, NE], F16)
        x2 = [f.sb(f"x2{u}", [P, 2, D], F16) for u in range(2)]
        logits = f.sb("logits", [P, NT, NE], F32)
        top = f.sb("top", [P, NT], F32)
        shifted = f.sb("shifted", [P, NT, NE], F32)
        e = f.sb("e", [P, NT, NE], F32)
        total = f.sb("total", [P, NT], F32)
        rec = f.sb("rec", [P, NT], F32)
        probs = f.sb("probs", [P, 2, NT, NE], F32)
        ranked = f.sb("ranked", [P, 2, NT, NE], F32)
        code = f.sb("code", [P, 2, NT], F32)
        ps_g = f.ps("ps_g", [P, KC, NE], F32)
        ps_x = [f.ps(f"ps_x{u}", [P, 2, KC, P], F16) for u in range(2)]
        ps_l = [f.ps(f"ps_l{u}", [P, NE], F32) for u in range(2)]
        gate_in, g_done, gh_done, gl_done, xh_done, xl_done, xt_done, xt_evac, l_done, l_evac = f.sems(
            "gate_in g_done gh_done gl_done xh_done xl_done xt_done xt_evac l_done l_evac")
        step, exp_done = f.sems("step exp_done")
        with f.block() as block:
            @block.sync
            def _(sp):
                sp.dma_start(gate[:, :], d["L1_ffn_gate_w"]).then_inc(gate_in, 16)

            @block.tensor
            def _(pe):
                pe.wait_ge(gate_in, 16)
                for k in range(KC):
                    last = pe.transpose(ps_g[:, k, :], gate[:, k * P:(k + 1) * P], m.ident[0:NE, 0:NE])
                last.then_inc(g_done, 1)

                def xt(t, u):
                    pe.wait_ge(xl_done, t + 1)
                    after(pe, xt_evac, t - 1)
                    transpose_parts(pe, ps_x[u], x2[u], m).then_inc(xt_done, 1)

                def logit(t, u):
                    pe.wait_ge(xt_evac, t + 1)
                    after(pe, l_evac, t - 1)
                    s = bass.ds(t * P, P)
                    for k in range(KC):
                        for n, (a, c) in enumerate(((0, 0), (0, 1), (1, 0), (1, 1))):
                            last = pe.matmul(ps_l[u][:, :], m.xT3[:, a, k, s], gT[:, c, k, :],
                                             start=(k == 0 and n == 0), stop=(k == KC - 1 and n == 3))
                    last.then_inc(l_done, 1)

                pe.wait_ge(gl_done, 1)
                run_tiles(pe, NT, [(0, xt), (1, logit)])

            @block.scalar
            def _(act):
                act.wait_ge(g_done, 1)
                act.activation(gT[:, 0, :, :], ps_g[:, :, :], ACT.Copy, scale=WS).then_inc(gh_done, 1)

                def xhi(t, u):
                    after(act, xt_done, t - 1)
                    act.activation(x2[u][:, 0, :], m.X[:, t, :], ACT.Copy).then_inc(xh_done, 1)

                run_tiles(act, NT, [(0, xhi)])
                act.wait_ge(step, 2)
                act.activation(e[:, :, :], shifted[:, :, :], ACT.Exp, scale=1.0 / WS).then_inc(exp_done, 1)

            @block.vector
            def _(dve):
                dve.wait_ge(gh_done, 1)
                dve.scalar_tensor_tensor(gT[:, 1, :, :], ps_g[:, :, :], WS, gT[:, 0, :, :], ALU.mult,
                                         ALU.subtract).then_inc(gl_done, 1)

                def xevac(t, u):
                    dve.wait_ge(xt_done, t + 1)
                    dve.tensor_copy(m.xT3[:, :, :, bass.ds(t * P, P)], ps_x[u][:, :, :, :]).then_inc(xt_evac, 1)

                def levac(t, u):
                    dve.wait_ge(l_done, t + 1)
                    dve.tensor_copy(logits[:, t, :], ps_l[u][:, :]).then_inc(l_evac, 1)

                run_tiles(dve, NT, [(0, xevac), (1, levac)])
                count = [0]

                def done(instruction):
                    instruction.then_inc(step, 1)
                    count[0] += 1
                    dve.wait_ge(step, count[0])

                def wide(x):
                    return x[:, :, None].to_broadcast([P, NT, NE])

                dve.wait_ge(l_evac, NT)
                done(dve.tensor_reduce(top[:, :], logits[:, :, :], AX.X, ALU.max))
                done(dve.tensor_tensor(shifted[:, :, :], logits[:, :, :], wide(top[:, :]), ALU.subtract))
                dve.wait_ge(exp_done, 1)
                done(dve.tensor_reduce(total[:, :], e[:, :, :], AX.X, ALU.add))
                done(dve.reciprocal(rec[:, :], total[:, :]))
                done(dve.tensor_tensor(probs[:, 0, :, :], e[:, :, :], wide(rec[:, :]), ALU.mult))
                descending = m.descending[:, None, :].to_broadcast([P, NT, NE])
                for c in range(2):
                    done(dve.tensor_reduce(m.score[:, c, :], probs[:, c, :, :], AX.X, ALU.max))
                    done(dve.tensor_tensor(ranked[:, c, :, :], probs[:, c, :, :], wide(m.score[:, c, :]), ALU.is_equal))
                    done(dve.tensor_tensor(shifted[:, :, :], ranked[:, c, :, :], descending, ALU.mult))
                    done(dve.tensor_reduce(code[:, c, :], shifted[:, :, :], AX.X, ALU.max))
                    done(dve.tensor_tensor(m.hot[:, c, :, :], descending, wide(code[:, c, :]), ALU.is_equal))
                    if c == 0:
                        done(dve.scalar_tensor_tensor(probs[:, 1, :, :], m.hot[:, 0, :, :], -2.0, probs[:, 0, :, :],
                                                      ALU.mult, ALU.add))

            @block.gpsimd
            def _(pool):
                def xlo(t, u):
                    pool.wait_ge(xh_done, t + 1)
                    after(pool, xt_done, t - 1)
                    pool.tensor_tensor(x2[u][:, 1, :], m.X[:, t, :], x2[u][:, 0, :], ALU.subtract).then_inc(xl_done, 1)

                run_tiles(pool, NT, [(0, xlo)])


FCH = [(0, P), (P, P), (2 * P, FE - 2 * P)]


def dense_experts(nc, m, experts):
    E = len(experts)
    with Phase(nc, "moe") as f:
        raw_g = f.sb("raw_g", [P, KC, 2, FE], F32)
        raw_d = f.sb("raw_d", [P, 3, D], F32)
        wg = [f.sb(f"wg{e}", [P, 2, KC, 2, FE], F16) for e in range(2)]
        wd = [f.sb(f"wd{e}", [P, 2, 3, D], F16) for e in range(2)]
        th = [f.sb(f"th{u}", [P, FE], F32) for u in range(2)]
        a_ = [f.sb(f"a{u}", [P, FE], F32) for u in range(2)]
        h = [f.sb(f"h{u}", [P, FE], F32) for u in range(2)]
        h2 = [f.sb(f"h2{u}", [P, 2, FE], F16) for u in range(2)]
        hT = [f.sb(f"hT{u}", [P, 2, 3, P], F16) for u in range(2)]
        ps_g = [[f.ps(f"ps_g{u}{n}", [P, FE], F32) for n in range(2)] for u in range(2)]
        ps_h = f.ps("ps_h", [P, 2, 3, P], F16)
        ps_y = [f.ps(f"ps_y{u}", [P, D], F32) for u in range(2)]
        w_in, wh_done, wl_done, g_done, th_done, a_done, h_done, hh_done, hl_done = f.sems(
            "w_in wh_done wl_done g_done th_done a_done h_done hh_done hl_done")
        ht_done, ht_evac, y_done, acc_done = f.sems("ht_done ht_evac y_done acc_done")
        LAST = slice(0, FCH[2][1])
        with f.block() as block:
            @block.sync
            def _(sp):
                for i, (gate, up, down, _) in enumerate(experts):
                    after(sp, wl_done, 3 * i)
                    for n, w in enumerate((gate, up)):
                        sp.dma_start(raw_g[:, :, n, :], w.rearrange("(k p) n -> p k n", p=P)).then_inc(w_in, 16)
                    sp.dma_start(raw_d[:, 0:2, :], down[0:2 * P, :].rearrange("(k p) n -> p k n", p=P)).then_inc(w_in, 16)
                    sp.dma_start(raw_d[LAST, 2, :], down[2 * P:FE, :]).then_inc(w_in, 16)

            @block.tensor
            def _(pe):
                for i in range(E):
                    T0, w = i * NT, i % 2

                    def gu(t, u):
                        after(pe, h_done, T0 + t - 1)
                        s = bass.ds(t * P, P)
                        for n in range(2):
                            last = products(pe, ps_g[u][n][:, :], lambda k: m.xT3[:, 0, k, s], lambda k: m.xT3[:, 1, k, s],
                                            lambda k: wg[w][:, 0, k, n, :], lambda k: wg[w][:, 1, k, n, :], KC)
                            last.then_inc(g_done, 1)

                    def tr(t, u):
                        pe.wait_ge(hl_done, T0 + t + 1)
                        after(pe, ht_evac, T0 + t)
                        for part in range(2):
                            for k, (at, size) in enumerate(FCH):
                                last = pe.transpose(ps_h[0:size, part, k, :], h2[u][:, part, at:at + size], m.ident16[:, :])
                        last.then_inc(ht_done, 1)

                    def down(t, u):
                        pe.wait_ge(ht_evac, T0 + t + 1)
                        after(pe, acc_done, T0 + t - 1)
                        for k, (_, size) in enumerate(FCH):
                            for n, (a, c) in enumerate(((0, 0), (0, 1), (1, 0))):
                                last = pe.matmul(ps_y[u][:, :], hT[u][0:size, a, k, :], wd[w][0:size, c, k, :],
                                                 start=(k == 0 and n == 0), stop=(k == 2 and n == 2))
                        last.then_inc(y_done, 1)

                    pe.wait_ge(wl_done, 3 * i + 3)
                    run_tiles(pe, NT, [(3, down), (2, tr), (0, gu)])

            def split(i, eng, part):
                w = i % 2
                if part == 0:
                    eng.wait_ge(w_in, 64 * (i + 1))
                    after(eng, y_done, NT * (i - 1))
                else:
                    eng.wait_ge(wh_done, 3 * i + 3)
                for out, raw in ((wg[w][:, part], raw_g[:, :, :, :]), (wd[w][:, part, 0:2, :], raw_d[:, 0:2, :]),
                                 (wd[w][LAST, part, 2, :], raw_d[LAST, 2, :])):
                    if part == 0:
                        eng.activation(out, raw, ACT.Copy, scale=WS).then_inc(wh_done, 1)
                    else:
                        hi = {0: wg[w][:, 0], 1: wd[w][:, 0, 0:2, :], 2: wd[w][LAST, 0, 2, :]}[split.n]
                        eng.scalar_tensor_tensor(out, raw, WS, hi, ALU.mult, ALU.subtract).then_inc(wl_done, 1)
                        split.n = (split.n + 1) % 3
            split.n = 0

            @block.scalar
            def _(act):
                split(0, act, 0)
                for i in range(E):
                    T0 = i * NT
                    if i + 1 < E:
                        split(i + 1, act, 0)

                    def tanh(t, u):
                        act.wait_ge(g_done, (T0 + t) * 2 + 1)
                        after(act, a_done, T0 + t - 1)
                        act.activation(th[u][:, :], ps_g[u][0][:, :], ACT.Tanh, scale=0.5 / WS).then_inc(th_done, 1)

                    def hhi(t, u):
                        act.wait_ge(h_done, T0 + t + 1)
                        after(act, ht_done, T0 + t - 1)
                        act.activation(h2[u][:, 0, :], h[u][:, :], ACT.Copy).then_inc(hh_done, 1)

                    def hevac(t, u):
                        act.wait_ge(ht_done, T0 + t + 1)
                        after(act, y_done, T0 + t - 1)
                        act.activation(hT[u][:, :, 0:2, :], ps_h[:, :, 0:2, :], ACT.Copy)
                        act.activation(hT[u][LAST, :, 2, :], ps_h[LAST, :, 2, :], ACT.Copy).then_inc(ht_evac, 1)

                    run_tiles(act, NT, [(1, hhi), (2, hevac), (0, tanh)])

            @block.vector
            def _(dve):
                split(0, dve, 1)
                for i in range(E):
                    T0 = i * NT
                    if i + 1 < E:
                        split(i + 1, dve, 1)

                    def swiglu(t, u):
                        dve.wait_ge(th_done, T0 + t + 1)
                        dve.scalar_tensor_tensor(a_[u][:, :], th[u][:, :], 1.0, ps_g[u][0][:, :], ALU.add, ALU.mult).then_inc(a_done, 1)
                        dve.wait_ge(a_done, T0 + t + 1)
                        dve.wait_ge(g_done, (T0 + t) * 2 + 2)
                        after(dve, hl_done, T0 + t - 1)
                        dve.scalar_tensor_tensor(h[u][:, :], a_[u][:, :], 0.5 / WS ** 2, ps_g[u][1][:, :], ALU.mult,
                                                 ALU.mult).then_inc(h_done, 1)

                    def accumulate(t, u):
                        dve.wait_ge(y_done, T0 + t + 1)
                        weight = experts[i][3]
                        dve.scalar_tensor_tensor(m.X[:, t, :], ps_y[u][:, :], 1.0 / WS if weight is None else weight(t),
                                                 m.X[:, t, :], ALU.mult, ALU.add).then_inc(acc_done, 1)

                    after(dve, acc_done, T0)
                    run_tiles(dve, NT, [(1, swiglu), (3, accumulate)])

            @block.gpsimd
            def _(pool):
                for i in range(E):
                    T0 = i * NT

                    def hlo(t, u):
                        pool.wait_ge(hh_done, T0 + t + 1)
                        after(pool, ht_done, T0 + t - 1)
                        pool.tensor_tensor(h2[u][:, 1, :], h[u][:, :], h2[u][:, 0, :], ALU.subtract).then_inc(hl_done, 1)

                    run_tiles(pool, NT, [(1, hlo)])


def final_norm(nc, m, out):
    with Phase(nc, "final") as f:
        ln = LayerNorm(f, m, "ln", 1e-5)
        out_done = f.sem("out_done")
        rows = out.rearrange("b (t p) n -> p (b t) n", p=P)
        with f.block() as block:
            @block.vector
            def _(dve):
                run_tiles(dve, NT, [(0, lambda t, u: ln.statistics(dve, m.X[:, t, :][:, None, :], t, u)),
                                    (1, lambda t, u: ln.normalize(dve, m.X[:, t, :], m.X[:, t, :], t, u))])

            @block.gpsimd
            def _(pool):
                run_tiles(pool, NT, [(0, lambda t, u: ln.root(pool, t, u))])

            @block.sync
            def _(sp):
                for c in range(4):
                    s = slice(c * NT // 4, (c + 1) * NT // 4)
                    sp.wait_ge(ln.s_used, (c + 1) * NT // 4)
                    sp.dma_start(rows[:, s, :], m.X[:, s, :]).then_inc(out_done, 16)
                sp.wait_ge(out_done, 64)


def experts(nc, m, d, out):
    with ExitStack() as ctx:
        def sb(name, shape, dt):
            return ctx.enter_context(nc.sbuf_tensor(name, shape, dt))

        m.xT3 = sb("xT3", [P, 2, KC, NT * P], F16)
        m.hot = sb("hot", [P, 2, NT, NE], F32)
        m.score = sb("score", [P, 2, NT], F32)
        m.comb = sb("comb", [P, NT, NE], F32)
        route(nc, m, d)
        shared_gu, shared_d = d["L1_ffn_shared_gate_up"], d["L1_ffn_shared_down"]
        dense = [(shared_gu[:, s * FE:(s + 1) * FE], shared_gu[:, SI + s * FE:SI + (s + 1) * FE],
                  shared_d[s * FE:(s + 1) * FE, :], None) for s in range(2)]
        combine(nc, m)
        for e in range(NE):
            dense.append((d["L1_ffn_w_gate_up"][e, :, 0:FE], d["L1_ffn_w_gate_up"][e, :, FE:2 * FE],
                          d["L1_ffn_w_down"][e, :, :], (lambda t, e=e: m.comb[:, t, e:e + 1])))
        dense_experts(nc, m, dense)
        final_norm(nc, m, out)


def combine(nc, m):
    with Phase(nc, "comb") as f:
        w = f.sb("w", [P, 2, NT, NE], F32)
        w_done, c_done = f.sems("w_done c_done")
        with f.block() as block:
            @block.vector
            def _(dve):
                for c in range(2):
                    dve.scalar_tensor_tensor(w[:, c, :, :], m.hot[:, c, :, :], 1.0 / WS,
                                             m.score[:, c, :][:, :, None].to_broadcast([P, NT, NE]),
                                             ALU.mult, ALU.mult).then_inc(w_done, 1)
                dve.wait_ge(w_done, 2)
                dve.tensor_tensor(m.comb[:, :, :], w[:, 0, :, :], w[:, 1, :, :], ALU.add).then_inc(c_done, 1)


class Memory:
    pass


CONST_COLS = 4 * P + 2 * TB * HD + 32 + NE


def build(nc, d, out):
    m = Memory()
    with ExitStack() as ctx:
        def sb(name, shape, dt):
            return ctx.enter_context(nc.sbuf_tensor(name, shape, dt))

        m.X = sb("X", [P, NT, D], F32)
        m.consts = sb("consts", [P, CONST_COLS], F32)
        m.ident = m.consts[:, 0:P]
        m.masks = m.consts[:, P:4 * P].rearrange("p (a k) -> p a k", a=3)
        m.rope = m.consts[:, 4 * P:4 * P + 2 * TB * HD].rearrange("p (a t d) -> p a t d", a=2, d=HD)
        m.select = m.consts[:, CONST_COLS - NE - 32:CONST_COLS - NE]
        m.descending = m.consts[:, CONST_COLS - NE:CONST_COLS]
        m.ones = sb("ones", [P, P], F32)
        m.ident16 = sb("ident16", [P, P], F16)
        m.identb = sb("identb", [P, P], BF16)
        m.masks16 = sb("masks16", [P, 3, P], BF16)
        m.minus_half = sb("minus_half", [P, 1], F32)
        m.gamma = sb("gamma", [P, 2], F32)
        with ExitStack() as layer0:
            def l0(name, shape, dt):
                return layer0.enter_context(nc.sbuf_tensor(name, shape, dt))

            m.wfcT = l0("wfcT", [P, KC, FF], F16)
            m.wprojT = l0("wprojT", [P, FF // P, D], F16)
            with ExitStack() as attn:
                def la(name, shape, dt):
                    return attn.enter_context(nc.sbuf_tensor(name, shape, dt))

                m.wqkv_h = la("wqkv_h", [P, KC, D + 2 * KV], F16)
                m.wqkv_l = la("wqkv_l", [P, KC, D + 2 * KV], F16)
                m.wo_h = la("wo_h", [P, KC, D], F16)
                m.wo_l = la("wo_l", [P, KC, D], F16)
                load_and_prepare(nc, m, d)
                with nc.sbuf_tensor("O", [P, TB, D], F32) as m.O:
                    with nc.sbuf_tensor("QT", [P, HQ // 2, N], F16) as QT, \
                            nc.sbuf_tensor("KTe", [P, HKV, N], F16) as KTe, \
                            nc.sbuf_tensor("KTo", [P, HKV, N], F16) as KTo, \
                            nc.sbuf_tensor("V", [P, TB, HKV, 32], F32) as V:
                        for b in range(B):
                            project_qkv(nc, m, b, QT, [KTe, KTo], V)
                            attend(nc, m, b, QT, [KTe, KTo], V)
                            attention_output(nc, m, b)
            ternary_ffn(nc, m)
        linear_attention(nc, m, d)
        experts(nc, m, d, out)


_INS = ['L0_attn_x', 'L0_attn_wq', 'L0_attn_wk', 'L0_attn_wv', 'L0_attn_wo', 'L0_ffn_w_fc', 'L0_ffn_w_proj',
        'L1_attn_Wqk', 'L1_attn_bqk', 'L1_attn_Wv', 'L1_attn_bv', 'L1_attn_Wu', 'L1_attn_bu', 'L1_attn_Wo',
        'L1_attn_bo', 'L1_attn_ln_g', 'L1_attn_ln_b', 'L1_ffn_gate_w', 'L1_ffn_w_gate_up', 'L1_ffn_w_down',
        'L1_ffn_shared_gate_up', 'L1_ffn_shared_down']


def _constants():
    c = np.zeros((P, CONST_COLS), np.float32)
    c[:, 0:P] = np.eye(P)
    rows, cols = np.arange(P)[:, None], np.arange(P)[None, :]
    c[:, P:2 * P] = np.where(cols > rows, -1e30, 0.0)
    c[:, 2 * P:3 * P] = np.where(rows > cols, -1e30, 0.0)
    c[:, 3 * P:4 * P] = c[:, 2 * P:3 * P]
    freq = np.float32(10000.0) ** (-(np.arange(HD // 2, dtype=np.float32) * np.float32(2.0 / HD)))
    phase = np.arange(N, dtype=np.float32)[:, None] * freq[None, :].astype(np.float32)
    cos, sin = np.cos(phase), np.sin(phase)
    table = np.stack([np.stack([cos, cos], -1), np.stack([-sin, sin], -1)]) / WS
    table = table.reshape(2, TB, P, HD).transpose(2, 0, 1, 3)
    c[:, 4 * P:CONST_COLS - 32 - NE] = table.reshape(P, -1)
    c[:, CONST_COLS - NE:] = NE - np.arange(NE)
    c[:, CONST_COLS - 32 - NE:CONST_COLS - NE] = np.tile(np.eye(32), (4, 1))
    return c


def kernel(**inputs):
    import numpy as _np
    import concourse.bacc as _bacc
    from concourse import mybir as _mybir
    from concourse.bass_utils import run_bass_kernel_spmd as _run

    nc = _bacc.Bacc("TRN2", target_bir_lowering=False, num_devices=1)
    arrays, d = {}, {}
    for name in _INS:
        a = _np.ascontiguousarray(inputs[name])
        arrays[f"in_{name}_dram"] = a
        d[name] = nc.dram_tensor(f"in_{name}_dram", a.shape, _mybir.dt.from_np(a.dtype), kind="ExternalInput").ap()
    a = _constants()
    arrays["in_consts_dram"] = a
    d["consts"] = nc.dram_tensor("in_consts_dram", a.shape, _mybir.dt.float32, kind="ExternalInput").ap()
    out = nc.dram_tensor("out_0_dram", (B, N, D), _mybir.dt.float32, kind="ExternalOutput").ap()
    build(nc, d, out)
    r = _run(nc, [arrays], core_ids=[0])
    return r.results[0]["out_0_dram"]
```

```python
from contextlib import ExitStack

import numpy as np

import concourse.bass as bass
from concourse import mybir

P = 128
D = 512
KC = D // P
B, N = 2, 1024
NT = B * N // P
TB = N // P
HQ, HKV, HD = 32, 8, 16
GQ = HQ // HKV
KV = HKV * HD
FF = 4 * D
HL = 16
DL = D // HL
NE, TOPK, FE = 16, 2, 352
GS = 2 * P
NG = B * N * TOPK // GS + NE - 1
SI = 2 * FE
WS = 64.0

LO_ROW = 32
KV_SCALE = 1.0 / 16

F32, F16, BF16 = mybir.dt.float32, mybir.dt.float16, mybir.dt.bfloat16
I32, U32 = mybir.dt.int32, mybir.dt.uint32
ALU = mybir.AluOpType
ACT = mybir.ActivationFunctionType
AX = mybir.AxisListType


def run_tiles(eng, n, stages):
    lag = max(l for l, _ in stages)

    def step(s, par):
        for l, fn in stages:
            if not isinstance(s, int) or 0 <= s - l < n:
                fn(s - l, (par - l) % 2)

    first = (lag + 3) // 2 * 2
    pairs = (n - first) // 2
    if pairs < 2:
        first, pairs = n + lag, 0
    for s in range(first):
        step(s, s % 2)
    if pairs:
        with eng.Fori(0, pairs) as i:
            for par in range(2):
                step(i * 2 + (first + par), par)
        for s in range(first + 2 * pairs, n + lag):
            step(s, s % 2)


def after(eng, sem, count):
    if not isinstance(count, int) or count > 0:
        eng.wait_ge(sem, count)


class Phase:

    def __init__(self, nc, name):
        self.nc, self.name = nc, name
        self.ctx, self.sem_ctx, self.held = ExitStack(), ExitStack(), []

    def __enter__(self):
        self.ctx.__enter__()
        self.sem_ctx.__enter__()
        return self

    def __exit__(self, *e):
        with self.nc.Block() as block:
            @block.gpsimd
            def _(pool):
                for s in self.held:
                    pool.sem_clear(s)
        self.sem_ctx.__exit__(*e)
        return self.ctx.__exit__(*e)

    def sb(self, name, shape, dt):
        return self.ctx.enter_context(self.nc.sbuf_tensor(f"{self.name}_{name}", shape, dt))

    def ps(self, name, shape, dt):
        return self.ctx.enter_context(self.nc.psum_tensor(f"{self.name}_{name}", shape, dt))

    def sem(self, name):
        self.held.append(self.sem_ctx.enter_context(self.nc.semaphore(f"{self.name}_{name}")))
        return self.held[-1]

    def sems(self, names):
        return [self.sem(n) for n in names.split()]

    def block(self):
        return self.nc.Block()


def products(pe, out, lhs_hi, lhs_lo, rhs_hi, rhs_lo, chunks):
    last = None
    for k in range(chunks):
        for n, (a, b) in enumerate(((lhs_hi, rhs_hi), (lhs_hi, rhs_lo), (lhs_lo, rhs_hi))):
            last = pe.matmul(out, a(k), b(k), start=(k == 0 and n == 0), stop=(k == chunks - 1 and n == 2))
    return last


def transpose_parts(pe, out, parts, m):
    for part in range(2):
        for k in range(out.shape[2]):
            last = pe.transpose(out[:, part, k, :], parts[:, part, k * P:(k + 1) * P], m.ident16[:, :])
    return last


def load_and_prepare(nc, m, d):
    NO = FF // P
    NP_ = D // P
    with Phase(nc, "prep") as f:
        w_fc = f.sb("w_fc", [P, NO, D], F32)
        w_proj = f.sb("w_proj", [P, NP_, FF], F32)
        t_fc = f.sb("t_fc", [P, NO, D], F16)
        t_proj = f.sb("t_proj", [P, NP_, FF], F16)
        w_qkv = f.sb("w_qkv", [P, KC, D + 2 * KV], F32)
        w_o = f.sb("w_o", [P, KC, D], F32)
        part = f.sb("part", [P, 8], F32)
        total = f.sb("total", [P, 2], F32)
        thr = f.sb("thr", [P, 2, 2], F32)
        ps_sum = f.ps("ps_sum", [P, 8], F32)
        ps_t = [f.ps(f"ps_t{i}", [P, 1024], F16) for i in range(4)]
        consts_in, x_in, wa_in = f.sems("consts_in x_in wa_in")
        fc_in = [f.sem(f"fc_in{c}") for c in range(4)]
        proj_in = [f.sem(f"proj_in{c}") for c in range(4)]
        ident_done, hi_done, lo_done, abs_done, sum_done, tot_done, thr_done = f.sems(
            "ident_done hi_done lo_done abs_done sum_done tot_done thr_done")
        neg_done, tern_done, tr_done, evac_done = f.sems("neg_done tern_done tr_done evac_done")
        fc_rows = d["L0_ffn_w_fc"].rearrange("(n p) k -> p n k", p=P)
        proj_rows = d["L0_ffn_w_proj"].rearrange("(n p) k -> p n k", p=P)
        C4 = NO // 4

        def chunk(c):
            if c < 4:
                s = slice(c * C4, (c + 1) * C4)
                return w_fc[:, s, :], t_fc[:, s, :], fc_in[c]
            return w_proj[:, c - 4, :], t_proj[:, c - 4, :], proj_in[c - 4]

        with f.block() as block:
            @block.sync
            def _(sp):
                sp.dma_start(m.consts[:, :], d["consts"][:, 0:TABLES + 32]).then_inc(consts_in, 16)
                for c in range(4):
                    sp.dma_start(w_fc[:, c * C4:(c + 1) * C4, :], fc_rows[:, c * C4:(c + 1) * C4, :]).then_inc(fc_in[c], 16)
                for c in range(4):
                    sp.dma_start(w_proj[:, c, :], proj_rows[:, c, :]).then_inc(proj_in[c], 16)

            @block.gpsimd
            def _(pool):
                pool.memset(m.ones[:, :], 1.0).then_inc(ident_done, 1)
                pool.memset(m.minus_half[:, :], -0.5)

            @block.scalar
            def _(act):
                for n, (w, at, size) in enumerate((("wq", 0, D), ("wk", D, KV), ("wv", D + KV, KV))):
                    act.dma_start(w_qkv[:, :, at:at + size],
                                  d[f"L0_attn_{w}"].rearrange("(k p) n -> p k n", p=P)).then_inc(wa_in, 16)
                act.dma_start(w_o[:, :, :], d["L0_attn_wo"].rearrange("(k p) n -> p k n", p=P)).then_inc(wa_in, 16)
                act.dma_start(m.X[:, :, :], d["L0_attn_x"].rearrange("b (t p) n -> p (b t) n", p=P)).then_inc(x_in, 16)
                act.wait_ge(consts_in, 16)
                act.activation(m.ident16[:, :], m.ident, ACT.Copy).then_inc(ident_done, 1)
                act.activation(m.masks16[:, :, :], m.masks, ACT.Copy).then_inc(ident_done, 1)
                act.activation(m.identb[:, :], m.ident, ACT.Copy).then_inc(ident_done, 1)
                act.wait_ge(wa_in, 64)
                act.activation(m.wqkv_h[:, :, :], w_qkv[:, :, :], ACT.Copy, scale=WS).then_inc(hi_done, 1)
                act.activation(m.wo_h[:, :, :], w_o[:, :, :], ACT.Copy, scale=WS).then_inc(hi_done, 1)
                for c in range(8):
                    src, junk, arrived = chunk(c)
                    act.wait_ge(arrived, 16)
                    act.activation(junk, src, ACT.Abs, accum_out=part[:, c:c + 1]).then_inc(abs_done, 1)
                for g in range(16):
                    act.wait_ge(tr_done, g + 1)
                    dst = m.wfcT[:, g // 2, (g % 2) * 1024:(g % 2 + 1) * 1024] if g < 8 else \
                        m.wprojT[:, 2 * (g - 8):2 * (g - 8) + 2, :].rearrange("p a n -> p (a n)")
                    act.activation(dst, ps_t[g % 4][:, :], ACT.Copy).then_inc(evac_done, 1)
                act.wait_ge(x_in, 16)

            @block.tensor
            def _(pe):
                pe.wait_ge(ident_done, 4)
                pe.wait_ge(abs_done, 8)
                pe.matmul(ps_sum[:, :], m.ones[:, :], part[:, :], start=True, stop=True).then_inc(sum_done, 1)
                for g in range(16):
                    after(pe, evac_done, g - 3)
                    if g < 8:
                        pe.wait_ge(tern_done, 4 if g % 2 else 2)
                    else:
                        pe.wait_ge(tern_done, 8)
                    for r in range(8):
                        if g < 8:
                            src = t_fc[:, (g % 2) * 8 + r, (g // 2) * P:(g // 2 + 1) * P]
                        else:
                            ic = 2 * (g - 8) + r // 4
                            src = t_proj[:, r % 4, ic * P:(ic + 1) * P]
                        last = pe.transpose(ps_t[g % 4][:, r * P:(r + 1) * P], src, m.ident16[:, :])
                    last.then_inc(tr_done, 1)

            @block.vector
            def _(dve):
                dve.wait_ge(hi_done, 1)
                dve.scalar_tensor_tensor(m.wqkv_l[:, :, :], w_qkv[:, :, :], WS, m.wqkv_h[:, :, :],
                                         ALU.mult, ALU.subtract).then_inc(lo_done, 1)
                dve.wait_ge(hi_done, 2)
                dve.scalar_tensor_tensor(m.wo_l[:, :, :], w_o[:, :, :], WS, m.wo_h[:, :, :],
                                         ALU.mult, ALU.subtract).then_inc(lo_done, 1)
                dve.wait_ge(sum_done, 1)
                dve.tensor_reduce(total[:, :], ps_sum[:, :].rearrange("p (w c) -> p w c", w=2), AX.X,
                                  ALU.add).then_inc(tot_done, 1)
                dve.wait_ge(tot_done, 1)
                dve.tensor_scalar(m.gamma[:, :], total[:, :], 1.0 / (D * FF), None, ALU.mult).then_inc(thr_done, 1)
                dve.tensor_scalar(thr[:, 0, :], total[:, :], 0.5 / (D * FF), 0.5e-6, ALU.mult,
                                  ALU.add).then_inc(thr_done, 1)
                dve.tensor_scalar(thr[:, 1, :], total[:, :], -0.5 / (D * FF), -0.5e-6, ALU.mult,
                                  ALU.add).then_inc(thr_done, 1)
                dve.wait_ge(thr_done, 3)
                for c in range(8):
                    src, dst, _ = chunk(c)
                    w = c // 4
                    dve.tensor_scalar(dst, src, thr[:, 1, w:w + 1], None, ALU.is_lt).then_inc(neg_done, 1)
                    dve.wait_ge(neg_done, c + 1)
                    dve.scalar_tensor_tensor(dst, src, thr[:, 0, w:w + 1], dst, ALU.is_gt,
                                             ALU.subtract).then_inc(tern_done, 1)


def project_qkv(nc, m, b, QT, KT, V):
    HB = HQ + 2 * HKV
    with Phase(nc, f"qkv{b}") as f:
        x2 = [f.sb(f"x2{u}", [P, 2, D], F16) for u in range(2)]
        xT = [f.sb(f"xT{u}", [P, 2, KC, P], F16) for u in range(2)]
        t1 = [f.sb(f"t1{u}", [P, HQ + HKV, HD], F32) for u in range(2)]
        t2 = [f.sb(f"t2{u}", [P, HQ + HKV, HD], F32) for u in range(2)]
        rot = t1
        stack = [f.sb(f"stack{u}", [P, HB, 64], F16) for u in range(2)]
        pad = f.sb("pad", [P, 1], F32)
        ps_xt = [f.ps(f"ps_xt{u}", [P, 2, KC, P], F16) for u in range(2)]
        ps_qkv = f.ps("ps_qkv", [P, 1024], F32)
        ps_v = f.ps("ps_v", [P, 512], F32)
        ps_q = [f.ps(f"ps_q{u}", [P, 8, P], F16) for u in range(2)]
        ps_k = f.ps("ps_k", [P, 8, P], F16)
        xh_done, xl_done, xt_done, xt_evac, proj_done, v_done = f.sems(
            "xh_done xl_done xt_done xt_evac proj_done v_done")
        rope_done, rot_done, qhi_done, qlo_done, khi_done, kst_done = f.sems(
            "rope_done rot_done qhi_done qlo_done khi_done kst_done")
        tr_done, qevac, kevac, init_done, halves, kt_zero = f.sems("tr_done qevac kevac init_done halves kt_zero")

        with f.block() as block:
            @block.tensor
            def _(pe):
                def xt(t, u):
                    pe.wait_ge(xl_done, t + 1)
                    after(pe, xt_evac, t - 1)
                    transpose_parts(pe, ps_xt[u], x2[u], m).then_inc(xt_done, 1)

                def proj(t, u):
                    pe.wait_ge(xt_evac, t + 1)
                    after(pe, rope_done, t)
                    after(pe, v_done, t)
                    for at, size, out in ((0, D, ps_qkv[:, 0:D]), (D, KV, ps_qkv[:, D:D + KV]), (D + KV, KV, ps_v[:, 0:KV])):
                        last = products(pe, out, lambda k: xT[u][:, 0, k, :],
                                        lambda k: xT[u][:, 1, k, :], lambda k: m.wqkv_h[:, k, at:at + size],
                                        lambda k: m.wqkv_l[:, k, at:at + size], KC)
                    last.then_inc(proj_done, 1)

                def tr(t, u):
                    pe.wait_ge(qhi_done, t + 1)
                    pe.wait_ge(qlo_done, t + 1)
                    pe.wait_ge(kst_done, t + 1)
                    after(pe, qevac, t)
                    after(pe, kevac, t)
                    for g, out in enumerate((ps_q[0], ps_q[1], ps_k)):
                        for r in range(8):
                            at = 2 * (8 * g + r)
                            last = pe.transpose(out[:, r, :], stack[u][:, at:at + 2, :], m.ident16[:, :])
                    last.then_inc(tr_done, 1)

                run_tiles(pe, TB, [(1, xt), (2, proj), (3, tr)])

            @block.scalar
            def _(act):
                def xhi(t, u):
                    after(act, xt_done, t - 1)
                    act.activation(x2[u][:, 0, :], m.X[:, t + b * TB, :], ACT.Copy).then_inc(xh_done, 1)

                def vals(t, u):
                    act.wait_ge(proj_done, t + 1)
                    act.activation(V[:, t, :, 0:HD], ps_v[:, 0:KV].rearrange(
                        "p (h d) -> p h d", d=HD), ACT.Copy, scale=1.0 / WS).then_inc(v_done, 1)

                def qhi(t, u):
                    act.wait_ge(rot_done, t + 1)
                    after(act, tr_done, t - 1)
                    for at in (0, 2 * HD):
                        last = act.activation(stack[u][:, 0:HQ, at:at + HD], rot[u][:, 0:HQ, :], ACT.Copy)
                    last.then_inc(qhi_done, 1)

                def evac(t, u):
                    act.wait_ge(tr_done, t + 1)
                    for g in range(2):
                        last = act.activation(QT[:, 8 * g:8 * g + 8, bass.ds(t * P, P)], ps_q[g][:, :, :], ACT.Copy)
                    last.then_inc(qevac, 1)

                act.wait_ge(init_done, 3)
                run_tiles(act, TB, [(0, xhi), (2, vals), (2, qhi), (3, evac)])

            @block.vector
            def _(dve):
                for u in range(2):
                    dve.memset(stack[u][:, :, 3 * HD:64], 0.0).then_inc(halves, 1)
                dve.wait_ge(halves, 2)
                for u in range(2):
                    dve.memset(stack[u][:, HQ:HB, 3 * HD:3 * HD + 1], 1.0).then_inc(init_done, 1)
                dve.memset(V[:, :, :, HD + 1:32], 0.0)
                dve.memset(V[:, :, :, HD:HD + 1], 1.0).then_inc(init_done, 1)

                def xevac(t, u):
                    dve.wait_ge(xt_done, t + 1)
                    after(dve, proj_done, t - 1)
                    dve.tensor_copy(xT[u][:, :, :, :], ps_xt[u][:, :, :, :]).then_inc(xt_evac, 1)

                def rope(t, u):
                    dve.wait_ge(proj_done, t + 1)
                    after(dve, qhi_done, t - 1)
                    after(dve, kst_done, t - 1)
                    H = HQ + HKV
                    qk = ps_qkv[:, 0:D + KV].rearrange("p (h d) -> p h d", d=HD)
                    cos = m.rope[:, 0, t, :][:, None, :].to_broadcast([P, H, HD])
                    dve.tensor_tensor(t1[u][:, :, :], qk, cos, ALU.mult)
                    pairs = qk.rearrange("p h (i e) -> p h i e", e=2)
                    outs = t2[u][:, :, :].rearrange("p h (i e) -> p h i e", e=2)
                    sins = m.rope[:, 1, t, :].rearrange("p (i e) -> p i e", e=2)
                    for e in range(2):
                        last = dve.tensor_tensor(outs[:, :, :, e], pairs[:, :, :, 1 - e],
                                                 sins[:, :, e][:, None, :].to_broadcast([P, H, HD // 2]), ALU.mult)
                    last.then_inc(rope_done, 1)

                def qlo(t, u):
                    dve.wait_ge(qhi_done, t + 1)
                    dve.tensor_tensor(stack[u][:, 0:HQ, HD:2 * HD], rot[u][:, 0:HQ, :], stack[u][:, 0:HQ, 0:HD],
                                      ALU.subtract).then_inc(qlo_done, 1)

                def evac(t, u):
                    dve.wait_ge(tr_done, t + 1)
                    for half in range(2):
                        r = slice(64 * half, 64 * half + 64)
                        last = dve.tensor_copy(KT[half][r, :, bass.ds(t * P, P)], ps_k[r, :, :])
                    last.then_inc(kevac, 1)

                if b == 0:
                    dve.wait_ge(kt_zero, 2)
                run_tiles(dve, TB, [(1, xevac), (2, rope), (2, qlo), (3, evac)])

            @block.gpsimd
            def _(pool):
                if b == 0:
                    for half in range(2):
                        pool.memset(KT[half][:, :, :], 0.0).then_inc(kt_zero, 1)
                pool.wait_ge(init_done, 3)

                def xlo(t, u):
                    pool.wait_ge(xh_done, t + 1)
                    after(pool, xt_done, t - 1)
                    pool.tensor_tensor(x2[u][:, 1, :], m.X[:, t + b * TB, :], x2[u][:, 0, :],
                                       ALU.subtract).then_inc(xl_done, 1)

                def rotate(t, u):
                    after(pool, tr_done, t - 1)
                    pool.wait_ge(rope_done, t + 1)
                    pool.tensor_tensor(rot[u][:, :, :], t1[u][:, :, :], t2[u][:, :, :], ALU.add).then_inc(rot_done, 1)

                def keys(t, u):
                    pool.wait_ge(rot_done, t + 1)
                    pool.tensor_tensor(pad[:, :], m.minus_half[:, :], m.minus_half[:, :], ALU.add)
                    k = rot[u][:, HQ:HQ + HKV, :]
                    blocks = stack[u][:, HQ:HB, :].rearrange("p (j c) d -> p j c d", c=2)
                    for c in range(2):
                        for at in (0, HD):
                            last = pool.tensor_copy(blocks[:, :, c, at:at + HD], k)
                    last.then_inc(khi_done, 1)
                    pool.wait_ge(khi_done, t + 1)
                    for c in range(2):
                        last = pool.tensor_tensor(blocks[:, :, c, 2 * HD:3 * HD], k, blocks[:, :, c, 0:HD], ALU.subtract)
                    last.then_inc(kst_done, 1)

                run_tiles(pool, TB, [(0, xlo), (2, rotate), (2, keys)])


def score_items():
    items = []
    for qt in range(TB):
        for c in range(1 + qt // 4):
            n = min(4, qt + 1 - 4 * c) * P
            per = 512 // n if n <= 256 else 1
            for h in range(0, GQ, per):
                items.append((qt, c, list(range(h, h + per)), n))
    return items


def attend(nc, m, b, QT, KT, V):
    S = score_items()
    T = [(qt, kt) for qt in range(TB) for kt in range(qt + 1)]
    PAIRS = len(T) // 2
    QUADS = PAIRS // 2
    assert len(T) % 4 == 0
    SPREAD = PAIRS - 4
    VC = HD + 1
    ORDER = ((), (1,), (0, 2))

    def events():
        out, ring = [], 0
        sums, later = [], []
        for j in range(-1, HKV):
            n = 0
            for p in range(PAIRS):
                g = j * PAIRS + p
                upto = len(S) * (p + 1) // SPREAD if p < SPREAD else len(S)
                turns = []
                while j + 1 < HKV and n < upto:
                    turns.append(("s", j + 1, n))
                    n += 1
                if j + 1 < HKV and p == SPREAD:
                    turns.append(("m", j + 1))
                turns += [("c", jj, qt) for jj, qt in sums]
                sums, later = later, []
                others = [("t", g, j, p)] if j >= 0 else []
                if j >= 0 and g % 2 and g >= 3:
                    others.append(("v", (g - 3) // 2))
                    later = ended((g - 3) // 2)
                at = ORDER[len(others)]
                for i in range(len(turns) + 1):
                    while others and at[-len(others)] <= i or others and i == len(turns):
                        out.append(others.pop(0))
                    if i < len(turns):
                        out.append((turns[i][0], ring, *turns[i][1:]))
                        ring += 1
        for q in (HKV * QUADS - 1,):
            out.append(("v", q))
            later += ended(q)
        for jj, qt in sums + later:
            out.append(("c", ring, jj, qt))
            ring += 1
        return out

    def banks(q):
        j, at = q // QUADS, 4 * (q % QUADS)
        return [(2 * q + i // 2, i % 2, j, *T[at + i]) for i in range(4)]

    def ended(q):
        return [(j, qt) for _, _, j, qt, kt in banks(q) if kt == qt]

    EVENTS = events()
    summed = {e[2] * TB + e[3]: e[1] + 1 for e in EVENTS if e[0] == "c"}
    maxima = {e[2]: e[1] + 1 for e in EVENTS if e[0] == "m"}
    with Phase(nc, f"attn{b}") as f:
        prob = [f.sb(f"prob{u}", [P, 1024], F32) for u in range(4)]
        oT = [f.sb(f"oT{u}", [P, GQ, P], F32) for u in range(2)]
        mx = f.sb("mx", [P, 2, GQ, TB], F32)
        mm = f.sb("mm", [P, GQ, TB], F32)
        negm = f.sb("negm", [P, GQ, TB], F16)
        mT = f.sb("mT", [GQ * TB, P], F16)
        rec = [f.sb(f"rec{u}", [P, GQ], F32) for u in range(2)]
        ps_s = [f.ps(f"ps_s{u}", [P, 512], F32) for u in range(2)]
        ps_t = [f.ps(f"ps_t{u}", [P, 1024], F32) for u in range(2)]
        ps_o = [f.ps(f"ps_o{u}", [P, GQ, P], F32) for u in range(2)]
        ring_done, ring_free, mx_init, mm_done, negm_done, mt_in = f.sems(
            "ring_done ring_free mx_init mm_done negm_done mt_in")
        t_done, exp_done, v_done, o_evac, rec_done = f.sems("t_done exp_done v_done o_evac rec_done")

        with f.block() as block:
            @block.tensor
            def _(pe):
                for kind, *a in EVENTS:
                    if kind in "smc":
                        after(pe, ring_free, a[0] - 1)
                        bank = ps_s[a[0] % 2]
                    if kind == "s":
                        _, j, n = a
                        qt, c, heads, cols = S[n]
                        diagonal = c == qt // 4
                        for at, h in enumerate(heads):
                            out = bank[:, at * cols:(at + 1) * cols]
                            last = pe.matmul(out, QT[:, j * 2 + h // 2, qt * P:(qt + 1) * P],
                                             KT[h % 2][:, j, c * 512:c * 512 + cols], start=True, stop=not diagonal)
                            if diagonal:
                                last = pe.matmul(out[:, cols - P:cols], m.identb[:, :], m.masks16[:, 0, :],
                                                 start=False, stop=True)
                        last.then_inc(ring_done, 1)
                    if kind == "m":
                        pe.wait_ge(negm_done, a[1] + 1)
                        pe.transpose(bank[0:GQ * TB, 0:P // 2].bitcast(F16), negm[:, :, :],
                                     m.ident16[:, :]).then_inc(ring_done, 1)
                    if kind == "t":
                        g, j, p = a
                        if p == 0:
                            pe.wait_ge(mt_in, j * 32 + 32)
                        after(pe, exp_done, g - 1)
                        for i, (qt, kt) in enumerate(T[2 * p:2 * p + 2]):
                            for par in range(2):
                                out = ps_t[g % 2][:, i * 512 + par * 256:i * 512 + par * 256 + 256]
                                last = pe.matmul(out, KT[par][:, j, kt * P:(kt + 1) * P],
                                                 QT[:, 2 * j:2 * j + 2, qt * P:(qt + 1) * P],
                                                 start=True, stop=kt != qt)
                                if kt == qt:
                                    last = pe.matmul(out, m.identb[:, :], m.masks16[:, 1:3, :], start=False, stop=True)
                        last.then_inc(t_done, 1)
                    if kind == "v":
                        q, = a
                        pe.wait_ge(exp_done, 2 * q + 2)
                        for pair, half, j, qt, kt in banks(q):
                            if kt == 0:
                                after(pe, o_evac, j * TB + qt - 1)
                            c = kt % 4
                            pe.matmul(ps_o[(j * TB + qt) % 2][32 * c:32 * c + 32, :, :], V[:, kt, j, :],
                                      prob[pair % 4][:, half * 512:half * 512 + 512],
                                      start=kt < 4, stop=kt + 4 > qt, skip_group_check=True).then_inc(v_done, 1)
                    if kind == "c":
                        _, j, qt = a
                        o = j * TB + qt
                        rows = 32 * min(qt + 1, 4)
                        pe.wait_ge(o_evac, o + 1)
                        for slot in range(GQ):
                            last = pe.matmul(bank[:, slot * VC:(slot + 1) * VC], oT[o % 2][0:rows, slot, :],
                                             m.select[0:rows, 0:VC], start=True, stop=True)
                        last.then_inc(ring_done, 1)

            @block.scalar
            def _(act):
                for kind, *a in EVENTS:
                    if kind == "t":
                        g = a[0]
                        act.wait_ge(t_done, g + 1)
                        after(act, v_done, 2 * (g - 4) + 2)
                        act.activation(prob[g % 4][:, :], ps_t[g % 2][:, :], ACT.Exp,
                                       scale=HD ** -0.5).then_inc(exp_done, 1)
                    if kind == "v":
                        for i, (_, _, j, qt, kt) in enumerate(banks(a[0])):
                            if kt < qt:
                                continue
                            o = j * TB + qt
                            rows = 32 * min(qt + 1, 4)
                            act.wait_ge(v_done, 4 * a[0] + i + 1)
                            after(act, ring_done, summed.get(o - 2, 0))
                            act.activation(oT[o % 2][0:rows, :, :], ps_o[o % 2][0:rows, :, :],
                                           ACT.Copy).then_inc(o_evac, 1)

            @block.vector
            def _(dve):
                dve.memset(mx[:, 1, :, :], -3.0e38).then_inc(mx_init, 1)
                dve.wait_ge(mx_init, 1)
                for kind, *a in EVENTS:
                    if kind in "smc":
                        dve.wait_ge(ring_done, a[0] + 1)
                        bank = ps_s[a[0] % 2]
                    if kind == "s":
                        _, j, n = a
                        qt, c, heads, cols = S[n]
                        h = heads[0]
                        dve.tensor_reduce(mx[:, c, h:h + len(heads), qt],
                                          bank[:, 0:len(heads) * cols].rearrange("p (h k) -> p h k", k=cols),
                                          AX.X, ALU.max).then_inc(ring_free, 1)
                        if n == len(S) - 1:
                            dve.wait_ge(ring_free, a[0] + 1)
                            dve.tensor_tensor(mm[:, :, :], mx[:, 0, :, :], mx[:, 1, :, :], ALU.max).then_inc(mm_done, 1)
                            dve.wait_ge(mm_done, j + 1)
                            dve.tensor_scalar(negm[:, :, :].rearrange("p (e a) q -> p a e q", e=2),
                                              mm[:, :, :].rearrange("p (a e) q -> p a e q", e=2), -1.0, None,
                                              ALU.mult).then_inc(negm_done, 1)
                    if kind == "m":
                        after(dve, mt_in, a[1] * 32)
                        dve.tensor_copy(mT[:, :], bank[0:GQ * TB, 0:P // 2].bitcast(F16)).then_inc(ring_free, 1)
                    if kind == "c":
                        _, j, qt = a
                        u = qt % 2
                        o = bank[:, 0:GQ * VC].rearrange("p (s v) -> p s v", v=VC)
                        dve.reciprocal(rec[u][:, :], o[:, :, HD]).then_inc(rec_done, 1)
                        dve.wait_ge(rec_done, j * TB + qt + 1)
                        out = m.O[:, qt, j * GQ * HD:(j + 1) * GQ * HD]
                        dve.tensor_tensor(out.rearrange("p (a e v) -> p e a v", a=2, e=2),
                                          o[:, :, 0:HD].rearrange("p (e a) v -> p e a v", e=2),
                                          rec[u][:, :].rearrange("p (e a) -> p e a", e=2)[:, :, :, None]
                                          .to_broadcast([P, 2, 2, HD]), ALU.mult).then_inc(ring_free, 1)

            @block.sync
            def _(sp):
                R = 2 * TB
                for j in range(HKV):
                    sp.wait_ge(ring_free, maxima[j])
                    for par in range(2):
                        row = 64 * par + 3 * HD
                        sp.dma_start(QT[row:row + 1, 2 * j:2 * j + 2, :], mT[par * R:(par + 1) * R, :]).then_inc(mt_in, 16)


class LayerNorm:

    def __init__(self, f, m, name, eps, n=1):
        self.n, self.m, self.eps = n, m, eps
        self.stats = [f.sb(f"{name}_stats{u}", [P, n, 6], F32) for u in range(2)]
        self.pad = f.sb(f"{name}_pad", [P, 1], F32)
        self.mv = [f.sb(f"{name}_mv{u}", [P, 2], F32) for u in range(2)]
        self.var = [f.sb(f"{name}_var{u}", [P, 1], F32) for u in range(2)]
        self.rstd = [f.sb(f"{name}_rstd{u}", [P, 1], F32) for u in range(2)]
        self.s_stats, self.s_mv, self.s_var, self.s_rstd, self.s_used = f.sems(
            f"{name}_stats {name}_mv {name}_var {name}_rstd {name}_used")

    def statistics(self, dve, x, t, u):
        for c in range(self.n):
            last = dve.bn_stats(self.stats[u][:, c, :], x[:, c, :])
        last.then_inc(self.s_stats, 1)
        dve.wait_ge(self.s_stats, t + 1)
        dve.memset(self.pad[:, :], 0.0)
        dve.bn_aggr(self.mv[u][:, :], self.stats[u][:, :, :]).then_inc(self.s_mv, 1)
        dve.wait_ge(self.s_mv, t + 1)
        dve.tensor_scalar(self.var[u][:, :], self.mv[u][:, 1:2], self.eps, None, ALU.add).then_inc(self.s_var, 1)

    def root(self, pool, t, u):
        pool.wait_ge(self.s_var, t + 1)
        after(pool, self.s_used, t - 1)
        pool.tensor_tensor(self.rstd[u][:, :], self.var[u][:, :], self.m.minus_half[:, :],
                           ALU.pow).then_inc(self.s_rstd, 1)

    def normalize(self, dve, out, x, t, u):
        dve.wait_ge(self.s_rstd, t + 1)
        dve.tensor_scalar(out, x, self.mv[u][:, 0:1], self.rstd[u][:, :], ALU.subtract, ALU.mult).then_inc(self.s_used, 1)


def attention_output(nc, m, b):
    with Phase(nc, f"wo{b}") as f:
        o2 = [f.sb(f"o2{u}", [P, 2, D], F16) for u in range(2)]
        oT = [f.sb(f"oT{u}", [P, 2, KC, P], F16) for u in range(2)]
        r = [f.sb(f"r{u}", [P, D], F32) for u in range(2)]
        ps_ot = [f.ps(f"ps_ot{u}", [P, 2, KC, P], F16) for u in range(2)]
        ps_y = [f.ps(f"ps_y{u}", [P, D], F32) for u in range(2)]
        oh_done, ol_done, ot_done, ot_evac, y_done, r_done = f.sems("oh_done ol_done ot_done ot_evac y_done r_done")
        ln = LayerNorm(f, m, "ln", 1e-5)
        with f.block() as block:
            @block.tensor
            def _(pe):
                def ot(t, u):
                    pe.wait_ge(ol_done, t + 1)
                    after(pe, ot_evac, t - 1)
                    transpose_parts(pe, ps_ot[u], o2[u], m).then_inc(ot_done, 1)

                def wo(t, u):
                    pe.wait_ge(ot_evac, t + 1)
                    after(pe, r_done, t - 1)
                    products(pe, ps_y[u][:, :], lambda k: oT[u][:, 0, k, :], lambda k: oT[u][:, 1, k, :],
                             lambda k: m.wo_h[:, k, :], lambda k: m.wo_l[:, k, :], KC).then_inc(y_done, 1)

                run_tiles(pe, TB, [(1, ot), (2, wo)])

            @block.scalar
            def _(act):
                def hi(t, u):
                    after(act, ot_done, t - 1)
                    act.activation(o2[u][:, 0, :], m.O[:, t, :], ACT.Copy).then_inc(oh_done, 1)

                run_tiles(act, TB, [(0, hi)])

            @block.vector
            def _(dve):
                def oevac(t, u):
                    dve.wait_ge(ot_done, t + 1)
                    after(dve, y_done, t - 1)
                    dve.tensor_copy(oT[u][:, :, :, :], ps_ot[u][:, :, :, :]).then_inc(ot_evac, 1)

                def residual(t, u):
                    dve.wait_ge(y_done, t + 1)
                    dve.scalar_tensor_tensor(r[u][:, :], ps_y[u][:, :], 1.0 / WS, m.X[:, t + b * TB, :],
                                             ALU.mult, ALU.add).then_inc(r_done, 1)
                    dve.wait_ge(r_done, t + 1)
                    ln.statistics(dve, r[u][:, None, :], t, u)

                def norm(t, u):
                    ln.normalize(dve, m.X[:, t + b * TB, :], r[u][:, :], t, u)

                run_tiles(dve, TB, [(1, oevac), (3, norm), (2, residual)])

            @block.gpsimd
            def _(pool):
                def lo(t, u):
                    pool.wait_ge(oh_done, t + 1)
                    after(pool, ot_done, t - 1)
                    pool.tensor_tensor(o2[u][:, 1, :], m.O[:, t, :], o2[u][:, 0, :], ALU.subtract).then_inc(ol_done, 1)

                run_tiles(pool, TB, [(0, lo), (2, lambda t, u: ln.root(pool, t, u))])


class AbsmaxQuantizer:
    LIMIT = (128.0 - 1e-6) / 128.0

    def __init__(self, f, name):
        self.g = [f.sb(f"{name}_g{u}", [P, 1], F32) for u in range(2)]
        self.limit = [f.sb(f"{name}_limit{u}", [P, 2], F32) for u in range(2)]
        self.s_max, self.s_limit, self.s_clipped = f.sems(f"{name}_max {name}_limit {name}_clipped")

    def apply(self, dve, x, t, u):
        dve.tensor_reduce(self.g[u][:, :], x, AX.X, ALU.max, apply_absolute_value=True).then_inc(self.s_max, 1)
        dve.wait_ge(self.s_max, t + 1)
        for n, sign in enumerate((1.0, -1.0)):
            dve.tensor_scalar(self.limit[u][:, n:n + 1], self.g[u][:, :], sign * self.LIMIT, None,
                              ALU.mult).then_inc(self.s_limit, 1)
        dve.wait_ge(self.s_limit, t * 2 + 2)
        dve.tensor_scalar(x, x, self.limit[u][:, 0:1], self.limit[u][:, 1:2], ALU.min,
                          ALU.max).then_inc(self.s_clipped, 1)


def ternary_ffn(nc, m):
    NB = FF // D
    NK = FF // P
    with Phase(nc, "ffn") as f:
        xn = [f.sb(f"xn{u}", [P, D], F32) for u in range(2)]
        x2 = [f.sb(f"x2{u}", [P, 2, D], F16) for u in range(2)]
        xT = [f.sb(f"xT{u}", [P, 2, KC, P], F16) for u in range(2)]
        h = [f.sb(f"h{u}", [P, NB, D], F32) for u in range(2)]
        hn = [f.sb(f"hn{u}", [P, FF], F32) for u in range(2)]
        h2 = [f.sb(f"h2{u}", [P, 2, FF], F16) for u in range(2)]
        hT = [f.sb(f"hT{u}", [P, 2, NK, P], F16) for u in range(2)]
        r = [f.sb(f"r{u}", [P, D], F32) for u in range(2)]
        ps_x = f.ps("ps_x", [P, 2, KC, P], F16)
        ps_fc = [f.ps(f"ps_fc{n}", [P, D], F32) for n in range(NB)]
        ps_h = [f.ps(f"ps_h{n}", [P, 8, P], F16) for n in range(2)]
        ps_y = f.ps("ps_y", [P, D], F32)
        ln_x = LayerNorm(f, m, "lnx", 1e-6)
        ln_h = LayerNorm(f, m, "lnh", 1e-6, NB)
        ln_r = LayerNorm(f, m, "lnr", 1e-5)
        q_x, q_h = AbsmaxQuantizer(f, "qx"), AbsmaxQuantizer(f, "qh")
        xh_done, xl_done, xt_done, xt_evac, fc_done, gelu_done = f.sems("xh_done xl_done xt_done xt_evac fc_done gelu_done")
        hh_done, hl_done, ht_done, ht_evac_a, ht_evac_d, y_done, r_done = f.sems(
            "hh_done hl_done ht_done ht_evac_a ht_evac_d y_done r_done")

        def part_of(g):
            return g // 2, (g % 2) * 8

        with f.block() as block:
            @block.tensor
            def _(pe):
                def xt(t, u):
                    pe.wait_ge(xh_done, t + 1)
                    pe.wait_ge(xl_done, t + 1)
                    after(pe, xt_evac, t)
                    transpose_parts(pe, ps_x, x2[u], m).then_inc(xt_done, 1)

                def fc(t, u, banks):
                    pe.wait_ge(xt_evac, t + 1)
                    for n in banks:
                        after(pe, gelu_done, t * NB - (NB - n - 1))
                        for k in range(KC):
                            for part in range(2):
                                last = pe.matmul(ps_fc[n][:, :], xT[u][:, part, k, :],
                                                 m.wfcT[:, k, n * D:(n + 1) * D],
                                                 start=(k == 0 and part == 0), stop=(k == KC - 1 and part == 1))
                        last.then_inc(fc_done, 1)

                def ht(t, u, turns):
                    pe.wait_ge(hh_done, t + 1)
                    pe.wait_ge(hl_done, t + 1)
                    for g in turns:
                        part, k0 = part_of(g)
                        after(pe, (ht_evac_a, ht_evac_d)[g % 2], t * 2 + g // 2)
                        for k in range(8):
                            last = pe.transpose(ps_h[g % 2][:, k, :],
                                                h2[u][:, part, (k0 + k) * P:(k0 + k + 1) * P], m.ident16[:, :])
                        last.then_inc(ht_done, 1)

                def proj(t, u):
                    pe.wait_ge(ht_evac_a, t * 2 + 2)
                    pe.wait_ge(ht_evac_d, t * 2 + 2)
                    after(pe, r_done, t)
                    for part in range(2):
                        for k in range(NK):
                            last = pe.matmul(ps_y[:, :], hT[u][:, part, k, :], m.wprojT[:, k, :],
                                             start=(k == 0 and part == 0), stop=(k == NK - 1 and part == 1))
                    last.then_inc(y_done, 1)

                of = lambda fn, *what: (lambda t, u: fn(t, u, what))
                run_tiles(pe, NT, [(4, of(fc, 0)), (7, of(ht, 0, 1)), (4, of(fc, 1, 2)), (7, of(ht, 2, 3)),
                                   (4, of(fc, 3)), (3, xt), (7, proj)])

            def evacuate(eng, copy, sem, g):
                def evac(t, u):
                    part, k0 = part_of(g)
                    after(eng, y_done, t - 1)
                    eng.wait_ge(ht_done, t * 4 + g + 1)
                    copy(hT[u][:, part, k0:k0 + 8, :], ps_h[g % 2][:, :, :]).then_inc(sem, 1)
                return evac

            @block.scalar
            def _(act):
                def xhi(t, u):
                    act.wait_ge(q_x.s_clipped, t + 1)
                    after(act, xt_done, t - 1)
                    act.activation(x2[u][:, 0, :], xn[u][:, :], ACT.Copy).then_inc(xh_done, 1)

                def gelu(*banks):
                    def fn(t, u):
                        after(act, ln_h.s_used, t - 1)
                        for n in banks:
                            act.wait_ge(fc_done, t * NB + n + 1)
                            act.activation(h[u][:, n, :], ps_fc[n][:, :], ACT.Gelu, scale=m.gamma[:, 0:1]).then_inc(gelu_done, 1)
                    return fn

                def hhi(t, u):
                    act.wait_ge(q_h.s_clipped, t + 1)
                    after(act, ht_done, t * 4 - 4)
                    act.activation(h2[u][:, 0, :], hn[u][:, :], ACT.Copy).then_inc(hh_done, 1)

                copy = lambda out, in_: act.activation(out, in_, ACT.Copy)
                run_tiles(act, NT, [(7, evacuate(act, copy, ht_evac_a, 0)), (4, gelu(0, 1)),
                                    (7, evacuate(act, copy, ht_evac_a, 2)), (4, gelu(2, 3)), (2, xhi), (6, hhi)])

            @block.vector
            def _(dve):
                def x_stats(t, u):
                    ln_x.statistics(dve, m.X[:, t, :][:, None, :], t, u)

                def x_norm(t, u):
                    after(dve, xl_done, t - 1)
                    ln_x.normalize(dve, xn[u][:, :], m.X[:, t, :], t, u)
                    dve.wait_ge(ln_x.s_used, t + 1)
                    q_x.apply(dve, xn[u][:, :], t, u)

                def x_evac(t, u):
                    dve.wait_ge(xt_done, t + 1)
                    after(dve, fc_done, t * NB - NB)
                    dve.tensor_copy(xT[u][:, :, :, :], ps_x[:, :, :, :]).then_inc(xt_evac, 1)

                def h_stats(t, u):
                    dve.wait_ge(gelu_done, t * NB + NB)
                    ln_h.statistics(dve, h[u], t, u)

                def h_norm(t, u):
                    after(dve, hl_done, t - 1)
                    ln_h.normalize(dve, hn[u][:, :], h[u][:, :, :].rearrange("p n k -> p (n k)"), t, u)
                    dve.wait_ge(ln_h.s_used, t + 1)
                    q_h.apply(dve, hn[u][:, :], t, u)

                def residual(t, u):
                    dve.wait_ge(y_done, t + 1)
                    dve.scalar_tensor_tensor(r[u][:, :], ps_y[:, :], m.gamma[:, 1:2], m.X[:, t, :],
                                             ALU.mult, ALU.add).then_inc(r_done, 1)
                    dve.wait_ge(r_done, t + 1)
                    ln_r.statistics(dve, r[u][:, None, :], t, u)

                def norm(t, u):
                    ln_r.normalize(dve, m.X[:, t, :], r[u][:, :], t, u)

                turn = lambda g: evacuate(dve, dve.tensor_copy, ht_evac_d, g)
                run_tiles(dve, NT, [(6, h_norm), (9, norm), (8, residual), (7, turn(1)), (5, h_stats), (7, turn(3)),
                                    (3, x_evac), (1, x_norm), (0, x_stats)])

            @block.gpsimd
            def _(pool):
                def xlo(t, u):
                    pool.wait_ge(xh_done, t + 1)
                    after(pool, xt_done, t - 1)
                    pool.tensor_tensor(x2[u][:, 1, :], xn[u][:, :], x2[u][:, 0, :], ALU.subtract).then_inc(xl_done, 1)

                def hlo(t, u):
                    pool.wait_ge(hh_done, t + 1)
                    after(pool, ht_done, t * 4 - 4)
                    pool.tensor_tensor(h2[u][:, 1, :], hn[u][:, :], h2[u][:, 0, :],
                                       ALU.subtract).then_inc(hl_done, 1)

                run_tiles(pool, NT, [(8, lambda t, u: ln_r.root(pool, t, u)), (5, lambda t, u: ln_h.root(pool, t, u)),
                                     (6, hlo), (2, xlo), (0, lambda t, u: ln_x.root(pool, t, u))])


def linear_weights(nc, m, d):
    names = ("Wqk", "Wv", "Wu", "Wo")
    with Phase(nc, "linw") as f:
        raw = [f.sb(f"raw{n}", [P, KC, D], F32) for n in names]
        brow = f.sb("brow", [LO_ROW + 1, 4, D], F32)
        w_in = [f.sem(f"in_{n}") for n in names]
        b_in, b_zero, bh_done, ones_done, hi_done, lo_done, bl_done = f.sems(
            "b_in b_zero bh_done ones_done hi_done lo_done bl_done")
        with f.block() as block:
            @block.sync
            def _(sp):
                for i, n in enumerate(names):
                    sp.dma_start(raw[i][:, :, :], d[f"L1_attn_{n}"].rearrange("(k p) n -> p k n", p=P)).then_inc(w_in[i], 16)
                for i, n in enumerate(("ln_g", "ln_b")):
                    sp.dma_start(m.ln_gb[:, i, :], d[f"L1_attn_{n}"][None, :].to_broadcast([P, D])).then_inc(m.gb_in, 16)

            @block.gpsimd
            def _(pool):
                pool.memset(brow[:, :, :], 0.0).then_inc(b_zero, 1)
                pool.memset(m.ones_row[:, :], 1.0).then_inc(ones_done, 1)
                pool.wait_ge(b_zero, 1)
                for i, n in enumerate(("bqk", "bv", "bu", "bo")):
                    for row in (0, LO_ROW):
                        pool.dma_start(brow[row:row + 1, i, :], d[f"L1_attn_{n}"][None, :]).then_inc(b_in, 16)

            @block.scalar
            def _(act):
                for i in range(4):
                    act.wait_ge(w_in[i], 16)
                    act.activation(m.w1[:, 0, i, :, :], raw[i][:, :, :], ACT.Copy, scale=WS).then_inc(hi_done, 1)
                act.wait_ge(b_in, 16 * 8)
                act.activation(m.bias[:, :, :], brow[:, :, :], ACT.Copy, scale=WS).then_inc(bh_done, 1)

            @block.vector
            def _(dve):
                for i in range(4):
                    dve.wait_ge(hi_done, i + 1)
                    dve.scalar_tensor_tensor(m.w1[:, 1, i, :, :], raw[i][:, :, :], WS, m.w1[:, 0, i, :, :],
                                             ALU.mult, ALU.subtract).then_inc(lo_done, 1)
                dve.wait_ge(bh_done, 1)
                low = slice(LO_ROW, LO_ROW + 1)
                dve.scalar_tensor_tensor(m.bias[low, :, :], brow[low, :, :], WS, m.bias[low, :, :],
                                         ALU.mult, ALU.subtract).then_inc(bl_done, 1)


def biased(pe, m, out, i, xT):
    pe.matmul(out, m.ones_row[:, :], m.bias[:, i, :], start=True, stop=False)
    for k in range(KC):
        for n, (a, b) in enumerate(((0, 0), (0, 1), (1, 0))):
            last = pe.matmul(out, xT[:, a, k, :], m.w1[:, b, i, k, :], start=False, stop=(k == KC - 1 and n == 2))
    return last


def linear_features(nc, m, b):
    with Phase(nc, f"lin{b}") as f:
        x2 = [f.sb(f"x2{u}", [P, 2, D], F16) for u in range(2)]
        xT = [f.sb(f"xT{u}", [P, 2, KC, P], F16) for u in range(2)]
        e = [f.sb(f"e{u}", [P, D], F32) for u in range(2)]
        relu = [f.sb(f"relu{u}", [P, D], F32) for u in range(2)]
        k1 = [f.sb(f"k1{u}", [P, D], F32) for u in range(2)]
        tanh = [f.sb(f"tanh{u}", [P, 2, D], F32) for u in range(2)]
        k_ = [f.sb(f"k{u}", [P, D], F32) for u in range(2)]
        v_ = [f.sb(f"v{u}", [P, D], F32) for u in range(2)]
        ps_x = f.ps("ps_x", [P, 2, KC, P], F16)
        ps_z = [f.ps(f"ps_z{n}", [P, D], F32) for n in range(3)]
        ps_kv = f.ps("ps_kv", [P, KC, P], F32)
        ps_k = f.ps("ps_k", [P, KC, P], F32)
        xh_done, xl_done, xt_done, xt_evac, z_done, e_done, tanh_done, relu_done, k1_done = f.sems(
            "xh_done xl_done xt_done xt_evac z_done e_done tanh_done relu_done k1_done")
        k_done, v_done, u_done, kv_done, kt_done, kth_done, ktl_done, kvh_done, kvl_done, zero_done = f.sems(
            "k_done v_done u_done kv_done kt_done kth_done ktl_done kvh_done kvl_done zero_done")
        with f.block() as block:
            @block.tensor
            def _(pe):
                def xt(t, u):
                    pe.wait_ge(xl_done, t + 1)
                    after(pe, xt_evac, t)
                    transpose_parts(pe, ps_x, x2[u], m).then_inc(xt_done, 1)

                def z(t, u):
                    pe.wait_ge(xt_evac, t + 1)
                    for n, sem in enumerate((relu_done, v_done, u_done)):
                        after(pe, sem, t)
                        biased(pe, m, ps_z[n][:, :], n, xT[u]).then_inc(z_done, 1)

                def kv(t, u):
                    pe.wait_ge(k_done, t + 1)
                    pe.wait_ge(v_done, t + 1)
                    for g in range(KC):
                        s = slice(g * P, (g + 1) * P)
                        last = pe.matmul(ps_kv[:, g, :], k_[u][:, s], v_[u][:, s],
                                         start=isinstance(t, int) and t == 0 and g == 0,
                                         stop=isinstance(t, int) and t == TB - 1 and g == KC - 1)
                    last.then_inc(kv_done, 1)
                    after(pe, kth_done, t)
                    after(pe, ktl_done, t)
                    for g in range(KC):
                        last = pe.transpose(ps_k[:, g, :], k_[u][:, g * P:(g + 1) * P], m.ident)
                    last.then_inc(kt_done, 1)

                run_tiles(pe, TB, [(1, xt), (2, z), (3, kv)])

            @block.scalar
            def _(act):
                def xhi(t, u):
                    after(act, xt_done, t - 1)
                    act.activation(x2[u][:, 0, :], m.X[:, t + b * TB, :], ACT.Copy).then_inc(xh_done, 1)

                def nonlinear(t, u):
                    after(act, k1_done, t - 1)
                    act.wait_ge(z_done, t * 3 + 1)
                    act.activation(e[u][:, :], ps_z[0][:, :], ACT.Exp, scale=1.0 / WS).then_inc(e_done, 1)
                    after(act, u_done, t - 1)
                    for n in range(2):
                        act.wait_ge(z_done, t * 3 + 2 + n)
                        act.activation(tanh[u][:, n, :], ps_z[1 + n][:, :], ACT.Tanh, scale=0.5 / WS).then_inc(tanh_done, 1)

                def kt_hi(t, u):
                    act.wait_ge(kt_done, t + 1)
                    act.activation(m.kT[:, 0, :, bass.ds(t * P, P)], ps_k[:, :, :], ACT.Copy).then_inc(kth_done, 1)

                run_tiles(act, TB, [(0, xhi), (2, nonlinear), (3, kt_hi)])
                act.wait_ge(zero_done, 2)
                act.wait_ge(kv_done, TB)
                for a in range(4):
                    s = slice(a * DL, (a + 1) * DL)
                    act.activation(m.kv[s, 0, :, s], ps_kv[s, :, s], ACT.Copy, scale=KV_SCALE / (2 * WS)).then_inc(kvh_done, 1)

            @block.vector
            def _(dve):
                for part in range(2):
                    dve.memset(m.kv[:, part, :, :], 0.0).then_inc(zero_done, 1)

                def xevac(t, u):
                    dve.wait_ge(xt_done, t + 1)
                    after(dve, z_done, t * 3 - 3)
                    dve.tensor_copy(xT[u][:, :, :, :], ps_x[:, :, :, :]).then_inc(xt_evac, 1)

                def features(t, u):
                    dve.wait_ge(e_done, t + 1)
                    after(dve, k_done, t - 1)
                    dve.tensor_scalar(relu[u][:, :], ps_z[0][:, :], 0.0, 1.0 / WS, ALU.max, ALU.mult).then_inc(relu_done, 1)
                    dve.wait_ge(relu_done, t + 1)
                    dve.scalar_tensor_tensor(k1[u][:, :], e[u][:, :], 1.0, relu[u][:, :], ALU.min, ALU.add).then_inc(k1_done, 1)
                    dve.wait_ge(tanh_done, t * 2 + 1)
                    after(dve, kv_done, t - 1)
                    dve.scalar_tensor_tensor(v_[u][:, :], tanh[u][:, 0, :], 1.0, ps_z[1][:, :], ALU.add, ALU.mult).then_inc(v_done, 1)
                    dve.wait_ge(tanh_done, t * 2 + 2)
                    dve.scalar_tensor_tensor(m.U[:, t, :], tanh[u][:, 1, :], 1.0, ps_z[2][:, :], ALU.add, ALU.mult).then_inc(u_done, 1)

                def kt_lo(t, u):
                    dve.wait_ge(kth_done, t + 1)
                    s = bass.ds(t * P, P)
                    dve.tensor_tensor(m.kT[:, 1, :, s], ps_k[:, :, :], m.kT[:, 0, :, s], ALU.subtract).then_inc(ktl_done, 1)

                run_tiles(dve, TB, [(1, xevac), (2, features), (3, kt_lo)])
                dve.wait_ge(zero_done, 2)
                for a in range(4):
                    s = slice(a * DL, (a + 1) * DL)
                    dve.wait_ge(kvh_done, a + 1)
                    dve.scalar_tensor_tensor(m.kv[s, 1, :, s], ps_kv[s, :, s], KV_SCALE / (2 * WS), m.kv[s, 0, :, s],
                                             ALU.mult, ALU.subtract).then_inc(kvl_done, 1)

            @block.gpsimd
            def _(pool):
                def xlo(t, u):
                    pool.wait_ge(xh_done, t + 1)
                    after(pool, xt_done, t - 1)
                    pool.tensor_tensor(x2[u][:, 1, :], m.X[:, t + b * TB, :], x2[u][:, 0, :], ALU.subtract).then_inc(xl_done, 1)

                def minus_one(t, u):
                    pool.wait_ge(k1_done, t + 1)
                    after(pool, kt_done, t - 1)
                    pool.tensor_tensor(k_[u][:, :], k1[u][:, :], m.ones[:, 0:1].to_broadcast([P, D]), ALU.subtract).then_inc(k_done, 1)

                run_tiles(pool, TB, [(0, xlo), (2, minus_one)])


def linear_output(nc, m, b):
    with Phase(nc, f"lino{b}") as f:
        w = [f.sb(f"w{u}", [P, D], F32) for u in range(2)]
        n1 = [f.sb(f"n1{u}", [P, D], F32) for u in range(2)]
        n2 = [f.sb(f"n2{u}", [P, D], F32) for u in range(2)]
        w2 = [f.sb(f"w2{u}", [P, 2, D], F16) for u in range(2)]
        wT = [f.sb(f"wT{u}", [P, 2, KC, P], F16) for u in range(2)]
        r = [f.sb(f"r{u}", [P, D], F32) for u in range(2)]
        ps_q = [f.ps(f"ps_q{u}", [P, KC, P], F32) for u in range(2)]
        ps_w = [f.ps(f"ps_w{u}", [P, 2, KC, P], F16) for u in range(2)]
        ps_y = [f.ps(f"ps_y{u}", [P, D], F32) for u in range(2)]
        ln_q = LayerNorm(f, m, "lnq", 1e-5 * KV_SCALE ** 2)
        ln_r = LayerNorm(f, m, "lnr", 1e-5)
        q_done, n1_done, n2_done, w_done, wh_done, wl_done, wt_done, wt_evac, y_done, r_done = f.sems(
            "q_done n1_done n2_done w_done wh_done wl_done wt_done wt_evac y_done r_done")
        with f.block() as block:
            @block.tensor
            def _(pe):
                def q(t, u):
                    after(pe, n1_done, t - 1)
                    s = bass.ds(t * P, P)
                    for g in range(KC):
                        for n, (a, c) in enumerate(((0, 0), (0, 1), (1, 0))):
                            last = pe.matmul(ps_q[u][:, g, :], m.kT[:, a, g, s], m.kv[:, c, g, :], start=(n == 0), stop=(n == 2))
                    last.then_inc(q_done, 1)

                def wt(t, u):
                    pe.wait_ge(wl_done, t + 1)
                    after(pe, wt_evac, t - 1)
                    transpose_parts(pe, ps_w[u], w2[u], m).then_inc(wt_done, 1)

                def wo(t, u):
                    pe.wait_ge(wt_evac, t + 1)
                    after(pe, r_done, t - 1)
                    biased(pe, m, ps_y[u][:, :], 3, wT[u]).then_inc(y_done, 1)

                run_tiles(pe, TB, [(3, wo), (2, wt), (0, q)])

            @block.scalar
            def _(act):
                def whi(t, u):
                    act.wait_ge(w_done, t + 1)
                    after(act, wt_done, t - 1)
                    act.activation(w2[u][:, 0, :], w[u][:, :], ACT.Copy).then_inc(wh_done, 1)

                def wevac(t, u):
                    act.wait_ge(wt_done, t + 1)
                    after(act, y_done, t - 1)
                    act.activation(wT[u][:, :, :, :], ps_w[u][:, :, :, :], ACT.Copy).then_inc(wt_evac, 1)

                run_tiles(act, TB, [(2, wevac), (1, whi)])

            @block.vector
            def _(dve):
                def stats(t, u):
                    dve.wait_ge(q_done, t + 1)
                    ln_q.statistics(dve, ps_q[u][:, :, :].rearrange("p g n -> p (g n)")[:, None, :], t, u)

                def gate(t, u):
                    dve.scalar_tensor_tensor(n1[u][:, :], ps_q[u][:, :, :].rearrange("p g n -> p (g n)"),
                                             ln_q.mv[u][:, 0:1], m.ln_gb[:, 0, :], ALU.subtract, ALU.mult).then_inc(n1_done, 1)
                    dve.wait_ge(n1_done, t + 1)
                    dve.wait_ge(ln_q.s_rstd, t + 1)
                    dve.scalar_tensor_tensor(n2[u][:, :], n1[u][:, :], ln_q.rstd[u][:, :], m.ln_gb[:, 1, :],
                                             ALU.mult, ALU.add).then_inc(ln_q.s_used, 1)
                    dve.wait_ge(ln_q.s_used, t + 1)
                    after(dve, wl_done, t - 1)
                    dve.scalar_tensor_tensor(w[u][:, :], m.U[:, t, :], 0.5 / WS, n2[u][:, :], ALU.mult, ALU.mult).then_inc(w_done, 1)

                def residual(t, u):
                    dve.wait_ge(y_done, t + 1)
                    dve.scalar_tensor_tensor(r[u][:, :], ps_y[u][:, :], 1.0 / WS, m.X[:, t + b * TB, :],
                                             ALU.mult, ALU.add).then_inc(r_done, 1)
                    dve.wait_ge(r_done, t + 1)
                    ln_r.statistics(dve, r[u][:, None, :], t, u)

                def norm(t, u):
                    ln_r.normalize(dve, m.X[:, t + b * TB, :], r[u][:, :], t, u)

                if b == 0:
                    dve.wait_ge(m.gb_in, 32)
                run_tiles(dve, TB, [(1, gate), (4, norm), (0, stats), (3, residual)])

            @block.gpsimd
            def _(pool):
                def wlo(t, u):
                    pool.wait_ge(wh_done, t + 1)
                    after(pool, wt_done, t - 1)
                    pool.tensor_tensor(w2[u][:, 1, :], w[u][:, :], w2[u][:, 0, :], ALU.subtract).then_inc(wl_done, 1)

                run_tiles(pool, TB, [(1, wlo), (0, lambda t, u: ln_q.root(pool, t, u)),
                                     (3, lambda t, u: ln_r.root(pool, t, u))])


def linear_attention(nc, m, d):
    with ExitStack() as ctx:
        def sb(name, shape, dt):
            return ctx.enter_context(nc.sbuf_tensor(name, shape, dt))

        m.w1 = sb("w1", [P, 2, 4, KC, D], F16)
        m.bias = sb("bias", [LO_ROW + 1, 4, D], F16)
        m.ones_row = sb("ones_row", [LO_ROW + 1, P], F16)
        m.ln_gb = sb("ln_gb", [P, 2, D], F32)
        m.gb_in = ctx.enter_context(nc.semaphore("gb_in"))
        linear_weights(nc, m, d)
        m.kT = sb("kT", [P, 2, KC, N], F16)
        m.kv = sb("kv", [P, 2, KC, P], F16)
        m.U = sb("U", [P, TB, D], F32)
        for b in range(B):
            linear_features(nc, m, b)
            linear_output(nc, m, b)


def route(nc, m, d):
    with Phase(nc, "route") as f:
        gate = f.sb("gate", [NE, D], F32)
        gT = f.sb("gT", [P, 2, KC, NE], F16)
        x2 = [f.sb(f"x2{u}", [P, 2, D], F16) for u in range(2)]
        logits = f.sb("logits", [P, NT, NE], F32)
        top = f.sb("top", [P, NT], F32)
        shifted = f.sb("shifted", [P, NT, NE], F32)
        e = f.sb("e", [P, NT, NE], F32)
        total = f.sb("total", [P, NT], F32)
        rec = f.sb("rec", [P, NT], F32)
        probs = f.sb("probs", [P, 2, NT, NE], F32)
        ranked = f.sb("ranked", [P, 2, NT, NE], F32)
        code = f.sb("code", [P, 2, NT], F32)
        ps_g = f.ps("ps_g", [P, KC, NE], F32)
        ps_x = [f.ps(f"ps_x{u}", [P, 2, KC, P], F16) for u in range(2)]
        ps_l = [f.ps(f"ps_l{u}", [P, NE], F32) for u in range(2)]
        gate_in, g_done, gh_done, gl_done, xh_done, xl_done, xt_done, xt_evac, l_done, l_evac = f.sems(
            "gate_in g_done gh_done gl_done xh_done xl_done xt_done xt_evac l_done l_evac")
        step, exp_done, tables_in = f.sems("step exp_done tables_in")
        stored = [f.sem(f"stored{u}") for u in range(2)]
        x2_rows = m.x2_d.rearrange("(t p) n -> t p n", p=P)
        with f.block() as block:
            @block.sync
            def _(sp):
                sp.dma_start(gate[:, :], d["L1_ffn_gate_w"]).then_inc(gate_in, 16)
                sp.dma_start(m.tables[:, :], d["consts"][:, TABLES + 32:CONST_COLS]).then_inc(tables_in, 16)
                for t in range(NT):
                    sp.wait_ge(xl_done, t + 1)
                    sp.dma_start(x2_rows[t], x2[t % 2][:, :, :].rearrange("p a n -> p (a n)")).then_inc(stored[t % 2], 16)
                for u in range(2):
                    sp.wait_ge(stored[u], 16 * NT // 2)

            @block.tensor
            def _(pe):
                pe.wait_ge(gate_in, 16)
                for k in range(KC):
                    last = pe.transpose(ps_g[:, k, :], gate[:, k * P:(k + 1) * P], m.ident[0:NE, 0:NE])
                last.then_inc(g_done, 1)

                def xt(t, u):
                    pe.wait_ge(xl_done, t + 1)
                    after(pe, xt_evac, t - 1)
                    transpose_parts(pe, ps_x[u], x2[u], m).then_inc(xt_done, 1)

                def logit(t, u):
                    pe.wait_ge(xt_evac, t + 1)
                    after(pe, l_evac, t - 1)
                    s = bass.ds(t * P, P)
                    for k in range(KC):
                        for n, (a, c) in enumerate(((0, 0), (0, 1), (1, 0), (1, 1))):
                            last = pe.matmul(ps_l[u][:, :], m.xT3[:, a, k, s], gT[:, c, k, :],
                                             start=(k == 0 and n == 0), stop=(k == KC - 1 and n == 3))
                    last.then_inc(l_done, 1)

                pe.wait_ge(gl_done, 1)
                run_tiles(pe, NT, [(1, xt), (2, logit)])

            @block.scalar
            def _(act):
                act.wait_ge(g_done, 1)
                act.activation(gT[:, 0, :, :], ps_g[:, :, :], ACT.Copy, scale=WS).then_inc(gh_done, 1)

                def xhi(t, u):
                    after(act, xt_done, t - 1)
                    if isinstance(t, int):
                        after(act, stored[u], 16 * (t // 2))
                    else:
                        act.wait_ge(stored[u], t * 8 - 8 * u)
                    act.activation(x2[u][:, 0, :], m.X[:, t, :], ACT.Copy).then_inc(xh_done, 1)

                run_tiles(act, NT, [(0, xhi)])
                act.wait_ge(step, 2)
                act.activation(e[:, :, :], shifted[:, :, :], ACT.Exp, scale=1.0 / WS).then_inc(exp_done, 1)

            @block.vector
            def _(dve):
                dve.wait_ge(gh_done, 1)
                dve.scalar_tensor_tensor(gT[:, 1, :, :], ps_g[:, :, :], WS, gT[:, 0, :, :], ALU.mult,
                                         ALU.subtract).then_inc(gl_done, 1)

                def xevac(t, u):
                    dve.wait_ge(xt_done, t + 1)
                    dve.tensor_copy(m.xT3[:, :, :, bass.ds(t * P, P)], ps_x[u][:, :, :, :]).then_inc(xt_evac, 1)

                def levac(t, u):
                    dve.wait_ge(l_done, t + 1)
                    dve.tensor_copy(logits[:, t, :], ps_l[u][:, :]).then_inc(l_evac, 1)

                run_tiles(dve, NT, [(1, xevac), (2, levac)])
                count = [0]

                def done(instruction):
                    instruction.then_inc(step, 1)
                    count[0] += 1
                    dve.wait_ge(step, count[0])

                def wide(x):
                    return x[:, :, None].to_broadcast([P, NT, NE])

                dve.wait_ge(l_evac, NT)
                dve.wait_ge(tables_in, 16)
                done(dve.tensor_reduce(top[:, :], logits[:, :, :], AX.X, ALU.max))
                done(dve.tensor_tensor(shifted[:, :, :], logits[:, :, :], wide(top[:, :]), ALU.subtract))
                dve.wait_ge(exp_done, 1)
                done(dve.tensor_reduce(total[:, :], e[:, :, :], AX.X, ALU.add))
                done(dve.reciprocal(rec[:, :], total[:, :]))
                done(dve.tensor_tensor(probs[:, 0, :, :], e[:, :, :], wide(rec[:, :]), ALU.mult))
                descending = m.descending[:, None, :].to_broadcast([P, NT, NE])
                for c in range(2):
                    done(dve.tensor_reduce(m.score[:, c, :], probs[:, c, :, :], AX.X, ALU.max))
                    done(dve.tensor_tensor(ranked[:, c, :, :], probs[:, c, :, :], wide(m.score[:, c, :]), ALU.is_equal))
                    done(dve.tensor_tensor(shifted[:, :, :], ranked[:, c, :, :], descending, ALU.mult))
                    done(dve.tensor_reduce(code[:, c, :], shifted[:, :, :], AX.X, ALU.max))
                    done(dve.tensor_tensor(m.hot[:, c, :, :], descending, wide(code[:, c, :]), ALU.is_equal))
                    if c == 0:
                        done(dve.scalar_tensor_tensor(probs[:, 1, :, :], m.hot[:, 0, :, :], -2.0, probs[:, 0, :, :],
                                                      ALU.mult, ALU.add))

            @block.gpsimd
            def _(pool):
                def xlo(t, u):
                    pool.wait_ge(xh_done, t + 1)
                    after(pool, xt_done, t - 1)
                    pool.tensor_tensor(x2[u][:, 1, :], m.X[:, t, :], x2[u][:, 0, :], ALU.subtract).then_inc(xl_done, 1)

                run_tiles(pool, NT, [(0, xlo)])


FCH = [(0, P), (P, P), (2 * P, FE - 2 * P)]


def shared_expert(nc, m, experts, out):
    E = len(experts)
    with Phase(nc, "moe") as f:
        raw_g = f.sb("raw_g", [P, KC, 2, FE], F32)
        raw_d = f.sb("raw_d", [P, 3, D], F32)
        wg = [f.sb(f"wg{e}", [P, 2, KC, 2, FE], F16) for e in range(2)]
        wd = [f.sb(f"wd{e}", [P, 2, 3, D], F16) for e in range(2)]
        th = [f.sb(f"th{u}", [P, FE], F32) for u in range(2)]
        a_ = [f.sb(f"a{u}", [P, FE], F32) for u in range(2)]
        h = [f.sb(f"h{u}", [P, FE], F32) for u in range(2)]
        h2 = [f.sb(f"h2{u}", [P, 2, FE], F16) for u in range(2)]
        hT = [f.sb(f"hT{u}", [P, 2, 3, P], F16) for u in range(2)]
        ps_g = [[f.ps(f"ps_g{u}{n}", [P, FE], F32) for n in range(2)] for u in range(2)]
        ps_h = f.ps("ps_h", [P, 2, 3, P], F16)
        ps_y = [f.ps(f"ps_y{u}", [P, D], F32) for u in range(2)]
        w_in, wh_done, wl_done, g_done, th_done, a_done, h_done, hh_done, hl_done = f.sems(
            "w_in wh_done wl_done g_done th_done a_done h_done hh_done hl_done")
        ht_done, ht_evac, y_done, acc_done = f.sems("ht_done ht_evac y_done acc_done")
        yg = [f.sb(f"yg{u}", [P, 2, D], F32) for u in range(2)]
        yg_in = [[f.sem(f"yg_in{u}{c}") for c in range(2)] for u in range(2)]
        yg_used, out_done = f.sems("yg_used out_done")
        ln = LayerNorm(f, m, "ln", 1e-5)
        out_rows = out.rearrange("b (t p) n -> p (b t) n", p=P)
        LAST = slice(0, FCH[2][1])
        with f.block() as block:
            @block.sync
            def _(sp):
                for i, (gate, up, down) in enumerate(experts):
                    after(sp, wl_done, 3 * i)
                    for n, w in enumerate((gate, up)):
                        sp.dma_start(raw_g[:, :, n, :], w.rearrange("(k p) n -> p k n", p=P)).then_inc(w_in, 16)
                    sp.dma_start(raw_d[:, 0:2, :], down[0:2 * P, :].rearrange("(k p) n -> p k n", p=P)).then_inc(w_in, 16)
                    sp.dma_start(raw_d[LAST, 2, :], down[2 * P:FE, :]).then_inc(w_in, 16)
                for c in range(NT // 2):
                    sp.wait_ge(ln.s_used, 2 * c + 2)
                    sp.dma_start(out_rows[:, 2 * c:2 * c + 2, :], m.X[:, 2 * c:2 * c + 2, :]).then_inc(out_done, 16)
                sp.wait_ge(out_done, 16 * NT // 2)

            @block.tensor
            def _(pe):
                for i in range(E):
                    T0, w = i * NT, i % 2

                    def gu(t, u):
                        after(pe, h_done, T0 + t - 1)
                        s = bass.ds(t * P, P)
                        for n in range(2):
                            last = products(pe, ps_g[u][n][:, :], lambda k: m.xT3[:, 0, k, s], lambda k: m.xT3[:, 1, k, s],
                                            lambda k: wg[w][:, 0, k, n, :], lambda k: wg[w][:, 1, k, n, :], KC)
                            last.then_inc(g_done, 1)

                    def tr(t, u):
                        pe.wait_ge(hl_done, T0 + t + 1)
                        after(pe, ht_evac, T0 + t)
                        for part in range(2):
                            for k, (at, size) in enumerate(FCH):
                                last = pe.transpose(ps_h[0:size, part, k, :], h2[u][:, part, at:at + size], m.ident16[:, :])
                        last.then_inc(ht_done, 1)

                    def down(t, u):
                        pe.wait_ge(ht_evac, T0 + t + 1)
                        after(pe, acc_done, T0 + t - 1)
                        for k, (_, size) in enumerate(FCH):
                            for n, (a, c) in enumerate(((0, 0), (0, 1), (1, 0))):
                                last = pe.matmul(ps_y[u][:, :], hT[u][0:size, a, k, :], wd[w][0:size, c, k, :],
                                                 start=(k == 0 and n == 0), stop=(k == 2 and n == 2))
                        last.then_inc(y_done, 1)

                    pe.wait_ge(wl_done, 3 * i + 3)
                    run_tiles(pe, NT, [(3, down), (2, tr), (0, gu)])

            def split(i, eng, part):
                w = i % 2
                if part == 0:
                    eng.wait_ge(w_in, 64 * (i + 1))
                    after(eng, y_done, NT * (i - 1))
                else:
                    eng.wait_ge(wh_done, 3 * i + 3)
                for out, raw in ((wg[w][:, part], raw_g[:, :, :, :]), (wd[w][:, part, 0:2, :], raw_d[:, 0:2, :]),
                                 (wd[w][LAST, part, 2, :], raw_d[LAST, 2, :])):
                    if part == 0:
                        eng.activation(out, raw, ACT.Copy, scale=WS).then_inc(wh_done, 1)
                    else:
                        hi = {0: wg[w][:, 0], 1: wd[w][:, 0, 0:2, :], 2: wd[w][LAST, 0, 2, :]}[split.n]
                        eng.scalar_tensor_tensor(out, raw, WS, hi, ALU.mult, ALU.subtract).then_inc(wl_done, 1)
                        split.n = (split.n + 1) % 3
            split.n = 0

            @block.scalar
            def _(act):
                split(0, act, 0)
                for i in range(E):
                    T0 = i * NT
                    if i + 1 < E:
                        split(i + 1, act, 0)

                    def tanh(t, u):
                        act.wait_ge(g_done, (T0 + t) * 2 + 1)
                        after(act, a_done, T0 + t - 1)
                        act.activation(th[u][:, :], ps_g[u][0][:, :], ACT.Tanh, scale=0.5 / WS).then_inc(th_done, 1)

                    def hhi(t, u):
                        act.wait_ge(h_done, T0 + t + 1)
                        after(act, ht_done, T0 + t - 1)
                        act.activation(h2[u][:, 0, :], h[u][:, :], ACT.Copy).then_inc(hh_done, 1)

                    def hevac(t, u):
                        act.wait_ge(ht_done, T0 + t + 1)
                        after(act, y_done, T0 + t - 1)
                        act.activation(hT[u][:, :, 0:2, :], ps_h[:, :, 0:2, :], ACT.Copy)
                        act.activation(hT[u][LAST, :, 2, :], ps_h[LAST, :, 2, :], ACT.Copy).then_inc(ht_evac, 1)

                    run_tiles(act, NT, [(1, hhi), (2, hevac), (0, tanh)])

            @block.vector
            def _(dve):
                split(0, dve, 1)
                for i in range(E):
                    T0 = i * NT
                    if i + 1 < E:
                        split(i + 1, dve, 1)

                    def swiglu(t, u):
                        dve.wait_ge(th_done, T0 + t + 1)
                        dve.scalar_tensor_tensor(a_[u][:, :], th[u][:, :], 1.0, ps_g[u][0][:, :], ALU.add, ALU.mult).then_inc(a_done, 1)
                        dve.wait_ge(a_done, T0 + t + 1)
                        dve.wait_ge(g_done, (T0 + t) * 2 + 2)
                        after(dve, hl_done, T0 + t - 1)
                        dve.scalar_tensor_tensor(h[u][:, :], a_[u][:, :], 0.5 / WS ** 2, ps_g[u][1][:, :], ALU.mult,
                                                 ALU.mult).then_inc(h_done, 1)

                    def accumulate(t, u):
                        dve.wait_ge(y_done, T0 + t + 1)
                        dve.scalar_tensor_tensor(m.X[:, t, :], ps_y[u][:, :], 1.0 / WS, m.X[:, t, :],
                                                 ALU.mult, ALU.add).then_inc(acc_done, 1)
                        if i == E - 1:
                            dve.wait_ge(acc_done, T0 + t + 1)
                            for c in range(2):
                                if isinstance(t, int):
                                    dve.wait_ge(yg_in[u][c], 16 * (t // 2 + 1))
                                else:
                                    dve.wait_ge(yg_in[u][c], t * 8 + (16 - 8 * u))
                                dve.scalar_tensor_tensor(m.X[:, t, :], yg[u][:, c, :], m.weight[:, c, t:t + 1] if isinstance(t, int)
                                                         else m.weight[:, c, bass.ds(t, 1)], m.X[:, t, :],
                                                         ALU.mult, ALU.add).then_inc(yg_used, 1)
                                dve.wait_ge(yg_used, t * 2 + c + 1)
                            dve.memset(ln.pad[:, :], 0.0)
                            ln.statistics(dve, m.X[:, t, :][:, None, :], t, u)

                    def norm(t, u):
                        ln.normalize(dve, m.X[:, t, :], m.X[:, t, :], t, u)

                    after(dve, acc_done, T0)
                    run_tiles(dve, NT, [(1, swiglu)] + [(5, norm)] * (i == E - 1) + [(3, accumulate)])

            @block.gpsimd
            def _(pool):
                for i in range(E):
                    T0 = i * NT

                    def hlo(t, u):
                        pool.wait_ge(hh_done, T0 + t + 1)
                        after(pool, ht_done, T0 + t - 1)
                        pool.tensor_tensor(h2[u][:, 1, :], h[u][:, :], h2[u][:, 0, :], ALU.subtract).then_inc(hl_done, 1)

                    if i < E - 1:
                        run_tiles(pool, NT, [(1, hlo)])
                for s in range(1, NT + 4):
                    if s >= 4:
                        ln.root(pool, s - 4, s % 2)
                    if s <= NT:
                        hlo(s - 1, (s - 1) % 2)
                    t = s - 2
                    if 0 <= t < NT:
                        for c in range(2):
                            after(pool, yg_used, 2 * t - 2)
                            pool.indirect_dma_start(yg[t % 2][:, c, :], None, m.y_d, bass.IndirectOffsetOnAxis(
                                ap=m.slot[:, c * NT + t:c * NT + t + 1], axis=0)).then_inc(yg_in[t % 2][c], 16)


def dispatch(nc, m):
    NB = 2 * NT
    with Phase(nc, "disp") as f:
        hot16 = f.sb("hot16", [P, NB, NE], F16)
        earlier = f.sb("earlier", [P, P], F16)
        ones16 = f.sb("ones16", [P, P], F16)
        incl = [f.sb(f"incl{n}", [P, NB, NE], F32) for n in range(2)]
        rank = f.sb("rank", [P, NB, NE], F32)
        work = f.sb("work", [P, NB, NE], F32)
        tiles = f.sb("tiles", [P, NE], F32)
        base = f.sb("base", [P, NE], F32)
        end = f.sb("end", [P, NE], F32)
        slot_f = f.sb("slot_f", [P, NB], F32)
        owner_f = f.sb("owner_f", [P, NB], F32)
        zero = f.sb("zero", [NG * 2, P], F32)
        rows = f.sb("rows", [NG * 2, P], F32)
        ps_pre = f.ps("ps_pre", [P, NB, NE], F32)
        ps_tot = f.ps("ps_tot", [P, NB, NE], F32)
        ps_tok = f.ps("ps_tok", [P, NG * 2], F32)
        step, count_done, slots_done, zeroed, zero_out, scattered, rows_in, tok_done = f.sems(
            "step count_done slots_done zeroed zero_out scattered rows_in tok_done")
        table = m.token_d.rearrange("(r p) o -> r (p o)", p=P)
        with f.block() as block:
            @block.vector
            def _(dve):
                count = [0]

                def done(instruction):
                    instruction.then_inc(step, 1)
                    count[0] += 1
                    dve.wait_ge(step, count[0])

                dve.memset(zero[:, :], 0.0).then_inc(zeroed, 1)
                done(dve.memset(ones16[:, :], 1.0))
                done(dve.tensor_scalar(earlier[:, :], m.masks[:, 0, :], -1.0, None, ALU.is_lt))
                done(dve.tensor_copy(hot16[:, :, :], m.hot[:, :, :, :].rearrange("p c t e -> p (c t) e")))
                dve.wait_ge(count_done, 1)
                done(dve.tensor_copy(incl[0][:, :, :], ps_tot[:, :, :]))
                for n in range(5):
                    a, b, w = incl[n % 2], incl[1 - n % 2], 1 << n
                    dve.tensor_copy(b[:, 0:w, :], a[:, 0:w, :])
                    done(dve.tensor_tensor(b[:, w:NB, :], a[:, w:NB, :], a[:, 0:NB - w, :], ALU.add))
                total = incl[1]
                done(dve.tensor_tensor(rank[:, :, :], total[:, :, :], ps_pre[:, :, :], ALU.add))
                done(dve.tensor_tensor(rank[:, :, :], rank[:, :, :], ps_tot[:, :, :], ALU.subtract))
                fits = work[:, 0:8, :].rearrange("p a e -> p (a e)").rearrange("p (e j) -> p e j", e=NE)
                done(dve.tensor_tensor(fits, total[:, NB - 1, :][:, :, None].to_broadcast([P, NE, 8]),
                                       m.multiples[:, None, :].to_broadcast([P, NE, 8]), ALU.is_gt))
                done(dve.tensor_reduce(tiles[:, :], fits, AX.X, ALU.add))
                done(dve.tensor_tensor(work[:, 0:NE, :], tiles[:, None, :].to_broadcast([P, NE, NE]), m.lower, ALU.mult))
                done(dve.tensor_reduce(base[:, :], work[:, 0:NE, :], AX.X, ALU.add))
                done(dve.tensor_tensor(end[:, :], base[:, :], tiles[:, :], ALU.add))
                done(dve.tensor_tensor(work[:, :, :], end[:, None, :].to_broadcast([P, NB, NE]),
                                       m.groups[:, :, None].to_broadcast([P, NB, NE]), ALU.is_le))
                done(dve.tensor_reduce(owner_f[:, :], work[:, :, :], AX.X, ALU.add))
                done(dve.tensor_scalar(m.owner[:, :], owner_f[:, :], NE - 1.0, None, ALU.min))
                done(dve.scalar_tensor_tensor(work[:, :, :], base[:, None, :].to_broadcast([P, NB, NE]), float(GS),
                                              rank[:, :, :], ALU.mult, ALU.add))
                done(dve.tensor_tensor(rank[:, :, :], work[:, :, :], hot16[:, :, :], ALU.mult))
                done(dve.tensor_reduce(slot_f[:, :], rank[:, :, :], AX.X, ALU.add))
                done(dve.tensor_copy(m.slot[:, :], slot_f[:, :]))
                dve.tensor_scalar(m.weight[:, :, :], m.score[:, :, :], 1.0 / WS, None, ALU.mult).then_inc(slots_done, 1)
                dve.wait_ge(tok_done, 1)
                done(dve.tensor_copy(m.token[:, :], ps_tok[:, :]))

            @block.tensor
            def _(pe):
                pe.wait_ge(step, 3)
                flat = hot16[:, :, :].rearrange("p b e -> p (b e)")
                pe.matmul(ps_pre[:, :, :].rearrange("p b e -> p (b e)"), earlier[:, :], flat, start=True, stop=True)
                pe.matmul(ps_tot[:, :, :].rearrange("p b e -> p (b e)"), ones16[:, :], flat, start=True,
                          stop=True).then_inc(count_done, 1)
                pe.wait_ge(rows_in, 16)
                pe.transpose(ps_tok[:, :], rows[:, :], m.ident[0:NG * 2, 0:NG * 2]).then_inc(tok_done, 1)

            @block.sync
            def _(sp):
                sp.wait_ge(zeroed, 1)
                sp.dma_start(table, zero[:, :]).then_inc(zero_out, 16)
                sp.wait_ge(scattered, 16 * NB)
                sp.dma_start(rows[:, :], table).then_inc(rows_in, 16)

            @block.gpsimd
            def _(pool):
                pool.wait_ge(zero_out, 16)
                pool.wait_ge(slots_done, 1)
                for b in range(NB):
                    pool.indirect_dma_start(m.token_d, bass.IndirectOffsetOnAxis(ap=m.slot[:, b:b + 1], axis=0),
                                            m.token_ids[:, b % NT:b % NT + 1], None).then_inc(scattered, 16)
                pool.wait_ge(scattered, 16 * NB)


def sparse_experts(nc, m, d):
    with Phase(nc, "sparse") as f:
        xg = [f.sb(f"xg{u}", [P, 2, 2 * D], F16) for u in range(2)]
        xT = [f.sb(f"xT{u}", [P, 2, 2, KC, P], F16) for u in range(2)]
        raw_g = [f.sb(f"raw_g{u}", [P, KC, 2 * FE], F32) for u in range(2)]
        raw_d = [f.sb(f"raw_d{u}", [P, 3, D], F32) for u in range(2)]
        wg = [f.sb(f"wg{u}", [P, 2, KC, 2 * FE], F16) for u in range(2)]
        wd = [f.sb(f"wd{u}", [P, 2, 3, D], F16) for u in range(2)]
        th = [f.sb(f"th{h}", [P, FE], F32) for h in range(2)]
        a_ = [f.sb(f"a{h}", [P, FE], F32) for h in range(2)]
        hid = [f.sb(f"hid{h}", [P, FE], F32) for h in range(2)]
        h2 = [f.sb(f"h2{u}", [P, 2, 2, FE], F16) for u in range(2)]
        hT = [f.sb(f"hT{h}", [P, 2, 3, P], F16) for h in range(2)]
        y = [f.sb(f"y{u}", [P, 2, D], F32) for u in range(2)]
        ps_x = f.ps("ps_x", [P, 2, KC, P], F16)
        ps_h = f.ps("ps_h", [P, 2, 3, P], F16)
        ps_g = [[f.ps(f"ps_g{h}{n}", [P, FE], F32) for n in range(2)] for h in range(2)]
        ps_y = [f.ps(f"ps_y{h}", [P, D], F32) for h in range(2)]
        g_in = [f.sem(f"g_in{u}") for u in range(2)]
        d_in = [f.sem(f"d_in{u}") for u in range(2)]
        x_in = [[f.sem(f"x_in{u}{h}") for h in range(2)] for u in range(2)]
        gh_done, gl_done, dh_done, dl_done, xt_done, xt_evac, gu_done, th_done, a_done, h_done = f.sems(
            "gh_done gl_done dh_done dl_done xt_done xt_evac gu_done th_done a_done h_done")
        hh_done, hl_done, ht_done, ht_evac, y_done, y_evac = f.sems("hh_done hl_done ht_done ht_evac y_done y_evac")
        y_out = [f.sem(f"y_out{u}") for u in range(2)]
        LAST = slice(0, FCH[2][1])
        y_rows = m.y_d.rearrange("(s h p) n -> s p h n", h=2, p=P)

        with f.block() as block:
            @block.sync
            def _(sp):
                for s in range(NG + 4):
                    if s < NG:
                        u = s % 2
                        e = sp.value_load(m.owner[0:1, s:s + 1], min_val=0, max_val=NE - 1)
                        after(sp, gl_done, s - 1)
                        sp.dma_start(raw_g[u][:, :, :], d["L1_ffn_w_gate_up"][bass.ds(e, 1), :, :]
                                     .rearrange("e (k p) n -> p (e k) n", p=P)).then_inc(g_in[u], 16)
                        after(sp, dl_done, (s - 1) * 2)
                        down = d["L1_ffn_w_down"][bass.ds(e, 1), :, :]
                        sp.dma_start(raw_d[u][:, 0:2, :], down[:, 0:2 * P, :].rearrange("e (k p) n -> p (e k) n", p=P)).then_inc(d_in[u], 16)
                        sp.dma_start(raw_d[u][LAST, 2, :], down[:, 2 * P:FE, :].rearrange("e p n -> p (e n)")).then_inc(d_in[u], 16)
                    if s >= 4:
                        t = s - 4
                        sp.wait_ge(y_evac, 2 * t + 2)
                        sp.dma_start(y_rows[t], y[t % 2][:, :, :]).then_inc(y_out[t % 2], 16)
                for u in range(2):
                    sp.wait_ge(y_out[u], 16 * ((NG + 1 - u) // 2))

            @block.tensor
            def _(pe):
                def xt(h):
                    def fn(t, u):
                        if isinstance(t, int):
                            pe.wait_ge(x_in[u][h], 16 * (t // 2 + 1))
                        else:
                            pe.wait_ge(x_in[u][h], t * 8 + (16 - 8 * u))
                        after(pe, xt_evac, t * 2 + h)
                        for part in range(2):
                            for k in range(KC):
                                last = pe.transpose(ps_x[:, part, k, :], xg[u][:, h, part * D + k * P:part * D + (k + 1) * P],
                                                    m.ident16[:, :])
                        last.then_inc(xt_done, 1)
                    return fn

                def gu(h):
                    def fn(t, u):
                        pe.wait_ge(xt_evac, t * 2 + 1 + h)
                        pe.wait_ge(gl_done, t + 1)
                        after(pe, h_done, t * 2 - 1 + h)
                        for n in range(2):
                            c = slice(n * FE, (n + 1) * FE)
                            products(pe, ps_g[h][n][:, :], lambda k: xT[u][:, h, 0, k, :], lambda k: xT[u][:, h, 1, k, :],
                                     lambda k: wg[u][:, 0, k, c], lambda k: wg[u][:, 1, k, c], KC).then_inc(gu_done, 1)
                    return fn

                def tr(h):
                    def fn(t, u):
                        pe.wait_ge(hl_done, t * 2 + h + 1)
                        after(pe, ht_evac, t * 2 + h)
                        for part in range(2):
                            for k, (at, size) in enumerate(FCH):
                                last = pe.transpose(ps_h[0:size, part, k, :], h2[u][:, h, part, at:at + size], m.ident16[:, :])
                        last.then_inc(ht_done, 1)
                    return fn

                def down(h):
                    def fn(t, u):
                        pe.wait_ge(ht_evac, t * 2 + h + 1)
                        pe.wait_ge(dl_done, t * 2 + 2)
                        after(pe, y_evac, t * 2 - 1 + h)
                        for k, (_, size) in enumerate(FCH):
                            for n, (a, c) in enumerate(((0, 0), (0, 1), (1, 0))):
                                last = pe.matmul(ps_y[h][:, :], hT[h][0:size, a, k, :], wd[u][0:size, c, k, :],
                                                 start=(k == 0 and n == 0), stop=(k == 2 and n == 2))
                        last.then_inc(y_done, 1)
                    return fn

                run_tiles(pe, NG, [(1, xt(0)), (3, tr(0)), (2, gu(0)), (1, xt(1)), (3, tr(1)), (2, gu(1)),
                                   (3, down(0)), (3, down(1))])

            @block.scalar
            def _(act):
                def gate_hi(t, u):
                    act.wait_ge(g_in[u], 16 * (t // 2 + 1)) if isinstance(t, int) else act.wait_ge(g_in[u], t * 8 + (16 - 8 * u))
                    after(act, gu_done, t * 4 - 4)
                    act.activation(wg[u][:, 0, :, :], raw_g[u][:, :, :], ACT.Copy, scale=WS).then_inc(gh_done, 1)

                def down_hi(t, u):
                    act.wait_ge(d_in[u], 32 * (t // 2 + 1)) if isinstance(t, int) else act.wait_ge(d_in[u], t * 16 + (32 - 16 * u))
                    after(act, y_done, t * 2 - 2)
                    act.activation(wd[u][:, 0, 0:2, :], raw_d[u][:, 0:2, :], ACT.Copy, scale=WS).then_inc(dh_done, 1)
                    act.activation(wd[u][LAST, 0, 2, :], raw_d[u][LAST, 2, :], ACT.Copy, scale=WS).then_inc(dh_done, 1)

                def tanh(h):
                    def fn(t, u):
                        act.wait_ge(gu_done, t * 4 + 2 * h + 1)
                        after(act, a_done, t * 2 - 1 + h)
                        act.activation(th[h][:, :], ps_g[h][0][:, :], ACT.Tanh, scale=0.5 / WS).then_inc(th_done, 1)
                    return fn

                def hhi(h):
                    def fn(t, u):
                        act.wait_ge(h_done, t * 2 + h + 1)
                        after(act, ht_done, t * 2 - 3 + h)
                        act.activation(h2[u][:, h, 0, :], hid[h][:, :], ACT.Copy).then_inc(hh_done, 1)
                    return fn

                def hevac(h):
                    def fn(t, u):
                        act.wait_ge(ht_done, t * 2 + h + 1)
                        after(act, y_done, t * 2 - 1 + h)
                        act.activation(hT[h][:, :, 0:2, :], ps_h[:, :, 0:2, :], ACT.Copy)
                        act.activation(hT[h][LAST, :, 2, :], ps_h[LAST, :, 2, :], ACT.Copy).then_inc(ht_evac, 1)
                    return fn

                run_tiles(act, NG, [(3, hevac(0)), (1, gate_hi), (2, tanh(0)), (3, hevac(1)), (2, hhi(0)), (2, down_hi),
                                    (2, tanh(1)), (2, hhi(1))])

            @block.vector
            def _(dve):
                def xevac(h):
                    def fn(t, u):
                        dve.wait_ge(xt_done, t * 2 + h + 1)
                        after(dve, gu_done, t * 4 - 6 + 2 * h)
                        dve.tensor_copy(xT[u][:, h, :, :, :], ps_x[:, :, :, :]).then_inc(xt_evac, 1)
                    return fn

                def gate_lo(t, u):
                    dve.wait_ge(gh_done, t + 1)
                    dve.scalar_tensor_tensor(wg[u][:, 1, :, :], raw_g[u][:, :, :], WS, wg[u][:, 0, :, :],
                                             ALU.mult, ALU.subtract).then_inc(gl_done, 1)

                def down_lo(t, u):
                    dve.wait_ge(dh_done, t * 2 + 2)
                    for s, k in ((slice(0, P), slice(0, 2)), (LAST, slice(2, 3))):
                        dve.scalar_tensor_tensor(wd[u][s, 1, k, :], raw_d[u][s, k, :], WS, wd[u][s, 0, k, :],
                                                 ALU.mult, ALU.subtract).then_inc(dl_done, 1)

                def swiglu(h):
                    def fn(t, u):
                        dve.wait_ge(th_done, t * 2 + h + 1)
                        dve.scalar_tensor_tensor(a_[h][:, :], th[h][:, :], 1.0, ps_g[h][0][:, :], ALU.add, ALU.mult).then_inc(a_done, 1)
                        dve.wait_ge(a_done, t * 2 + h + 1)
                        dve.wait_ge(gu_done, t * 4 + 2 * h + 2)
                        after(dve, hl_done, t * 2 - 1 + h)
                        dve.scalar_tensor_tensor(hid[h][:, :], a_[h][:, :], 0.5 / WS ** 2, ps_g[h][1][:, :], ALU.mult,
                                                 ALU.mult).then_inc(h_done, 1)
                    return fn

                def yevac(h):
                    def fn(t, u):
                        dve.wait_ge(y_done, t * 2 + h + 1)
                        if isinstance(t, int):
                            after(dve, y_out[u], 16 * (t // 2))
                        else:
                            dve.wait_ge(y_out[u], t * 8 - 8 * u)
                        dve.tensor_copy(y[u][:, h, :], ps_y[h][:, :]).then_inc(y_evac, 1)
                    return fn

                run_tiles(dve, NG, [(1, xevac(0)), (1, gate_lo), (2, swiglu(0)), (1, xevac(1)), (2, down_lo),
                                    (2, swiglu(1)), (3, yevac(0)), (3, yevac(1))])

            @block.gpsimd
            def _(pool):
                for s in range(NG + 2):
                    for h in range(2):
                        if s < NG:
                            u = s % 2
                            after(pool, xt_done, 2 * s - 3 + h)
                            pool.indirect_dma_start(xg[u][:, h, :], None, m.x2_d,
                                                    bass.IndirectOffsetOnAxis(ap=m.token[:, 2 * s + h:2 * s + h + 1], axis=0)
                                                    ).then_inc(x_in[u][h], 16)
                    if s >= 2:
                        t = s - 2
                        for h in range(2):
                            pool.wait_ge(hh_done, t * 2 + h + 1)
                            after(pool, ht_done, t * 2 - 3 + h)
                            pool.tensor_tensor(h2[t % 2][:, h, 1, :], hid[h][:, :], h2[t % 2][:, h, 0, :],
                                               ALU.subtract).then_inc(hl_done, 1)


def experts(nc, m, d, out):
    with ExitStack() as ctx:
        def sb(name, shape, dt):
            return ctx.enter_context(nc.sbuf_tensor(name, shape, dt))

        m.x2_d = nc.dram_tensor("x2_d", (B * N, 2 * D), F16, kind="Internal").ap()
        m.token_d = nc.dram_tensor("token_d", (NG * GS, 1), F32, kind="Internal").ap()
        m.y_d = nc.dram_tensor("y_d", (NG * GS, D), F32, kind="Internal").ap()
        m.xT3 = sb("xT3", [P, 2, KC, NT * P], F16)
        m.score = sb("score", [P, 2, NT], F32)
        tables = sb("tables", [P, CONST_COLS - TABLES - 32], F32)
        m.tables = tables
        m.descending, m.multiples, lower, m.groups, m.token_ids = [
            tables[:, at - TABLES - 32:at - TABLES - 32 + size] for at, size in _small_tables()[1:]]
        m.lower = lower.rearrange("p (a b) -> p a b", a=NE)
        m.weight = sb("weight", [P, 2, NT], F32)
        m.slot = sb("slot", [P, 2 * NT], U32)
        m.token = sb("token", [P, 2 * NG], U32)
        m.owner = sb("owner", [P, 2 * NT], U32)
        with nc.sbuf_tensor("hot", [P, 2, NT, NE], F32) as m.hot:
            route(nc, m, d)
            dispatch(nc, m)
        sparse_experts(nc, m, d)
        shared_gu, shared_d = d["L1_ffn_shared_gate_up"], d["L1_ffn_shared_down"]
        shared_expert(nc, m, [(shared_gu[:, s * FE:(s + 1) * FE], shared_gu[:, SI + s * FE:SI + (s + 1) * FE],
                               shared_d[s * FE:(s + 1) * FE, :]) for s in range(2)], out)


class Memory:
    pass


TABLES = 4 * P + 2 * TB * HD
CONST_COLS = TABLES + 32 + NE + 8 + NE * NE + 2 * NT + NT


def build(nc, d, out):
    m = Memory()
    with ExitStack() as ctx:
        def sb(name, shape, dt):
            return ctx.enter_context(nc.sbuf_tensor(name, shape, dt))

        m.X = sb("X", [P, NT, D], F32)
        m.consts = sb("consts", [P, TABLES + 32], F32)
        m.ident = m.consts[:, 0:P]
        m.masks = m.consts[:, P:4 * P].rearrange("p (a k) -> p a k", a=3)
        m.rope = m.consts[:, 4 * P:4 * P + 2 * TB * HD].rearrange("p (a t d) -> p a t d", a=2, d=HD)
        m.select = m.consts[:, TABLES:TABLES + 32]
        m.ones = sb("ones", [P, P], F32)
        m.ident16 = sb("ident16", [P, P], F16)
        m.identb = sb("identb", [P, P], BF16)
        m.masks16 = sb("masks16", [P, 3, P], BF16)
        m.minus_half = sb("minus_half", [P, 1], F32)
        m.gamma = sb("gamma", [P, 2], F32)
        with ExitStack() as layer0:
            def l0(name, shape, dt):
                return layer0.enter_context(nc.sbuf_tensor(name, shape, dt))

            m.wfcT = l0("wfcT", [P, KC, FF], F16)
            m.wprojT = l0("wprojT", [P, FF // P, D], F16)
            with ExitStack() as attn:
                def la(name, shape, dt):
                    return attn.enter_context(nc.sbuf_tensor(name, shape, dt))

                m.wqkv_h = la("wqkv_h", [P, KC, D + 2 * KV], F16)
                m.wqkv_l = la("wqkv_l", [P, KC, D + 2 * KV], F16)
                m.wo_h = la("wo_h", [P, KC, D], F16)
                m.wo_l = la("wo_l", [P, KC, D], F16)
                load_and_prepare(nc, m, d)
                with nc.sbuf_tensor("O", [P, TB, D], F32) as m.O:
                    with nc.sbuf_tensor("QT", [P, HQ // 2, N], F16) as QT, \
                            nc.sbuf_tensor("KTe", [P, HKV, N], F16) as KTe, \
                            nc.sbuf_tensor("KTo", [P, HKV, N], F16) as KTo, \
                            nc.sbuf_tensor("V", [P, TB, HKV, 32], F32) as V:
                        for b in range(B):
                            project_qkv(nc, m, b, QT, [KTe, KTo], V)
                            attend(nc, m, b, QT, [KTe, KTo], V)
                            attention_output(nc, m, b)
            ternary_ffn(nc, m)
        linear_attention(nc, m, d)
        experts(nc, m, d, out)


_INS = ['L0_attn_x', 'L0_attn_wq', 'L0_attn_wk', 'L0_attn_wv', 'L0_attn_wo', 'L0_ffn_w_fc', 'L0_ffn_w_proj',
        'L1_attn_Wqk', 'L1_attn_bqk', 'L1_attn_Wv', 'L1_attn_bv', 'L1_attn_Wu', 'L1_attn_bu', 'L1_attn_Wo',
        'L1_attn_bo', 'L1_attn_ln_g', 'L1_attn_ln_b', 'L1_ffn_gate_w', 'L1_ffn_w_gate_up', 'L1_ffn_w_down',
        'L1_ffn_shared_gate_up', 'L1_ffn_shared_down']


def _small_tables():
    sizes = (32, NE, 8, NE * NE, 2 * NT, NT)
    return [(TABLES + sum(sizes[:i]), size) for i, size in enumerate(sizes)]


def _constants():
    c = np.zeros((P, CONST_COLS), np.float32)
    c[:, 0:P] = np.eye(P)
    rows, cols = np.arange(P)[:, None], np.arange(P)[None, :]
    c[:, P:2 * P] = np.where(cols > rows, -1e30, 0.0)
    c[:, 2 * P:3 * P] = np.where(rows > cols, -1e30, 0.0)
    c[:, 3 * P:4 * P] = c[:, 2 * P:3 * P]
    freq = np.float32(10000.0) ** (-(np.arange(HD // 2, dtype=np.float32) * np.float32(2.0 / HD)))
    phase = np.arange(N, dtype=np.float32)[:, None] * freq[None, :].astype(np.float32)
    cos, sin = np.cos(phase), np.sin(phase)
    table = np.stack([np.stack([cos, cos], -1), np.stack([-sin, sin], -1)]) / WS
    table = table.reshape(2, TB, P, HD).transpose(2, 0, 1, 3)
    c[:, 4 * P:TABLES] = table.reshape(P, -1)
    small = (np.tile(np.eye(32), (4, 1)),
             NE - np.arange(NE),
             GS * np.arange(8),
             np.tril(np.ones((NE, NE)), -1).reshape(-1),
             np.arange(2 * NT),
             np.arange(NT)[None, :] * P + np.arange(P)[:, None])
    for (at, size), values in zip(_small_tables(), small):
        c[:, at:at + size] = values
    return c


def kernel(**inputs):
    import numpy as _np
    import concourse.bacc as _bacc
    from concourse import mybir as _mybir
    from concourse.bass_utils import run_bass_kernel_spmd as _run

    nc = _bacc.Bacc("TRN2", target_bir_lowering=False, num_devices=1)
    arrays, d = {}, {}
    for name in _INS:
        a = _np.ascontiguousarray(inputs[name])
        arrays[f"in_{name}_dram"] = a
        d[name] = nc.dram_tensor(f"in_{name}_dram", a.shape, _mybir.dt.from_np(a.dtype), kind="ExternalInput").ap()
    a = _constants()
    arrays["in_consts_dram"] = a
    d["consts"] = nc.dram_tensor("in_consts_dram", a.shape, _mybir.dt.float32, kind="ExternalInput").ap()
    out = nc.dram_tensor("out_0_dram", (B, N, D), _mybir.dt.float32, kind="ExternalOutput").ap()
    build(nc, d, out)
    r = _run(nc, [arrays], core_ids=[0])
    return r.results[0]["out_0_dram"]
```
